# Optimizing a Trainium2 kernel written in Bass

```python
import numpy as np
import jax
import jax.numpy as jnp

def _softmax(x, axis=-1):
    return jax.nn.softmax(x, axis=axis)

def _gelu(x):
    return jax.nn.gelu(x, approximate=True)

def _silu(x):
    return jax.nn.silu(x)

def _sigmoid(x):
    return jax.nn.sigmoid(x)

def _layernorm(x, axis=-1, eps=1e-05):
    m = jnp.mean(x, axis=axis, keepdims=True)
    v = jnp.var(x, axis=axis, keepdims=True)
    return (x - m) / jnp.sqrt(v + eps)

def _scatter_add(tgt, idx, src, axis=0):
    return tgt.at[idx].add(src)

def _segment_sum(src, seg, n):
    return jax.ops.segment_sum(src, seg, n)
kernel_name = 'mk_flamingo_gated_d2_seqx_r8_86a624'

def setup_inputs(seed: int=0):
    np.random.seed(seed)
    _w = jnp.asarray

    def _rec_inputs():
        import jax
        import jax.numpy as jnp
        _rk = jax.random.key(seed)
        x = -0.0005207 + 1.001 * jax.random.normal(jax.random.fold_in(_rk, 1), (64, 64, 128), jnp.float32)
        _lenS = 64 - jax.random.randint(jax.random.fold_in(_rk, 7), (64,), 0, max(1, 64 // 4) + 1, jnp.int32)
        _lenS2 = 64 - jax.random.randint(jax.random.fold_in(_rk, 8), (64,), 0, max(1, 64 // 4) + 1, jnp.int32)
        _ctx_1024P = jax.random.normal(jax.random.fold_in(_rk, 11), (64, 16, 128), jnp.float32)
        _ctx_1024c = jax.random.dirichlet(jax.random.fold_in(_rk, 511), 0.3 * jnp.ones((16,), jnp.float32), (64, 64))
        _ctx_1024t = jnp.einsum('bsk,bkd->bsd', _ctx_1024c, _ctx_1024P)
        _ctx_1024t = _ctx_1024t * jax.lax.rsqrt(jnp.mean(jnp.square(_ctx_1024t)) + 1e-12) * 0.953939
        ctx_1024 = -0.000514642 + 1.00011 * (_ctx_1024t + 0.3 * jax.random.normal(jax.random.fold_in(_rk, 611), (64, 64, 128), jnp.float32))
        _validS = jnp.arange(64)[None, :] < _lenS[:, None]
        _validS2 = jnp.arange(64)[None, :] < _lenS2[:, None]
        _causal = jnp.tril(jnp.ones((64, 64), dtype=bool))
        mask_BxSxS2_ik0 = jnp.where(jnp.broadcast_to(_validS2[:, None, :], (64, 64, 64)), 0, 1).astype(jnp.int32)
        _g = jax.random.normal(jax.random.fold_in(_rk, 9001), (2, 2), jnp.float32)
        _g = jnp.sign(_g) * jnp.maximum(jnp.abs(_g), 1.0) + (_g == 0) * 1.0
        g_xattn = _g[0]
        g_ffn = _g[1]
        return (x, ctx_1024, mask_BxSxS2_ik0, g_xattn, g_ffn)
    x, ctx_1024, mask_BxSxS2_ik0, g_xattn, g_ffn = _rec_inputs()

    def _L0_xattn_setup():
        import jax, jax.numpy as jnp
        import numpy as np
        B, S, E, NH = (1, 256, 128, 8)
        DH = E // NH
        EPS = 1e-06
        LN_EPS = 1e-05
        key = jax.random.key(seed)
        ks = jax.random.split(key, 8)
        q = jax.random.normal(ks[0], (B, S, E), dtype=jnp.float32)
        k = jax.random.normal(ks[1], (B, S, E), dtype=jnp.float32)
        v = jax.random.normal(ks[2], (B, S, E), dtype=jnp.float32)
        scale = 1.0 / np.sqrt(3 * E)
        igate_w = jax.random.normal(ks[3], (NH, 3 * E), dtype=jnp.float32) * scale
        igate_b = jax.random.normal(ks[4], (NH,), dtype=jnp.float32) * 0.1
        fgate_w = jax.random.normal(ks[5], (NH, 3 * E), dtype=jnp.float32) * scale
        fgate_b = jnp.linspace(3.0, 6.0, NH, dtype=jnp.float32)
        out_w = 1.0 + 0.1 * jax.random.normal(ks[6], (E,), dtype=jnp.float32)
        return {'q': q, 'k': k, 'v': v, 'igate_w': igate_w, 'igate_b': igate_b, 'fgate_w': fgate_w, 'fgate_b': fgate_b, 'out_w': out_w}
    _L0_xattn_all = _L0_xattn_setup()
    _L0_xattn_in = {k: v for k, v in _L0_xattn_all.items() if k in ('igate_w', 'igate_b', 'fgate_w', 'fgate_b', 'out_w')}
    del _L0_xattn_all

    def _L0_ffn_setup():
        import jax, jax.numpy as jnp
        import numpy as np
        QMAX = 127.0

        def _ste_round(v):
            return v + jax.lax.stop_gradient(jnp.round(v) - v)

        def _act_fake_quant(x, clip_factor):
            scale = jax.nn.sigmoid(clip_factor) * jnp.max(jnp.abs(x)) / QMAX
            return jnp.clip(_ste_round(x / scale), -QMAX - 1.0, QMAX) * scale

        def _weight_fake_quant(w):
            scale = jnp.max(jnp.abs(w), axis=1, keepdims=True) / QMAX
            return jnp.clip(_ste_round(w / scale), -QMAX - 1.0, QMAX) * scale
        key = jax.random.key(seed)
        k1, k2, k3, k4 = jax.random.split(key, 4)
        B, S, H, I = (8, 1024, 128, 352)
        return {'x': jax.random.normal(k1, (B, S, H), dtype=jnp.float32), 'clip_x': jnp.full((1,), 4.0, dtype=jnp.float32), 'clip_down': jnp.full((1,), 4.0, dtype=jnp.float32), 'w_gate': jax.random.normal(k2, (I, H), dtype=jnp.float32) * 0.02, 'w_up': jax.random.normal(k3, (I, H), dtype=jnp.float32) * 0.02, 'w_down': jax.random.normal(k4, (H, I), dtype=jnp.float32) * 0.02}
    _L0_ffn_all = _L0_ffn_setup()
    _L0_ffn_in = {k: v for k, v in _L0_ffn_all.items() if k in ('clip_x', 'clip_down', 'w_gate', 'w_up', 'w_down')}
    del _L0_ffn_all

    def _L1_xattn_setup():
        import jax, jax.numpy as jnp
        import numpy as np
        import math
        B, T, F, H = (16, 64, 128, 16)
        DK = F // H
        key = jax.random.key(seed)
        ks = jax.random.split(key, 14)
        s = 0.02
        return {'query': jax.random.normal(ks[0], (B, T, F), jnp.float32), 'key': jax.random.normal(ks[1], (B, T, F), jnp.float32), 'value': jax.random.normal(ks[2], (B, T, F), jnp.float32), 'pos_k': jax.random.normal(ks[3], (T, T, DK), jnp.float32), 'pos_v': jax.random.normal(ks[4], (T, T, DK), jnp.float32), 'mask': jax.random.randint(ks[5], (B, T, T), 0, 2, jnp.int32), 'Wq': jax.random.normal(ks[6], (F, F), jnp.float32) * s, 'bq': jnp.zeros((F,), jnp.float32), 'Wk': jax.random.normal(ks[7], (F, F), jnp.float32) * s, 'bk': jnp.zeros((F,), jnp.float32), 'Wv': jax.random.normal(ks[8], (F, F), jnp.float32) * s, 'bv': jnp.zeros((F,), jnp.float32), 'Wo': jax.random.normal(ks[9], (F, F), jnp.float32) * s, 'bo': jnp.zeros((F,), jnp.float32)}
    _L1_xattn_all = _L1_xattn_setup()
    _L1_xattn_in = {k: v for k, v in _L1_xattn_all.items() if k in ('pos_k', 'pos_v', 'Wq', 'bq', 'Wk', 'bk', 'Wv', 'bv', 'Wo', 'bo')}
    del _L1_xattn_all

    def _L1_ffn_setup():
        import jax, jax.numpy as jnp
        import numpy as np
        from jax import lax
        D = 128
        H = 512
        E = 8
        TOPK = 2
        key = jax.random.key(seed)
        ks = jax.random.split(key, 7)
        s = 0.02
        return {'x': jax.random.normal(ks[0], (2, 256, D), dtype=jnp.float32), 'W1': jax.random.normal(ks[1], (E, D, H), dtype=jnp.float32) * s, 'b1': jnp.zeros((E, H), dtype=jnp.float32), 'W2': jax.random.normal(ks[2], (E, H, D), dtype=jnp.float32) * s, 'b2': jnp.zeros((E, D), dtype=jnp.float32), 'Wr': jax.random.normal(ks[3], (D, E), dtype=jnp.float32) * s, 'br': jnp.zeros((E,), dtype=jnp.float32)}
    _L1_ffn_all = _L1_ffn_setup()
    _L1_ffn_in = {k: v for k, v in _L1_ffn_all.items() if k in ('W1', 'b1', 'W2', 'b2', 'Wr', 'br')}
    del _L1_ffn_all
    return {'x': x, 'ctx_1024': ctx_1024, 'mask_BxSxS2_ik0': mask_BxSxS2_ik0, 'g_xattn': g_xattn, 'g_ffn': g_ffn, 'L0_xattn_igate_w': _L0_xattn_in['igate_w'], 'L0_xattn_igate_b': _L0_xattn_in['igate_b'], 'L0_xattn_fgate_w': _L0_xattn_in['fgate_w'], 'L0_xattn_fgate_b': _L0_xattn_in['fgate_b'], 'L0_xattn_out_w': _L0_xattn_in['out_w'], 'L0_ffn_clip_x': _L0_ffn_in['clip_x'], 'L0_ffn_clip_down': _L0_ffn_in['clip_down'], 'L0_ffn_w_gate': _L0_ffn_in['w_gate'], 'L0_ffn_w_up': _L0_ffn_in['w_up'], 'L0_ffn_w_down': _L0_ffn_in['w_down'], 'L1_xattn_pos_k': _L1_xattn_in['pos_k'], 'L1_xattn_pos_v': _L1_xattn_in['pos_v'], 'L1_xattn_Wq': _L1_xattn_in['Wq'], 'L1_xattn_bq': _L1_xattn_in['bq'], 'L1_xattn_Wk': _L1_xattn_in['Wk'], 'L1_xattn_bk': _L1_xattn_in['bk'], 'L1_xattn_Wv': _L1_xattn_in['Wv'], 'L1_xattn_bv': _L1_xattn_in['bv'], 'L1_xattn_Wo': _L1_xattn_in['Wo'], 'L1_xattn_bo': _L1_xattn_in['bo'], 'L1_ffn_W1': _L1_ffn_in['W1'], 'L1_ffn_b1': _L1_ffn_in['b1'], 'L1_ffn_W2': _L1_ffn_in['W2'], 'L1_ffn_b2': _L1_ffn_in['b2'], 'L1_ffn_Wr': _L1_ffn_in['Wr'], 'L1_ffn_br': _L1_ffn_in['br']}

def reference(x, ctx_1024, mask_BxSxS2_ik0, g_xattn, g_ffn, L0_xattn_igate_w, L0_xattn_igate_b, L0_xattn_fgate_w, L0_xattn_fgate_b, L0_xattn_out_w, L0_ffn_clip_x, L0_ffn_clip_down, L0_ffn_w_gate, L0_ffn_w_up, L0_ffn_w_down, L1_xattn_pos_k, L1_xattn_pos_v, L1_xattn_Wq, L1_xattn_bq, L1_xattn_Wk, L1_xattn_bk, L1_xattn_Wv, L1_xattn_bv, L1_xattn_Wo, L1_xattn_bo, L1_ffn_W1, L1_ffn_b1, L1_ffn_W2, L1_ffn_b2, L1_ffn_Wr, L1_ffn_br):
    import jax
    import jax.numpy as jnp

    def _L0_xattn_ref(q, k, v, igate_w, igate_b, fgate_w, fgate_b, out_w):
        import jax, jax.numpy as jnp
        import numpy as np
        B, S, E, NH = (1, 256, 128, 8)
        DH = E // NH
        EPS = 1e-06
        LN_EPS = 1e-05
        Bq, Sq, Eq = q.shape
        nh = igate_b.shape[0]
        dh = Eq // nh
        gi = jnp.concatenate([q, k, v], axis=-1)
        ig = (gi @ igate_w.T + igate_b).transpose(0, 2, 1)
        fg = (gi @ fgate_w.T + fgate_b).transpose(0, 2, 1)
        qh = q.reshape(Bq, Sq, nh, dh).transpose(0, 2, 1, 3)
        kh = k.reshape(Bq, Sq, nh, dh).transpose(0, 2, 1, 3)
        vh = v.reshape(Bq, Sq, nh, dh).transpose(0, 2, 1, 3)
        log_f = jax.nn.log_sigmoid(fg)
        cs = jnp.cumsum(log_f, axis=-1)
        diff = cs[..., :, None] - cs[..., None, :]
        mask = jnp.tril(jnp.ones((Sq, Sq), dtype=bool))
        log_fg_mat = jnp.where(mask, diff, -jnp.inf)
        log_D = log_fg_mat + ig[..., None, :]
        max_log_D = jnp.max(log_D, axis=-1, keepdims=True)
        D = jnp.exp(log_D - max_log_D)
        qk = jnp.einsum('bhsd,bhtd->bhst', qh, kh) / jnp.sqrt(jnp.float32(dh))
        C = qk * D
        normalizer = jnp.maximum(jnp.abs(C.sum(-1, keepdims=True)), jnp.exp(-max_log_D))
        h = jnp.einsum('bhst,bhtd->bhsd', C / (normalizer + EPS), vh)
        mean = h.mean(-1, keepdims=True)
        var = ((h - mean) ** 2).mean(-1, keepdims=True)
        hn = (h - mean) / jnp.sqrt(var + LN_EPS)
        hn = hn * out_w.reshape(nh, dh)[None, :, None, :]
        return hn.transpose(0, 2, 1, 3).reshape(Bq, Sq, Eq)

    def _L0_ffn_ref(x, clip_x, clip_down, w_gate, w_up, w_down):
        import jax, jax.numpy as jnp
        import numpy as np
        QMAX = 127.0

        def _ste_round(v):
            return v + jax.lax.stop_gradient(jnp.round(v) - v)

        def _act_fake_quant(x, clip_factor):
            scale = jax.nn.sigmoid(clip_factor) * jnp.max(jnp.abs(x)) / QMAX
            return jnp.clip(_ste_round(x / scale), -QMAX - 1.0, QMAX) * scale

        def _weight_fake_quant(w):
            scale = jnp.max(jnp.abs(w), axis=1, keepdims=True) / QMAX
            return jnp.clip(_ste_round(w / scale), -QMAX - 1.0, QMAX) * scale
        xq = _act_fake_quant(x, clip_x[0])
        gate = jnp.einsum('bsh,ih->bsi', xq, _weight_fake_quant(w_gate))
        up = jnp.einsum('bsh,ih->bsi', xq, _weight_fake_quant(w_up))
        h = _act_fake_quant(jax.nn.silu(gate) * up, clip_down[0])
        return jnp.einsum('bsi,hi->bsh', h, _weight_fake_quant(w_down))

    def _L1_xattn_ref(query, key, value, pos_k, pos_v, mask, Wq, bq, Wk, bk, Wv, bv, Wo, bo):
        import jax, jax.numpy as jnp
        import numpy as np
        import math
        B, T, F, H = (16, 64, 128, 16)
        DK = F // H
        b = query.shape[0]

        def proj(x, W, bias):
            return (x @ W.T + bias).reshape(b, -1, H, DK).transpose(0, 2, 1, 3)
        q = proj(query, Wq, bq)
        k = proj(key, Wk, bk)
        v = proj(value, Wv, bv)
        A = jnp.einsum('bhtd,bhsd->bhts', q, k)
        Brel = jnp.einsum('bhtd,tsd->bhts', q, pos_k)
        scores = (A + Brel) / math.sqrt(DK)
        neg = jnp.finfo(scores.dtype).min
        m = mask[:, None, :, :] == 0
        scores = jnp.where(m, neg, scores)
        attn = jax.nn.softmax(scores, axis=-1)
        attn = jnp.where(m, 0.0, attn)
        x = jnp.einsum('bhts,bhsd->bhtd', attn, v)
        x = x + jnp.einsum('bhts,tsd->bhtd', attn, pos_v)
        x = x.transpose(0, 2, 1, 3).reshape(b, -1, F)
        return x @ Wo.T + bo

    def _L1_ffn_ref(x, W1, b1, W2, b2, Wr, br):
        import jax, jax.numpy as jnp
        import numpy as np
        from jax import lax
        D = 128
        H = 512
        E = 8
        TOPK = 2
        B, S, _ = x.shape
        xf = x.reshape(-1, D)
        logits = xf @ Wr + br
        topv, _ = lax.top_k(logits, TOPK)
        thresh = topv[:, TOPK - 1:TOPK]
        masked = jnp.where(logits >= thresh, logits, -jnp.inf)
        weights = jax.nn.softmax(masked, axis=-1)
        h = jax.nn.gelu(jnp.einsum('td,edh->eth', xf, W1) + b1[:, None, :], approximate=False)
        expert_out = jnp.einsum('eth,ehd->etd', h, W2) + b2[:, None, :]
        out = jnp.einsum('etd,te->td', expert_out, weights)
        return out.reshape(B, S, D)
    x = x + jnp.tanh(g_xattn[0]) * _L0_xattn_ref(_layernorm(x, axis=-1), ctx_1024, ctx_1024, L0_xattn_igate_w, L0_xattn_igate_b, L0_xattn_fgate_w, L0_xattn_fgate_b, L0_xattn_out_w)
    x = x + jnp.tanh(g_ffn[0]) * _L0_ffn_ref(_layernorm(x, axis=-1), L0_ffn_clip_x, L0_ffn_clip_down, L0_ffn_w_gate, L0_ffn_w_up, L0_ffn_w_down)
    x = x + jnp.tanh(g_xattn[1]) * _L1_xattn_ref(_layernorm(x, axis=-1), ctx_1024, ctx_1024, L1_xattn_pos_k, L1_xattn_pos_v, mask_BxSxS2_ik0, L1_xattn_Wq, L1_xattn_bq, L1_xattn_Wk, L1_xattn_bk, L1_xattn_Wv, L1_xattn_bv, L1_xattn_Wo, L1_xattn_bo)
    x = x + jnp.tanh(g_ffn[1]) * _L1_ffn_ref(_layernorm(x, axis=-1), L1_ffn_W1, L1_ffn_b1, L1_ffn_W2, L1_ffn_b2, L1_ffn_Wr, L1_ffn_br)
    return x

_drawn_inputs = setup_inputs


def setup_inputs(seed=0):
    import zlib

    import numpy as np

    out = dict(_drawn_inputs(seed))
    spreads = {'g_ffn': (-1.0, 0.6),
     'L1_xattn_bq': (0.0, 2.0),
     'L1_xattn_bk': (0.0, 2.0),
     'L1_xattn_bv': (0.0, 2.0),
     'L1_xattn_bo': (0.0, 0.432),
     'L1_ffn_b1': (0.0, 0.8),
     'L1_ffn_b2': (0.0, 0.617),
     'L1_ffn_br': (0.0, 0.285)}
    factors = {'L0_xattn_igate_b': 64.0,
     'L0_ffn_w_gate': 8.0,
     'L0_ffn_w_up': 8.0,
     'L0_ffn_w_down': 8.0,
     'L1_xattn_pos_k': 5.124,
     'L1_xattn_Wq': 5.498,
     'L1_xattn_Wk': 24.928,
     'L1_xattn_Wv': 2.863,
     'L1_ffn_W1': 2.804}
    for name, (base, spread) in spreads.items():
        noise = np.random.default_rng([zlib.crc32(name.encode()), seed]).standard_normal(out[name].shape)
        drawn = base * np.exp(spread * noise) if base else spread * noise
        out[name] = jnp.asarray(drawn.astype(out[name].dtype))
    for name, factor in factors.items():
        out[name] = (out[name] * factor).astype(out[name].dtype)
    return out
```

```python
from contextlib import ExitStack

import concourse.bass as bass
from concourse import mybir

P = 128
B, S, E = 64, 64, 128
TILES = B * S // P
GROUP = 4
GROUPS = TILES // GROUP
NH0, DH0 = 8, 16
LN_EPS = 1e-5
NORM_EPS = 1e-6
QMAX = 127.0
MAGIC = 1.5 * 2 ** 23
NH1, DH1 = 16, 8
EXPERTS, HID = 8, 512
CHUNKS = (128, 128, 96)
FAR = -1e30

F32 = mybir.dt.float32
F32R = mybir.dt.float32r
BF16 = mybir.dt.bfloat16
I32 = mybir.dt.int32
ALU = mybir.AluOpType
ACT = mybir.ActivationFunctionType
AX = mybir.AxisListType.X


class Names:

    def __init__(self, table):
        self.table = table

    def __getattr__(self, name):
        return self.table[name]


def cols(i, n):
    return bass.ds(i * n, n)


def upto(n):
    return n + 1


class Chain:

    def __init__(self, eng, sem):
        self.eng, self.sem, self.n = eng, sem, 0

    def link(self, ins):
        self.n += 1
        ins.then_inc(self.sem, 1)
        self.eng.wait_ge(self.sem, self.n)


def hold(eng, m):
    eng.sem_inc(m.held, 1)


def start_counts(nc, m):
    reused, credited = m.reused, m.credited
    m.reused, m.credited = [], []
    with nc.Block() as block:

        @block.sync
        def _(sp):
            for sem in reused:
                sp.sem_clear(sem)
            for sem in credited:
                sp.sem_inc(sem, 1)


def load_and_constants(nc, m):
    with nc.Block() as block:

        @block.sync
        def _(sp):
            sp.dma_start(m.X[:, :, :], m.x.rearrange("(i c) s f -> (c s) i f", c=2)).then_inc(m.x_loaded, 16)
            sp.dma_start(m.C[:, :, :], m.ctx.rearrange("(i c) s f -> (c s) i f", c=2)).then_inc(m.ctx_loaded, 16)

        @block.scalar
        def _(act):
            act.dma_start(m.gate_rows[0:NH0, :], m.igate_w).then_inc(m.gates_loaded, 16)
            act.dma_start(m.gate_rows[NH0:2 * NH0, :], m.fgate_w).then_inc(m.gates_loaded, 16)
            act.dma_start(m.gate_bias[:, 0:NH0], m.igate_b.partition_broadcast(P)).then_inc(m.gates_loaded, 16)
            act.dma_start(m.gate_bias[:, NH0:2 * NH0], m.fgate_b.partition_broadcast(P)).then_inc(m.gates_loaded, 16)
            act.dma_start(m.out_w_rows[:, :], m.out_w.partition_broadcast(P)).then_inc(m.scales_loaded, 16)
            act.dma_start(m.tanh_g[:, 0:2], m.g_xattn.partition_broadcast(P)).then_inc(m.scales_loaded, 16)
            act.dma_start(m.tanh_g[:, 2:4], m.g_ffn.partition_broadcast(P)).then_inc(m.scales_loaded, 16)
            for k, w in enumerate((m.w_gate, m.w_up)):
                act.dma_start(m.gu_raw[:, 3 * k:3 * k + 2, :], w[0:2 * P].rearrange("(c p) f -> p c f", p=P)).then_inc(m.ffn0_loaded, 16)
                act.dma_start(m.gu_raw[0:96, 3 * k + 2, :], w[2 * P:]).then_inc(m.ffn0_loaded, 16)
            act.dma_start(m.dn_raw[:, 0, :], m.w_down).then_inc(m.ffn0_loaded, 16)
            act.dma_start(m.clips[:, 0:1], m.clip_x.unsqueeze(0)).then_inc(m.clips_loaded, 16)
            act.dma_start(m.clips[:, 1:2], m.clip_down.unsqueeze(0)).then_inc(m.clips_loaded, 16)
            for k, w in enumerate((m.Wq, m.Wk, m.Wv, m.Wo)):
                act.dma_start(m.proj_raw[:, k, :], w).then_inc(m.proj_loaded, 16)
            act.dma_start(m.proj_bias[:, 0:1], m.bq.unsqueeze(1)).then_inc(m.proj_bias_loaded, 16)
            act.dma_start(m.proj_bias[:, 1:2], m.bk.unsqueeze(1)).then_inc(m.proj_bias_loaded, 16)
            act.dma_start(m.bv_rows[:, :], m.bv.partition_broadcast(P)).then_inc(m.proj_bias_loaded, 16)
            act.dma_start(m.bo_rows[:, :], m.bo.partition_broadcast(P)).then_inc(m.proj_bias_loaded, 16)
            act.dma_start(m.pos_k_raw[:, :, :], m.pos_k.rearrange("t s d -> s t d")).then_inc(m.pos_loaded, 16)
            act.wait_ge(m.const_step, 4)
            for p in range(2):
                act.dma_start(m.pos_v[p * S:(p + 1) * S, :, p * DH1:(p + 1) * DH1], m.pos_v_in.rearrange("t s d -> s t d")).then_inc(m.pos_loaded, 16)
            act.dma_start(m.Wr_sb[:, :], m.Wr).then_inc(m.moe_small_loaded, 16)
            act.dma_start(m.br_rows[:, :], m.br.partition_broadcast(P)).then_inc(m.moe_small_loaded, 16)
            act.dma_start(m.b2_sb[:, :], m.b2).then_inc(m.moe_small_loaded, 16)
            act.dma_start(m.b1_raw[:, :], m.b1.rearrange("e (c p) -> (e c) p", p=P)).then_inc(m.moe_small_loaded, 16)
            act.wait_ge(m.scales_loaded, 48)
            act.activation(m.tanh_g[:, :], m.tanh_g[:, :], ACT.Tanh).then_inc(m.tanh_ready, 1)

        @block.gpsimd
        def _(pool):
            step = Chain(pool, m.const_step)
            step.link(pool.memset(m.pos_v[:, :, :], 0.0))
            step.link(pool.memset(m.v_block[:, :, :, :, :], 0.0))
            for p in range(2):
                step.link(pool.memset(m.v_block[p * S:(p + 1) * S, :, :, p, DH1:DH1 + 1], 1.0))
            for mask, width in ((m.strip_mask, 32), (m.inner_mask, DH1)):
                for lo in range(0, P, P if width == 32 else 32):
                    rows = mask[lo:lo + (P if width == 32 else 32), :]
                    step.link(pool.memset(rows, 1.0))
                    step.link(pool.affine_select(out=rows, in_=rows, compare_op=ALU.is_ge, fill=0.0, base=0,
                                                 pattern=[[-width, 4]], channel_multiplier=1))
                    step.link(pool.affine_select(out=rows, in_=rows, compare_op=ALU.is_ge, fill=0.0, base=width - 1,
                                                 pattern=[[width, 4]], channel_multiplier=-1))
            step.link(pool.memset(m.ident[:, :], 0.0))
            step.link(pool.affine_select(out=m.ident[:, :], in_=m.ident[:, :], compare_op=ALU.not_equal, fill=1.0,
                                         base=0, pattern=[[-1, P]], channel_multiplier=1))
            step.link(pool.tensor_copy(m.ident_bf[:, :], m.ident[:, :]))
            step.link(pool.memset(m.ones[:, :], 1.0))
            step.link(pool.affine_select(out=m.cumsum_mat[:, :], in_=m.ones[:, :], compare_op=ALU.is_ge, fill=0.0,
                                         base=0, pattern=[[1, P]], channel_multiplier=-1))
            step.link(pool.memset(m.cumsum_mat[0:S, S:P], 0.0))
            step.link(pool.affine_select(out=m.head_mask[:, :], in_=m.ones[:, 0:NH0], compare_op=ALU.is_ge, fill=0.0,
                                         base=0, pattern=[[-DH0, NH0]], channel_multiplier=1))
            step.link(pool.affine_select(out=m.head_mask[:, :], in_=m.head_mask[:, :], compare_op=ALU.is_ge, fill=0.0,
                                         base=DH0 - 1, pattern=[[DH0, NH0]], channel_multiplier=-1))
            step.link(pool.memset(m.causal_add[:, :], 0.0))
            for c in range(2):
                half = m.causal_add[c * S:(c + 1) * S, :]
                step.link(pool.affine_select(out=half, in_=half, compare_op=ALU.is_ge, fill=FAR, base=0,
                                             pattern=[[1, S]], channel_multiplier=-1))
            for j in range(2):
                step.link(pool.memset(m.v_ones[j][:, :, DH0:DH0 + 1], 1.0))
            for k in (2, 5):
                step.link(pool.memset(m.gu_raw[96:P, k, :], 1.0))
            step.link(pool.memset(m.magic[:, :], MAGIC))
            step.link(pool.memset(m.minus_half[:, :], -0.5))


def stats_of(eng, m, tile):
    return eng.bn_stats(m.row_stats[:, tile, :], m.X[:, tile, :])


def finish_stats(nc, m, sm):
    stats = m.row_stats
    with nc.Block() as block:

        @block.vector
        def _(dve):
            step = Chain(dve, sm.dve)
            step.link(dve.tensor_tensor(m.row_mean[:, :], stats[:, :, 1], stats[:, :, 4], ALU.add))
            step.link(dve.tensor_scalar(m.row_mean[:, :], m.row_mean[:, :], 0.5, None, ALU.mult))
            step.link(dve.tensor_tensor(m.row_tmp[:, :], stats[:, :, 1], stats[:, :, 4], ALU.subtract))
            step.link(dve.scalar_tensor_tensor(m.row_tmp[:, :], m.row_tmp[:, :], 0.25, m.row_tmp[:, :], ALU.mult, ALU.mult))
            step.link(dve.tensor_tensor(m.row_rstd[:, :], stats[:, :, 2], stats[:, :, 5], ALU.add))
            step.link(dve.scalar_tensor_tensor(m.row_tmp[:, :], m.row_rstd[:, :], 1.0 / E, m.row_tmp[:, :], ALU.mult, ALU.add))
            step.link(dve.tensor_scalar(m.row_tmp[:, :], m.row_tmp[:, :], LN_EPS, None, ALU.add))
            dve.sem_inc(sm.variance, 1)

        @block.gpsimd
        def _(pool):
            pool.wait_ge(sm.variance, 1)
            pool.tensor_tensor(m.row_rstd[:, :], m.row_tmp[:, :], m.minus_half[:, 0:TILES], ALU.pow)


def normalize(eng, m, out, tile):
    return eng.tensor_scalar(out, m.X[:, tile, :], m.row_mean[:, cols(tile, 1)], m.row_rstd[:, cols(tile, 1)],
                             ALU.subtract, ALU.mult)


def l0_gates(nc, m):
    sm = m.gs
    with nc.Block() as block:

        @block.vector
        def _(dve):
            dve.wait_ge(m.x_loaded, 16)
            with dve.Fori(0, GROUPS) as g:
                for j in range(GROUP):
                    stats_of(dve, m, g * GROUP + j)
    finish_stats(nc, m, m.stat_sems[0])

    with nc.Block() as block:

        @block.gpsimd
        def _(pool):
            pool.wait_ge(m.ctx_loaded, 16)
            with pool.Fori(0, GROUPS) as g:
                pool.wait_ge(sm.ctx_turned, upto(g))
                pool.tensor_copy(m.stage_c[:, :, :], m.C[:, cols(g, GROUP), :]).then_inc(sm.ctx_staged, 1)
                pool.wait_ge(sm.xt_out, upto(g + 1))
                pool.tensor_copy(m.XT[:, cols(g, 512)], m.stage_xt[:, :]).then_inc(sm.stored, 1)
                pool.wait_ge(sm.ct_out, upto(g + 1))
                pool.tensor_copy(m.CT[:, cols(g, 512)], m.stage_ct[:, :]).then_inc(sm.stored, 1)

        @block.vector
        def _(dve):
            dve.wait_ge(m.gates_loaded, 64)
            dve.wait_ge(m.gw.turned, 3)
            for k in range(3):
                dve.tensor_copy(m.gate_w[:, k, :], m.ps[0][:, 16 * k:16 * k + 16]).then_inc(m.gw.ready, 1)
            with dve.Fori(0, GROUPS) as g:
                dve.wait_ge(sm.x_turned, upto(g))
                for j in range(GROUP):
                    normalize(dve, m, m.stage_x[:, j, :], g * GROUP + j).then_inc(sm.normed, 1)
                dve.wait_ge(sm.gates_done, upto(g + 1))
                dve.tensor_tensor(m.gates[:, cols(g, GROUP), :],
                                  m.ps[4][:, 0:64].rearrange("p (j n) -> p j n", j=GROUP),
                                  m.gate_bias[:, :].unsqueeze(1).to_broadcast([P, GROUP, 16]),
                                  ALU.add).then_inc(sm.gates_out, 1)

        @block.tensor
        def _(pe):
            pe.wait_ge(m.gates_loaded, 64)
            for k in range(3):
                pe.transpose(m.ps[0][:, 16 * k:16 * k + 16], m.gate_rows[0:16, k * P:(k + 1) * P],
                             m.ident[0:16, 0:16]).then_inc(m.gw.turned, 1)
            pe.wait_ge(m.gw.ready, 3)
            with pe.Fori(0, GROUPS) as g:
                pe.wait_ge(sm.normed, upto(g * GROUP + GROUP))
                pe.wait_ge(sm.xt_out, upto(g))
                for j in range(GROUP):
                    ins = pe.transpose(m.ps[1][:, j * P:(j + 1) * P], m.stage_x[:, j, :], m.ident[:, :])
                ins.then_inc(sm.x_turned, 1)
                pe.wait_ge(sm.ctx_staged, upto(g + 1))
                pe.wait_ge(sm.ct_out, upto(g))
                for j in range(GROUP):
                    ins = pe.transpose(m.ps[2][:, j * P:(j + 1) * P], m.stage_c[:, j, :], m.ident[:, :])
                ins.then_inc(sm.ctx_turned, 1)
                pe.wait_ge(sm.xt_out, upto(g + 1))
                pe.wait_ge(sm.ct_out, upto(g + 1))
                pe.wait_ge(sm.gates_out, upto(g))
                for j in range(GROUP):
                    tok = slice(j * P, (j + 1) * P)
                    out = m.ps[4][:, 16 * j:16 * j + 16]
                    pe.matmul(out, m.stage_xt[:, tok], m.gate_w[:, 0, :], start=True, stop=False)
                    pe.matmul(out, m.stage_ct[:, tok], m.gate_w[:, 1, :], start=False, stop=False)
                    ins = pe.matmul(out, m.stage_ct[:, tok], m.gate_w[:, 2, :], start=False, stop=True)
                ins.then_inc(sm.gates_done, 1)

        @block.scalar
        def _(act):
            with act.Fori(0, GROUPS) as g:
                act.wait_ge(sm.x_turned, upto(g + 1))
                act.wait_ge(sm.gates_done, upto(g))
                act.wait_ge(sm.stored, upto(2 * g))
                act.copy(m.stage_xt[:, :], m.ps[1][:, :]).then_inc(sm.xt_out, 1)
                act.wait_ge(sm.ctx_turned, upto(g + 1))
                act.copy(m.stage_ct[:, :], m.ps[2][:, :]).then_inc(sm.ct_out, 1)


def l0_gate_math(nc, m):
    sm = m.gm
    ig, fg = m.gates[:, :, 0:NH0], m.gates[:, :, NH0:2 * NH0]
    flat = m.logf[:, :, :].rearrange("p i h -> p (i h)")
    with nc.Block() as block:

        @block.scalar
        def _(act):
            step = Chain(act, sm.act)
            step.link(act.activation(m.softp[:, :, :], fg, ACT.Abs))
            step.link(act.activation(m.softp[:, :, :], m.softp[:, :, :], ACT.Exp, scale=-1.0))
            act.activation(m.softp[:, :, :], m.softp[:, :, :], ACT.Ln, bias=1.0).then_inc(sm.log1p, 1)
            act.wait_ge(sm.neg, 1)
            act.activation(m.exp_neg_max[:, :, :], m.exp_neg_max[:, :, :], ACT.Exp, scale=-1.0)

        @block.vector
        def _(dve):
            step = Chain(dve, sm.dve)
            step.link(dve.tensor_scalar(m.logf[:, :, :], fg, 0.0, None, ALU.min))
            dve.wait_ge(sm.log1p, 1)
            dve.tensor_tensor(m.logf[:, :, :], m.logf[:, :, :], m.softp[:, :, :], ALU.subtract).then_inc(sm.logf, 1)
            dve.wait_ge(sm.summed, 1)
            dve.tensor_copy(m.cumsum[:, :], m.ps[0][:, 0:256]).then_inc(sm.dve2, 1)
            dve.wait_ge(sm.dve2, 1)
            dve.tensor_tensor(m.g_nat[:, :, :], ig, m.cumsum[:, :].rearrange("p (i h) -> p i h", h=NH0),
                              ALU.subtract).then_inc(sm.g, 1)
            dve.wait_ge(sm.g_turned, 1)
            dve.tensor_copy(m.g_t[:, :, :], m.ps[1][:, 0:256].rearrange("p (u t) -> p u t", u=2)).then_inc(sm.dve2, 1)
            dve.wait_ge(sm.dve2, 2)
            for u in range(2):
                for c in range(2):
                    part = m.g_t[:, u, c * S:(c + 1) * S]
                    dve.tensor_tensor_scan(m.gmax_t[:, u, c * S:(c + 1) * S], part, part, -3e38,
                                           ALU.max, ALU.max).then_inc(sm.gmax, 1)
            dve.wait_ge(sm.gmax_turned, 1)
            dve.tensor_tensor(m.exp_neg_max[:, :, :].rearrange("p i h -> p (i h)"), m.ps[2][:, 0:256],
                              m.cumsum[:, :], ALU.add).then_inc(sm.neg, 1)

        @block.tensor
        def _(pe):
            pe.wait_ge(sm.logf, 1)
            pe.matmul(m.ps[0][:, 0:256], m.cumsum_mat[:, :], flat, start=True, stop=True).then_inc(sm.summed, 1)
            pe.wait_ge(sm.g, 1)
            g = m.g_nat[:, :, :].rearrange("p i h -> p (i h)")
            pe.transpose(m.ps[1][:, 0:P], g[:, 0:P], m.ident[:, :])
            pe.transpose(m.ps[1][:, P:2 * P], g[:, P:2 * P], m.ident[:, :]).then_inc(sm.g_turned, 1)
            pe.wait_ge(sm.gmax, 4)
            pe.transpose(m.ps[2][:, 0:P], m.gmax_t[:, 0, :], m.ident[:, :])
            pe.transpose(m.ps[2][:, P:2 * P], m.gmax_t[:, 1, :], m.ident[:, :]).then_inc(sm.gmax_turned, 1)

        @block.sync
        def _(sp):
            sp.wait_ge(sm.gmax, 4)
            for u in range(2):
                for c in range(2):
                    rows = m.gmax_dram[c, u * 16:(u + 1) * 16].rearrange("i h s -> (i h) s")
                    sp.dma_start(rows, m.gmax_t[:, u, c * S:(c + 1) * S]).then_inc(sm.saved, 16)
            sp.wait_ge(sm.saved, 64)


def l0_attention(nc, m):
    sm = m.at
    W = DH0 + 1
    with nc.Block() as block:

        @block.sync
        def _(sp):
            with sp.Fori(0, TILES // 2) as g:
                for j in range(2):
                    i = g * 2 + j
                    sp.wait_ge(sm.diff[j], upto(g))
                    for c in range(2):
                        row = m.gmax_dram[c, cols(i, 1)].rearrange("i h s -> (i h s)")
                        sp.dma_start(m.g_rows[j][c * S:(c + 1) * S, :], row.partition_broadcast(S)).then_inc(m.rows[j], 16)

        @block.gpsimd
        def _(pool):
            mask = m.head_mask[:, :].unsqueeze(2).to_broadcast([P, NH0, P])
            causal = m.causal_add[:, :].unsqueeze(1).to_broadcast([P, NH0, S])
            with pool.Fori(0, TILES // 2) as g:
                for j in range(2):
                    i = g * 2 + j
                    pool.wait_ge(sm.qk[j], upto(g))
                    q = m.XT[:, cols(i, P)].unsqueeze(1).to_broadcast([P, NH0, P])
                    pool.tensor_tensor(m.q_spread[j][:, :, :], q, mask, ALU.mult).then_inc(sm.spread[j], 1)
                    pool.wait_ge(sm.av[j], upto(g))
                    pool.tensor_copy(m.v_ones[j][:, :, 0:DH0],
                                     m.C[:, cols(i, 1), :].rearrange("p i (h d) -> p (i h) d", h=NH0)).then_inc(sm.v[j], 1)
                    pool.wait_ge(sm.diff[j], upto(g + 1))
                    pool.tensor_tensor(m.decay[j][:, :, :], m.decay[j][:, :, :], causal, ALU.add).then_inc(sm.causal[j], 1)

        @block.vector
        def _(dve):
            def difference(g, j):
                dve.wait_ge(m.rows[j], 32 * g + 32)
                own = m.g_nat[:, cols(g * 2 + j, 1), :].rearrange("p i h -> p (i h)").unsqueeze(2).to_broadcast([P, NH0, S])
                dve.tensor_tensor(m.decay[j][:, :, :], own, m.g_rows[j][:, :].rearrange("p (h s) -> p h s", h=NH0),
                                  ALU.subtract).then_inc(sm.diff[j], 1)

            with dve.Fori(0, TILES // 2) as g:
                for j in range(2):
                    dve.wait_ge(sm.c[j], upto(g))
                    difference(g, j)
                for j in range(2):
                    dve.wait_ge(sm.exp[j], upto(g + 1))
                    dve.wait_ge(sm.qk[j], upto(g + 1))
                    dve.wait_ge(sm.av[j], upto(g))
                    dve.tensor_tensor(m.c_t[j][:, :, :], m.ps[j][:, :].rearrange("p (h s) -> p h s", h=NH0),
                                      m.decay[j][:, :, :], ALU.mult).then_inc(sm.c[j], 1)

        @block.scalar
        def _(act):
            with act.Fori(0, TILES // 2) as g:
                for j in range(2):
                    act.wait_ge(sm.qk[j], upto(g))
                    act.activation(m.k_stage[j][:, :], m.CT[:, cols(g * 2 + j, P)], ACT.Copy, scale=DH0 ** -0.5).then_inc(sm.k[j], 1)
                for j in range(2):
                    act.wait_ge(sm.causal[j], upto(g + 1))
                    act.activation(m.decay[j][:, :, :], m.decay[j][:, :, :], ACT.Exp).then_inc(sm.exp[j], 1)
                for j in range(2):
                    act.wait_ge(sm.av[j], upto(g + 1))
                    for c in range(2):
                        act.copy(m.num[c * S:(c + 1) * S, cols(g * 2 + j, 1), :],
                                 m.ps[2 + 2 * j + c][c * S:(c + 1) * S, 0:NH0 * W].unsqueeze(1)).then_inc(sm.out[j], 1)

        @block.tensor
        def _(pe):
            with pe.Fori(0, TILES // 2) as g:
                for j in range(2):
                    pe.wait_ge(sm.k[j], upto(g + 1))
                    pe.wait_ge(sm.spread[j], upto(g + 1))
                    pe.wait_ge(sm.c[j], upto(g))
                    for c in range(2):
                        half = slice(c * S, (c + 1) * S)
                        ins = pe.matmul(m.ps[j][half, :], m.k_stage[j][:, half], m.q_spread[j][:, :, half],
                                        start=True, stop=True)
                    ins.then_inc(sm.qk[j], 1)
                for j in range(2):
                    pe.wait_ge(sm.c[j], upto(g + 1))
                    pe.wait_ge(sm.v[j], upto(g + 1))
                    pe.wait_ge(sm.out[j], upto(2 * g))
                    hold(pe, m)
                    for h in range(NH0):
                        for c in range(2):
                            half = slice(c * S, (c + 1) * S)
                            ins = pe.matmul(m.ps[2 + 2 * j + c][half, h * W:(h + 1) * W], m.c_t[j][half, h, :],
                                            m.v_ones[j][half, h, :], start=True, stop=True)
                    ins.then_inc(sm.av[j], 1)


def l0_attention_finish(nc, m):
    sm = m.af
    W = DH0 + 1
    num = m.num[:, :, :].rearrange("p i (h w) -> p (i h) w", w=W)
    hid = m.hid[:, :, :]
    N = TILES * NH0
    wide = [P, N, DH0]
    with nc.Block() as block:

        @block.vector
        def _(dve):
            step = Chain(dve, sm.dve)
            step.link(dve.scalar_tensor_tensor(m.den[:, :], num[:, :, DH0], -1.0, num[:, :, DH0], ALU.mult, ALU.max))
            step.link(dve.tensor_tensor(m.den[:, :], m.den[:, :], m.exp_neg_max[:, :, :].rearrange("p i h -> p (i h)"), ALU.max))
            step.link(dve.tensor_scalar(m.den[:, :], m.den[:, :], NORM_EPS, None, ALU.add))
            step.link(dve.reciprocal(m.den[:, :], m.den[:, :]))
            step.link(dve.tensor_tensor(hid, num[:, :, 0:DH0], m.den[:, :].unsqueeze(2).to_broadcast(wide), ALU.mult))
            step.link(dve.tensor_reduce(m.hmean[:, :], hid, AX, ALU.add))
            step.link(dve.tensor_scalar(m.hmean[:, :], m.hmean[:, :], 1.0 / DH0, None, ALU.mult))
            step.link(dve.tensor_tensor(hid, hid, m.hmean[:, :].unsqueeze(2).to_broadcast(wide), ALU.subtract))
            dve.sem_inc(sm.centered, 1)
            dve.wait_ge(sm.squared, 1)
            step.link(dve.tensor_reduce(m.hvar[:, :], m.hsq[:, :, :], AX, ALU.add))
            step.link(dve.tensor_scalar(m.hvar[:, :], m.hvar[:, :], 1.0 / DH0, LN_EPS, ALU.mult, ALU.add))
            dve.sem_inc(sm.var, 1)
            dve.wait_ge(m.tanh_ready, 1)
            step.link(dve.tensor_scalar(m.out_w_rows[:, :], m.out_w_rows[:, :], m.tanh_g[:, 0:1], None, ALU.mult))
            dve.wait_ge(sm.rstd, 1)
            step.link(dve.tensor_tensor(hid, hid, m.hvar[:, :].unsqueeze(2).to_broadcast(wide), ALU.mult))
            tiles = hid.rearrange("p (i h) d -> p i (h d)", h=NH0)
            step.link(dve.tensor_tensor(tiles, tiles, m.out_w_rows[:, :].unsqueeze(1).to_broadcast([P, TILES, E]), ALU.mult))
            step.link(dve.tensor_tensor(m.X[:, :, :], m.X[:, :, :], tiles, ALU.add))
            with dve.Fori(0, GROUPS) as g:
                for j in range(GROUP):
                    stats_of(dve, m, g * GROUP + j)

        @block.scalar
        def _(act):
            act.wait_ge(sm.centered, 1)
            act.activation(m.hsq[:, :, :], hid, ACT.Square).then_inc(sm.squared, 1)

        @block.gpsimd
        def _(pool):
            pool.wait_ge(sm.var, 1)
            half = m.minus_half[:, 0:1].to_broadcast([P, N])
            pool.tensor_tensor(m.hvar[:, :], m.hvar[:, :], half, ALU.pow).then_inc(sm.rstd, 1)


def l0_ffn_weights(nc, m):
    sm = m.fw
    with nc.Block() as block:

        @block.vector
        def _(dve):
            step = Chain(dve, sm.dve)
            dve.wait_ge(m.ffn0_loaded, 80)
            for raw, q, top, scale, n in ((m.gu_raw, m.gu_q, m.gu_top, m.gu_scale, 6), (m.dn_raw, m.dn_q, m.dn_top, m.dn_scale, 1)):
                wide = list(raw.shape)
                step.link(dve.tensor_reduce(top[:, :], raw, AX, ALU.max, apply_absolute_value=True))
                step.link(dve.tensor_scalar(scale[:, :], top[:, :], 1.0 / QMAX, None, ALU.mult))
                step.link(dve.reciprocal(top[:, :], scale[:, :]))
                step.link(dve.tensor_tensor(raw, raw, top[:, :].unsqueeze(2).to_broadcast(wide), ALU.mult))
                step.link(dve.tensor_scalar(raw, raw, MAGIC, None, ALU.add))
                step.link(dve.tensor_scalar(raw, raw, MAGIC + QMAX, MAGIC - QMAX - 1, ALU.min, ALU.max))
                step.link(dve.tensor_scalar(q, raw, MAGIC, None, ALU.subtract))
            step.link(dve.tensor_scalar(m.dn_diag[:, :], m.ident[:, :], m.dn_scale[:, 0:1], None, ALU.mult))
            dve.sem_inc(sm.quantized, 1)
            dve.wait_ge(sm.turned, 1)
            dve.tensor_copy(m.gu_t[:, :, :], m.ps[0][:, :].bitcast(BF16)[:, 0:6 * P].rearrange("p (k n) -> p k n", k=6)).then_inc(sm.dve, 1)
            dve.tensor_copy(m.dn_t[:, 0:2, :], m.ps[1][:, :].bitcast(BF16)[:, 0:2 * P].rearrange("p (k n) -> p k n", k=2))
            dve.tensor_copy(m.dn_t[0:96, 2, :], m.ps[1][0:96, :].bitcast(BF16)[:, 2 * P:3 * P])
            dve.tensor_copy(m.dn_row[:, :], m.ps[2][:, 0:P])

        @block.gpsimd
        def _(pool):
            pool.memset(m.dn_t[96:P, 2, :], 0.0)

        @block.tensor
        def _(pe):
            pe.wait_ge(sm.quantized, 1)
            for k in range(6):
                pe.transpose(m.ps[0][:, :].bitcast(BF16)[:, k * P:(k + 1) * P], m.gu_q[:, k, :], m.ident_bf[:, :])
            for k, n in enumerate((P, P, 96)):
                pe.transpose(m.ps[1][0:n, :].bitcast(BF16)[:, k * P:(k + 1) * P], m.dn_q[:, 0, k * P:k * P + n], m.ident_bf[:, :])
            pe.matmul(m.ps[2][:, 0:P], m.ones[:, :], m.dn_diag[:, :], start=True, stop=True).then_inc(sm.turned, 1)


def l0_ffn_norm(nc, m):
    with nc.Block() as block:

        @block.vector
        def _(dve):
            with dve.Fori(0, GROUPS) as g:
                for j in range(GROUP):
                    normalize(dve, m, m.XN[:, cols(g * GROUP + j, 1), :].rearrange("p i f -> p (i f)"),
                              g * GROUP + j).then_inc(m.fn.normed, 1)
                dve.wait_ge(m.fn.normed, upto(g * GROUP + GROUP))
                dve.tensor_reduce(m.x_top[:, cols(g, 1)], m.XN[:, cols(g, GROUP), :].rearrange("p i f -> p (i f)"),
                                  AX, ALU.max, apply_absolute_value=True)


def activation_scale(nc, m, sm, tops, clip, scales):
    with nc.Block() as block:

        @block.scalar
        def _(act):
            act.wait_ge(m.clips_loaded, 32)
            act.activation(m.clip_exp[0:1, :], clip, ACT.Exp, scale=-1.0).then_inc(sm.exp, 1)

        @block.vector
        def _(dve):
            step = Chain(dve, sm.dve)
            step.link(dve.tensor_reduce(m.top_col[:, :], tops, AX, ALU.max))
            dve.sem_inc(sm.col, 1)
            dve.wait_ge(sm.row, 1)
            step.link(dve.tensor_reduce(m.top_one[:, 0:1], m.ps[0][0:1, 0:P], AX, ALU.max))
            dve.wait_ge(sm.exp, 1)
            step.link(dve.tensor_scalar(m.top_one[:, 1:2], m.clip_exp[0:1, :], 1.0, None, ALU.add))
            step.link(dve.reciprocal(m.top_one[:, 1:2], m.top_one[:, 1:2]))
            step.link(dve.scalar_tensor_tensor(m.top_pair[:, 0:1], m.top_one[:, 0:1], 1.0 / QMAX, m.top_one[:, 1:2], ALU.mult, ALU.mult))
            step.link(dve.reciprocal(m.top_pair[:, 1:2], m.top_pair[:, 0:1]))
            dve.sem_inc(sm.pair, 1)
            dve.wait_ge(sm.spread, 1)
            dve.tensor_copy(scales[:, :], m.ps[1][:, 0:2])

        @block.tensor
        def _(pe):
            pe.wait_ge(sm.col, 1)
            pe.transpose(m.ps[0][0:1, 0:P], m.top_col[:, :], m.ident[:, :]).then_inc(sm.row, 1)
            pe.wait_ge(sm.pair, 1)
            pe.matmul(m.ps[1][:, 0:2], m.ones[0:1, :], m.top_pair[:, :], start=True, stop=True).then_inc(sm.spread, 1)


def l0_ffn_up(nc, m):
    sm = m.fu
    with nc.Block() as block:

        @block.vector
        def _(dve):
            dve.tensor_scalar(m.gu_scale[:, :], m.gu_scale[:, :], m.x_scale[:, 0:1], None, ALU.mult).then_inc(sm.scaled, 1)
            dve.wait_ge(sm.scaled, upto(1))
            with dve.Fori(0, GROUPS) as g:
                dve.wait_ge(sm.shifted, upto(g + 1))
                dve.tensor_scalar(m.round_x[:, :], m.round_x[:, :], MAGIC + QMAX, MAGIC - QMAX - 1, ALU.min, ALU.max).then_inc(sm.clipped, 1)
                dve.wait_ge(sm.clipped, upto(g + 1))
                dve.wait_ge(sm.turned, upto(g))
                dve.tensor_scalar(m.xq[:, :], m.round_x[:, :], MAGIC, None, ALU.subtract).then_inc(sm.quantized, 1)
                dve.wait_ge(sm.turned, upto(g + 1))
                dve.wait_ge(sm.upped, upto(3 * g))
                dve.tensor_copy(m.xq_t[:, :], m.ps[0][:, :].bitcast(BF16)[:, 0:512]).then_inc(sm.stood, 1)
                for k, n in enumerate(CHUNKS):
                    dve.wait_ge(sm.silu, upto(3 * g + k + 1))
                    h = m.HT[0:n, k, cols(g, 512)]
                    dve.scalar_tensor_tensor(h, m.ps[2 + 2 * k][0:n, :], m.gu_scale[0:n, 3 + k:4 + k],
                                             m.silu[k][0:n, :], ALU.mult, ALU.mult).then_inc(sm.hidden, 1)
                    dve.wait_ge(sm.hidden, upto(3 * g + k + 1))
                    dve.tensor_reduce(m.h_top[0:n, k, cols(g, 1)], h, AX, ALU.max, apply_absolute_value=True)

        @block.scalar
        def _(act):
            act.wait_ge(sm.scaled, upto(1))
            with act.Fori(0, GROUPS) as g:
                act.wait_ge(sm.quantized, upto(g))
                act.activation(m.round_x[:, :], m.XN[:, cols(g, GROUP), :].rearrange("p i f -> p (i f)"), ACT.Identity,
                               bias=m.magic[:, 0:1], scale=m.x_scale[:, 1:2]).then_inc(sm.shifted, 1)
                for k, n in enumerate(CHUNKS):
                    act.wait_ge(sm.upped, upto(3 * g + k + 1))
                    act.wait_ge(sm.hidden, upto(3 * g))
                    act.activation(m.silu[k][0:n, :], m.ps[1 + 2 * k][0:n, :], ACT.Silu, scale=m.gu_scale[0:n, k:k + 1]).then_inc(sm.silu, 1)

        @block.gpsimd
        def _(pool):
            pool.memset(m.HT[96:P, 2, :], 0.0)
            pool.memset(m.h_top[96:P, 2, :], 0.0)

        @block.tensor
        def _(pe):
            with pe.Fori(0, GROUPS) as g:
                pe.wait_ge(sm.quantized, upto(g + 1))
                pe.wait_ge(sm.stood, upto(g))
                for j in range(GROUP):
                    ins = pe.transpose(m.ps[0][:, :].bitcast(BF16)[:, j * P:(j + 1) * P], m.xq[:, j * P:(j + 1) * P], m.ident_bf[:, :])
                ins.then_inc(sm.turned, 1)
                pe.wait_ge(sm.stood, upto(g + 1))
                for k, n in enumerate(CHUNKS):
                    pe.wait_ge(sm.hidden, upto(3 * g))
                    pe.matmul(m.ps[1 + 2 * k][0:n, :], m.gu_t[:, k, 0:n], m.xq_t[:, :], start=True, stop=True)
                    pe.matmul(m.ps[2 + 2 * k][0:n, :], m.gu_t[:, 3 + k, 0:n], m.xq_t[:, :], start=True, stop=True).then_inc(sm.upped, 1)


def l0_ffn_down(nc, m):
    sm = m.fd
    with nc.Block() as block:

        @block.vector
        def _(dve):
            step = Chain(dve, sm.dve)
            step.link(dve.tensor_scalar(m.dn_row[:, :], m.dn_row[:, :], m.h_scale[:, 0:1], m.tanh_g[:, 2:3], ALU.mult, ALU.mult))
            scale = m.dn_row[:, :].unsqueeze(1).to_broadcast([P, GROUP, E])
            with dve.Fori(0, GROUPS) as g:
                dve.wait_ge(sm.shifted, upto(g + 1))
                dve.tensor_scalar(m.round_h[:, :, :], m.round_h[:, :, :], MAGIC + QMAX, MAGIC - QMAX - 1, ALU.min, ALU.max).then_inc(sm.clipped, 1)
                dve.wait_ge(sm.clipped, upto(g + 1))
                dve.wait_ge(sm.downed, upto(g))
                dve.tensor_scalar(m.hq[:, :, :], m.round_h[:, :, :], MAGIC, None, ALU.subtract).then_inc(sm.quantized, 1)
                dve.wait_ge(sm.downed, upto(g + 1))
                dve.tensor_tensor(m.down[:, :, :], m.ps[0][:, :].rearrange("p (j f) -> p j f", j=GROUP), scale, ALU.mult).then_inc(sm.out, 1)
                dve.wait_ge(sm.out, upto(g + 1))
                x = m.X[:, cols(g, GROUP), :]
                dve.tensor_tensor(x, x, m.down[:, :, :], ALU.add).then_inc(sm.added, 1)
                dve.wait_ge(sm.added, upto(g + 1))
                for j in range(GROUP):
                    stats_of(dve, m, g * GROUP + j)

        @block.scalar
        def _(act):
            with act.Fori(0, GROUPS) as g:
                act.wait_ge(sm.quantized, upto(g))
                act.activation(m.round_h[:, :, :], m.HT[:, :, cols(g, 512)], ACT.Identity, bias=m.magic[:, 0:1],
                               scale=m.h_scale[:, 1:2]).then_inc(sm.shifted, 1)

        @block.tensor
        def _(pe):
            with pe.Fori(0, GROUPS) as g:
                pe.wait_ge(sm.quantized, upto(g + 1))
                pe.wait_ge(sm.out, upto(g))
                for j in range(GROUP):
                    for k in range(3):
                        ins = pe.matmul(m.ps[0][:, j * P:(j + 1) * P], m.hq[:, k, j * P:(j + 1) * P], m.dn_t[:, k, :],
                                        start=(k == 0), stop=(k == 2))
                ins.then_inc(sm.downed, 1)


def l1_weights(nc, m):
    sm = m.lw
    with nc.Block() as block:

        @block.tensor
        def _(pe):
            pe.wait_ge(m.proj_loaded, 64)
            for k in range(4):
                ins = pe.transpose(m.ps[0][:, k * P:(k + 1) * P], m.proj_raw[:, k, :], m.ident[:, :])
            pe.wait_ge(m.pos_loaded, 48)
            for k in range(4):
                ins = pe.transpose(m.ps[1][:, k * S:(k + 1) * S],
                                   m.pos_k_raw[:, :, :].rearrange("s t d -> s (t d)")[:, k * P:(k + 1) * P], m.ident[0:S, 0:S])
            ins.then_inc(sm.turned, 1)

        @block.vector
        def _(dve):
            dve.wait_ge(sm.turned, 1)
            dve.tensor_copy(m.proj_t[:, :, :], m.ps[0][:, :].rearrange("p (k n) -> p k n", k=4))
            dve.tensor_copy(m.pos_k_td[:, :, :], m.ps[1][:, 0:4 * S].rearrange("p (k s) -> p k s", k=4)).then_inc(sm.stood, 1)
            dve.wait_ge(m.proj_bias_loaded, 64)
            dve.tensor_scalar(m.bo_rows[:, :], m.bo_rows[:, :], m.tanh_g[:, 1:2], None, ALU.mult)

        @block.sync
        def _(sp):
            sp.wait_ge(sm.stood, 1)
            pos = m.pos_k8[:, :, :].rearrange("d (k t) s -> d k t s", k=4)
            for t in range(16):
                sp.dma_start(pos[:, :, t, :], m.pos_k_td[DH1 * t:DH1 * (t + 1), :, :]).then_inc(sm.moved, 16)
            sp.wait_ge(sm.moved, 256)


def l1_project(nc, m):
    sm = m.pj
    with nc.Block() as block:

        @block.vector
        def _(dve):
            with dve.Fori(0, GROUPS) as g:
                dve.wait_ge(sm.turned, upto(g))
                for j in range(GROUP):
                    normalize(dve, m, m.stage_x[:, j, :], g * GROUP + j).then_inc(sm.normed, 1)

        @block.tensor
        def _(pe):
            with pe.Fori(0, GROUPS) as g:
                pe.wait_ge(sm.xt_out, upto(g))
                pe.wait_ge(sm.normed, upto(g * GROUP + GROUP))
                for j in range(GROUP):
                    ins = pe.transpose(m.ps[0][:, j * P:(j + 1) * P], m.stage_x[:, j, :], m.ident[:, :])
                ins.then_inc(sm.turned, 1)
                pe.wait_ge(sm.q_out, upto(g))
                pe.wait_ge(sm.k_out, upto(g))
                pe.matmul(m.ps[2][:, :], m.proj_t[:, 1, :], m.CT[:, cols(g, 512)], start=True, stop=True).then_inc(sm.k_done, 1)
                pe.wait_ge(sm.xt_out, upto(g + 1))
                pe.matmul(m.ps[1][:, :], m.proj_t[:, 0, :], m.stage_xt[:, :], start=True, stop=True).then_inc(sm.q_done, 1)
                pe.wait_ge(sm.q_back, upto(16 * g + 16))
                q = m.q8[:, :, :].rearrange("d h (b t) -> d (h b) t", t=S)
                for n in range(8):
                    bank = 3 + n % 4
                    pe.wait_ge(sm.rel_out, upto(8 * g + max(n - 3, 0)))
                    for t in range(8):
                        ins = pe.matmul(m.ps[bank][:, t * S:(t + 1) * S], q[:, :, 8 * n + t], m.pos_k8[:, 8 * n + t, :],
                                        start=True, stop=True)
                    ins.then_inc(sm.rel_done, 1)

        @block.scalar
        def _(act):
            with act.Fori(0, GROUPS) as g:
                act.wait_ge(sm.turned, upto(g + 1))
                act.wait_ge(sm.q_done, upto(g))
                act.copy(m.stage_xt[:, :], m.ps[0][:, :]).then_inc(sm.xt_out, 1)
                act.wait_ge(sm.k_done, upto(g + 1))
                act.activation(m.KT[:, cols(g, 512)], m.ps[2][:, :], ACT.Identity, bias=m.proj_bias[:, 1:2]).then_inc(sm.k_out, 1)
                act.wait_ge(sm.q_done, upto(g + 1))
                act.activation(m.QT[:, cols(g, 512)], m.ps[1][:, :], ACT.Identity, bias=m.proj_bias[:, 0:1]).then_inc(sm.q_out, 1)
                for n in range(8):
                    half = n // 4
                    act.wait_ge(sm.rel_done, upto(8 * g + n + 1))
                    if n % 4 == 0:
                        act.wait_ge(sm.rel_saved[half], upto(16 * g))
                    act.copy(m.rel[half][:, 512 * (n % 4):512 * (n % 4 + 1)], m.ps[3 + n % 4][:, :]).then_inc(sm.rel_out, 1)

        @block.sync
        def _(sp):
            with sp.Fori(0, GROUPS) as g:
                sp.wait_ge(sm.q_out, upto(g + 1))
                hold(sp, m)
                sp.dma_start(m.q_dram[:, cols(g, 512)], m.QT[:, cols(g, 512)]).then_inc(sm.q_saved, 16)
                sp.wait_ge(sm.q_saved, upto(16 * g + 16))
                sp.wait_ge(sm.rel_done, upto(8 * g))
                hold(sp, m)
                sp.dma_start(m.q8[:, :, :], m.q_dram[:, cols(g, 512)].rearrange("(h d) t -> d h t", d=DH1)).then_inc(sm.q_back, 16)
                for half in range(2):
                    sp.wait_ge(sm.rel_out, upto(8 * g + 4 * half + 4))
                    hold(sp, m)
                    rows = m.rel_dram[cols(g, 1)].rearrange("g h b t s -> (g h b) (t s)")
                    sp.dma_start(rows[:, 2048 * half:2048 * (half + 1)], m.rel[half][:, :]).then_inc(sm.rel_saved[half], 16)
            for half in range(2):
                sp.wait_ge(sm.rel_saved[half], upto(16 * GROUPS))


def l1_attention(nc, m):
    sm = m.a1
    W = DH1 + 1
    scores = m.wide[0][:, :]
    turned = m.wide[1][:, :]
    rel_v = m.wide[2][0:S, :]
    with nc.Block() as block:

        @block.sync
        def _(sp):
            with sp.Fori(0, GROUPS) as g:
                for j in range(GROUP):
                    i = g * GROUP + j
                    z = j % 2
                    sp.wait_ge(sm.added, upto(g * GROUP + max(j - 1, 0)))
                    hold(sp, m)
                    for c in range(2):
                        sp.dma_start(m.rel_in[z][c * S:(c + 1) * S, :, :],
                                     m.rel_dram[cols(g, 1), :, 2 * j + c].rearrange("g h t s -> (g t) h s")).then_inc(m.rel_sem[j], 16)
                    sp.wait_ge(sm.masked, upto(g * GROUP + max(j - 1, 0)))
                    hold(sp, m)
                    sp.dma_start(m.mask_in[z][:, :], m.mask[cols(i, 2)].rearrange("b t s -> (b t) s")).then_inc(m.mask_sem[j], 16)
                sp.wait_ge(sm.pv_out, upto(g + 1))
                hold(sp, m)
                sp.dma_start(m.pv_dram[cols(g, 1)].rearrange("g n t e -> (g n) (t e)"), m.pv[:, :]).then_inc(sm.pv_saved, 16)
                sp.wait_ge(sm.pv_saved, upto(16 * g + 16))
                hold(sp, m)
                sp.wait_ge(sm.summed, upto(g))
                hold(sp, m)
                sp.dma_start(m.pv_in[:, :, :], m.pv_dram[cols(g, 1)].rearrange("g (n c) t e -> (g c t) n e", c=2)).then_inc(sm.pv_back, 16)

        @block.gpsimd
        def _(pool):
            with pool.Fori(0, GROUPS) as g:
                for j in range(GROUP):
                    pool.wait_ge(sm.v_done, upto(g * GROUP + j))
                    src = m.CT[:, cols(g * GROUP + j, P)].rearrange("p (c s) -> p c s", c=2)
                    for twice in range(2):
                        pool.tensor_copy(m.ct_twice[:, :, twice, :], src).then_inc(sm.ct_staged, 1)

        @block.vector
        def _(dve):
            strips = m.strip_mask[:, :].unsqueeze(2).to_broadcast([P, 4, P])
            inner = m.inner_mask[:, :].unsqueeze(2).to_broadcast([P, 4, P])
            with dve.Fori(0, GROUPS) as g:
                for j in range(GROUP):
                    n = g * GROUP + j
                    z = j % 2
                    dve.wait_ge(m.mask_sem[j], 16 * g + 16)
                    dve.wait_ge(sm.scored, upto(g * GROUP + max(j - 1, 0)))
                    dve.tensor_scalar(m.mask_add[z][:, :], m.mask_in[z][:, :], 0.0, FAR, ALU.is_equal, ALU.mult).then_inc(sm.masked, 1)
                    q = m.QT[:, cols(n, P)].unsqueeze(1).to_broadcast([P, 4, P])
                    k = m.KT[:, cols(n, P)].unsqueeze(1).to_broadcast([P, 4, P])
                    dve.tensor_tensor(m.q_strip[z][:, :, :], q, strips, ALU.mult).then_inc(sm.spread, 1)
                    dve.tensor_tensor(m.k_inner[z][:, :, :], k, inner, ALU.mult).then_inc(sm.spread, 1)
                    dve.wait_ge(sm.v_done, upto(n + 1))
                    dve.wait_ge(sm.av_done, upto(n))
                    for c in range(2):
                        for p in range(2):
                            half = slice(p * S, (p + 1) * S)
                            src = m.ps7[half, c * P:(c + 1) * P].rearrange("s (n p d) -> s n p d", p=2, d=DH1)[:, :, p, :]
                            bias = m.bv_rows[half, :].rearrange("s (n p d) -> s n p d", p=2, d=DH1)[:, :, p, :]
                            dve.tensor_tensor(m.v_block[half, :, c, p, 0:DH1], src, bias, ALU.add).then_inc(sm.v_out, 1)
                    dve.wait_ge(m.rel_sem[j], 32 * g + 32)
                    dve.wait_ge(sm.scored, upto(n + 1))
                    dve.wait_ge(sm.exped, upto(g * GROUP + max(j - 1, 0)))
                    t = m.soft[z][:, :, :]
                    dve.tensor_tensor(t, scores.rearrange("p (h s) -> p h s", s=S), m.rel_in[z][:, :, :], ALU.add).then_inc(sm.added, 1)
                    dve.wait_ge(sm.added, upto(n + 1))
                    dve.tensor_reduce(m.row_max[:, :], t, AX, ALU.max).then_inc(sm.maxed, 1)
                    dve.wait_ge(sm.maxed, upto(2 * n + 1))
                    dve.tensor_scalar(m.row_max[:, :], m.row_max[:, :], FAR / 10, None, ALU.max).then_inc(sm.maxed, 1)
                    dve.wait_ge(sm.maxed, upto(2 * n + 2))
                    dve.tensor_tensor(t, t, m.row_max[:, :].unsqueeze(2).to_broadcast([P, NH1, S]), ALU.subtract).then_inc(sm.shifted, 1)
                dve.wait_ge(sm.pv_back, upto(16 * g + 16))
                dve.wait_ge(sm.av_out, upto(8 * g + 8))
                av = m.av[:, :, :].rearrange("p i (h w) -> p (i h) w", w=W)
                dve.tensor_scalar(m.row_sum[:, :], av[:, :, DH1], 1e-30, None, ALU.max).then_inc(sm.small, 1)
                dve.wait_ge(sm.small, upto(4 * g + 1))
                dve.reciprocal(m.row_sum[:, :], m.row_sum[:, :]).then_inc(sm.small, 1)
                att = m.att[:, :, :].rearrange("p i (h d) -> p (i h) d", d=DH1)
                pv = m.pv_in[:, :, :].rearrange("p n (q d) -> p (n q) d", d=DH1)
                dve.wait_ge(sm.att_turned, upto(g))
                dve.tensor_tensor(att, av[:, :, 0:DH1], pv, ALU.add).then_inc(sm.summed, 1)
                dve.wait_ge(sm.summed, upto(g + 1))
                dve.wait_ge(sm.small, upto(4 * g + 2))
                dve.tensor_tensor(att, att, m.row_sum[:, :].unsqueeze(2).to_broadcast([P, GROUP * NH1, DH1]), ALU.mult).then_inc(sm.att_done, 1)
                dve.wait_ge(sm.wo_done, upto(g + 1))
                bo = m.bo_rows[:, :].unsqueeze(1).to_broadcast([P, GROUP, E])
                dve.scalar_tensor_tensor(m.res[:, :, :], m.ps7[:, :].rearrange("p (i f) -> p i f", f=E), m.tanh_g[:, 1:2],
                                         bo, ALU.mult, ALU.add).then_inc(sm.small, 1)
                dve.wait_ge(sm.small, upto(4 * g + 3))
                x = m.X[:, cols(g, GROUP), :]
                dve.tensor_tensor(x, x, m.res[:, :, :], ALU.add).then_inc(sm.small, 1)
                dve.wait_ge(sm.small, upto(4 * g + 4))
                for j in range(GROUP):
                    stats_of(dve, m, g * GROUP + j)

        @block.scalar
        def _(act):
            with act.Fori(0, GROUPS) as g:
                for j in range(GROUP):
                    n = g * GROUP + j
                    z = j % 2
                    act.wait_ge(sm.shifted, upto(n + 1))
                    act.wait_ge(sm.p_turned, upto(g * GROUP + max(j - 1, 0)))
                    act.activation(m.expd[z][:, :, :], m.soft[z][:, :, :], ACT.Exp, scale=DH1 ** -0.5).then_inc(sm.exped, 1)
                    act.wait_ge(sm.p_turned, upto(n + 1))
                    if j == 0:
                        act.wait_ge(sm.pv_done, upto(g))
                    act.copy(m.p_t[:, j, :], turned).then_inc(sm.pt_out, 1)
                    act.wait_ge(sm.av_done, upto(n + 1))
                    if j == 0:
                        act.wait_ge(sm.summed, upto(g))
                    for c in range(2):
                        half = slice(c * S, (c + 1) * S)
                        src = m.ps6[half, 0:288].rearrange("t (n c q) -> t n c q", c=2, n=8)[:, :, c, :]
                        act.copy(m.av[half, j, :].rearrange("t (n q) -> t n q", n=8), src).then_inc(sm.av_out, 1)
                act.wait_ge(sm.pv_done, upto(g + 1))
                act.wait_ge(sm.pv_saved, upto(16 * g))
                act.copy(m.pv[:, :], rel_v).then_inc(sm.pv_out, 1)
                act.wait_ge(sm.att_turned, upto(g + 1))
                act.copy(m.att_t[:, :], m.ps7[:, :]).then_inc(sm.att_out, 1)

        @block.tensor
        def _(pe):
            def scores_of(g, j):
                n = g * GROUP + j
                z = j % 2
                pe.wait_ge(sm.spread, upto(2 * n + 2))
                pe.wait_ge(sm.added, upto(n))
                for half in range(2):
                    out = scores[:, 512 * half:512 * (half + 1)]
                    pe.matmul(out, m.ident_bf[:, :], m.mask_add[z][:, :].unsqueeze(1).to_broadcast([P, 8, S]),
                              start=True, stop=False, skip_group_check=True)
                    for st in range(2):
                        for c in range(2):
                            ins = pe.matmul(scores[c * S:(c + 1) * S, 512 * half + 256 * st:512 * half + 256 * (st + 1)],
                                            m.q_strip[z][:, 2 * half + st, c * S:(c + 1) * S],
                                            m.k_inner[z][:, :, c * S:(c + 1) * S], start=False, stop=True,
                                            skip_group_check=True)
                ins.then_inc(sm.scored, 1)

            def values_of(g, j):
                n = g * GROUP + j
                pe.wait_ge(sm.ct_staged, upto(2 * n + 2))
                pe.wait_ge(sm.v_out, upto(4 * n))
                pe.wait_ge(sm.small, upto(4 * g))
                for c in range(2):
                    ins = pe.matmul(m.ps7[:, c * P:(c + 1) * P], m.ct_twice[:, c, :, :].rearrange("p a s -> p (a s)"),
                                    m.proj_t[:, 2, :], start=True, stop=True)
                ins.then_inc(sm.v_done, 1)

            def turn_and_sum(g, j):
                n = g * GROUP + j
                z = j % 2
                pe.wait_ge(sm.exped, upto(n + 1))
                pe.wait_ge(sm.pt_out, upto(n))
                for pair in range(8):
                    ins = pe.transpose(turned[:, P * pair:P * (pair + 1)],
                                       m.expd[z][:, 2 * pair:2 * pair + 2, :].rearrange("p h s -> p (h s)"), m.ident[:, :])
                ins.then_inc(sm.p_turned, 1)
                pe.wait_ge(sm.pt_out, upto(n + 1))
                pe.wait_ge(sm.v_out, upto(4 * n + 4))
                pe.wait_ge(sm.av_out, upto(2 * n))
                for pair in range(8):
                    ins = pe.matmul(m.ps6[:, 36 * pair:36 * (pair + 1)], m.p_t[:, j, P * pair:P * (pair + 1)],
                                    m.v_block[:, pair, :, :, :].rearrange("p c q w -> p (c q w)"), start=True, stop=True)
                ins.then_inc(sm.av_done, 1)

            with pe.Fori(0, GROUPS) as g:
                for j in range(GROUP):
                    values_of(g, j)
                    scores_of(g, j)
                    turn_and_sum(g, j)
                pe.wait_ge(sm.pv_out, upto(g))
                p = m.p_t[:, :, :].rearrange("p i (n t) -> p (i n) t", t=S)
                for t in range(S):
                    ins = pe.matmul(rel_v[:, 16 * t:16 * (t + 1)], p[:, :, t], m.pos_v[:, t, :], start=True, stop=True)
                ins.then_inc(sm.pv_done, 1)
                pe.wait_ge(sm.att_done, upto(g + 1))
                for j in range(GROUP):
                    ins = pe.transpose(m.ps7[:, P * j:P * (j + 1)], m.att[:, j, :], m.ident[:, :])
                ins.then_inc(sm.att_turned, 1)
                pe.wait_ge(sm.att_out, upto(g + 1))
                for j in range(GROUP):
                    ins = pe.matmul(m.ps7[:, P * j:P * (j + 1)], m.att_t[:, P * j:P * (j + 1)], m.proj_t[:, 3, :], start=True, stop=True)
                ins.then_inc(sm.wo_done, 1)


def expert_weights(nc, m):
    with nc.Block() as block:

        @block.vector
        def _(dve):
            dve.wait_ge(m.moe_loaded, 48)
            for raw, high, low in ((m.W1_sb, m.W1_h, m.W1_l), (m.W2_sb, m.W2_h, m.W2_l)):
                dve.tensor_copy(high, raw).then_inc(m.mo_split, 1)
            for k, (raw, high, low) in enumerate(((m.W1_sb, m.W1_h, m.W1_l), (m.W2_sb, m.W2_h, m.W2_l))):
                dve.wait_ge(m.mo_split, k + 1)
                dve.tensor_tensor(low, raw, high.bitcast(F32), ALU.subtract)
            dve.wait_ge(m.b1_turned, 1)
            dve.tensor_copy(m.b1_cols[:, :], m.ps[0][:, 0:4 * EXPERTS])

        @block.tensor
        def _(pe):
            pe.wait_ge(m.moe_small_loaded, 64)
            pe.transpose(m.ps[0][:, 0:4 * EXPERTS], m.b1_raw[:, :], m.ident[0:4 * EXPERTS, 0:4 * EXPERTS]).then_inc(m.b1_turned, 1)


def router(nc, m):
    sm = m.ro
    wide = [P, TILES, EXPERTS]
    with nc.Block() as block:

        @block.vector
        def _(dve):
            dve.wait_ge(m.moe_small_loaded, 64)
            with dve.Fori(0, GROUPS // 2) as g2:
                for z in range(2):
                    g = g2 * 2 + z
                    dve.wait_ge(sm.turned[z], upto(g2))
                    for j in range(GROUP):
                        ins = normalize(dve, m, m.stage_x[z][:, j, :], g * GROUP + j)
                    ins.then_inc(sm.normed[z], 1)
                for z in range(2):
                    g = g2 * 2 + z
                    dve.wait_ge(sm.logits[z], upto(g2 + 1))
                    dve.tensor_tensor(m.logit[:, cols(g, GROUP), :], m.ps[2 + z][:, 0:32].rearrange("p (j e) -> p j e", e=EXPERTS),
                                      m.br_rows[:, :].unsqueeze(1).to_broadcast([P, GROUP, EXPERTS]), ALU.add).then_inc(sm.taken[z], 1)

        @block.tensor
        def _(pe):
            with pe.Fori(0, GROUPS // 2) as g2:
                for z in range(2):
                    pe.wait_ge(sm.normed[z], upto(g2 + 1))
                    pe.wait_ge(sm.xt_out[z], upto(g2))
                    for j in range(GROUP):
                        ins = pe.transpose(m.ps[z][:, P * j:P * (j + 1)], m.stage_x[z][:, j, :], m.ident[:, :])
                    ins.then_inc(sm.turned[z], 1)
                for z in range(2):
                    pe.wait_ge(sm.xt_out[z], upto(g2 + 1))
                    pe.wait_ge(sm.taken[z], upto(g2))
                    for j in range(GROUP):
                        ins = pe.matmul(m.ps[2 + z][:, EXPERTS * j:EXPERTS * (j + 1)], m.stage_xt[z][:, P * j:P * (j + 1)],
                                        m.Wr_sb[:, :], start=True, stop=True)
                    ins.then_inc(sm.logits[z], 1)

        @block.scalar
        def _(act):
            with act.Fori(0, GROUPS // 2) as g2:
                for z in range(2):
                    act.wait_ge(sm.turned[z], upto(g2 + 1))
                    act.wait_ge(sm.logits[z], upto(g2))
                    act.copy(m.stage_xt[z][:, :], m.ps[z][:, :]).then_inc(sm.xt_out[z], 1)
                    act.wait_ge(sm.xt_out[z], upto(g2 + 1))
                    act.copy(m.XR[:, cols(g2 * 2 + z, 512)], m.stage_xt[z][:, :])

    with nc.Block() as block:

        @block.vector
        def _(dve):
            step = Chain(dve, m.rt.dve)
            for i in range(TILES):
                ins = dve.max(m.best[:, i, :], m.logit[:, i, :])
            step.link(ins)
            step.link(dve.tensor_tensor(m.chosen[:, :, :], m.logit[:, :, :], m.best[:, :, 1:2].to_broadcast(wide), ALU.is_ge))
            step.link(dve.tensor_tensor(m.logit[:, :, :], m.logit[:, :, :], m.best[:, :, 0:1].to_broadcast(wide), ALU.subtract))
            dve.sem_inc(m.rt.shifted, 1)
            dve.wait_ge(m.rt.exp, 1)
            step.link(dve.tensor_tensor(m.weight[:, :, :], m.weight[:, :, :], m.chosen[:, :, :], ALU.mult))
            step.link(dve.tensor_reduce(m.wsum[:, :], m.weight[:, :, :], AX, ALU.add))
            step.link(dve.reciprocal(m.wsum[:, :], m.wsum[:, :]))
            step.link(dve.tensor_scalar(m.wsum[:, :], m.wsum[:, :], m.tanh_g[:, 3:4], None, ALU.mult))
            dve.tensor_tensor(m.weight[:, :, :], m.weight[:, :, :], m.wsum[:, :].unsqueeze(2).to_broadcast(wide), ALU.mult)

        @block.scalar
        def _(act):
            act.wait_ge(m.rt.shifted, 1)
            act.activation(m.weight[:, :, :], m.logit[:, :, :], ACT.Exp).then_inc(m.rt.exp, 1)


def experts(nc, m):
    sm = m.mo
    UP = (2, 3, 6, 7)
    with nc.Block() as block:

        @block.gpsimd
        def _(pool):
            with pool.Fori(0, GROUPS) as g:
                pool.wait_ge(sm.w_turned, upto(g))
                pool.tensor_copy(m.w_stage[:, :, :], m.weight[:, cols(g, GROUP), :]).then_inc(sm.w_staged, 1)
                pool.wait_ge(sm.x_high, upto(g + 1))
                pool.tensor_tensor(m.xt_l[:, :], m.XR[:, cols(g, 512)], m.xt_h[:, :].bitcast(F32), ALU.subtract).then_inc(sm.x_low, 1)

        @block.vector
        def _(dve):
            def split(g, e):
                z = e % 2
                for c in range(4):
                    if c % 2:
                        dve.wait_ge(sm.gelu, upto(32 * g + 4 * e + c + 1))
                        dve.wait_ge(sm.down_done, upto(8 * g + max(e - 1, 0)))
                        dve.tensor_copy(m.h_h[z][:, c, :], m.h[c][:, :]).then_inc(sm.h_high, 1)
                for c in (0, 2, 1, 3):
                    if c % 2:
                        dve.wait_ge(sm.h_high, upto(16 * g + 2 * e + (c + 1) // 2))
                    else:
                        dve.wait_ge(sm.h_high2, upto(16 * g + 2 * e + c // 2 + 1))
                    dve.tensor_tensor(m.h_l[z][:, c, :], m.h[c][:, :], m.h_h[z][:, c, :].bitcast(F32), ALU.subtract).then_inc(sm.h_split, 1)

            def combine(g, e):
                dve.wait_ge(sm.down_done, upto(8 * g + e + 1))
                for j in range(GROUP):
                    if e == 0:
                        dve.wait_ge(sm.acc, upto(g + 1))
                    else:
                        dve.wait_ge(sm.combined, upto(32 * g + 4 * (e - 1) + j + 1))
                    dve.scalar_tensor_tensor(m.acc[:, j, :], m.ps[4 + e % 2][:, P * j:P * (j + 1)], m.weight[:, g * GROUP + j, e:e + 1],
                                             m.acc[:, j, :], ALU.mult, ALU.add).then_inc(sm.combined, 1)

            with dve.Fori(0, GROUPS) as g:
                for e in range(EXPERTS):
                    split(g, e)
                    if e == 0:
                        dve.wait_ge(sm.bias_done, upto(g + 1))
                        dve.wait_ge(sm.saved, upto(16 * g))
                        dve.tensor_tensor(m.acc[:, :, :], m.ps[1].rearrange("p (j f) -> p j f", f=E), m.X[:, cols(g, GROUP), :],
                                          ALU.add).then_inc(sm.acc, 1)
                    else:
                        combine(g, e - 1)
                combine(g, EXPERTS - 1)

        @block.scalar
        def _(act):
            with act.Fori(0, GROUPS) as g:
                act.wait_ge(sm.up_done, upto(32 * g))
                act.copy(m.xt_h[:, :], m.XR[:, cols(g, 512)]).then_inc(sm.x_high, 1)
                for e in range(EXPERTS):
                    for c in range(4):
                        n = 32 * g + 4 * e + c
                        act.wait_ge(sm.up_done, upto(n + 1))
                        act.wait_ge(sm.h_split, upto(32 * g + 4 * max(e, 0)))
                        act.activation(m.h[c][:, :], m.ps[UP[c]], ACT.Gelu, bias=m.b1_cols[:, 4 * e + c:4 * e + c + 1]).then_inc(sm.gelu, 1)
                        if c % 2 == 0:
                            act.wait_ge(sm.gelu, upto(n + 1))
                            act.wait_ge(sm.down_done, upto(8 * g + max(e - 1, 0)))
                            act.copy(m.h_h[e % 2][:, c, :], m.h[c][:, :]).then_inc(sm.h_high2, 1)
                    if e == 0:
                        act.wait_ge(sm.w_turned, upto(g + 1))
                        act.copy(m.weight_t[:, :], m.ps[0][0:EXPERTS, :]).then_inc(sm.w_out, 1)

        @block.tensor
        def _(pe):
            def up(g, e):
                for c in range(4):
                    pe.wait_ge(sm.gelu, upto(32 * g + 4 * max(e - 1, 0) + c + (1 if e else 0)) if e else upto(32 * g))
                    out, cs = m.ps[UP[c]], slice(c * P, (c + 1) * P)
                    pe.matmul(out, m.W1_h[:, e, cs], m.xt_h[:, :], start=True, stop=False)
                    pe.matmul(out, m.W1_l[:, e, cs], m.xt_h[:, :], start=False, stop=False)
                    if e == 0 and c == 0:
                        pe.wait_ge(sm.x_low, upto(g + 1))
                    pe.matmul(out, m.W1_h[:, e, cs], m.xt_l[:, :], start=False, stop=True).then_inc(sm.up_done, 1)

            def down(g, e):
                bank, z = m.ps[4 + e % 2], e % 2
                pe.wait_ge(sm.h_split, upto(32 * g + 4 * e + 4))
                pe.wait_ge(sm.combined, upto(32 * g + 4 * max(e - 1, 0)))
                for j in range(GROUP):
                    out, tok = bank[:, P * j:P * (j + 1)], slice(P * j, P * (j + 1))
                    for c in range(4):
                        pe.matmul(out, m.h_h[z][:, c, tok], m.W2_h[:, e, c, :], start=(c == 0), stop=False)
                        pe.matmul(out, m.h_h[z][:, c, tok], m.W2_l[:, e, c, :], start=False, stop=False)
                        ins = pe.matmul(out, m.h_l[z][:, c, tok], m.W2_h[:, e, c, :], start=False, stop=(c == 3))
                ins.then_inc(sm.down_done, 1)

            with pe.Fori(0, GROUPS) as g:
                pe.wait_ge(sm.x_high, upto(g + 1))
                up(g, 0)
                pe.wait_ge(sm.w_staged, upto(g + 1))
                pe.wait_ge(sm.w_out, upto(g))
                for j in range(GROUP):
                    ins = pe.transpose(m.ps[0][0:EXPERTS, P * j:P * (j + 1)], m.w_stage[:, j, :], m.ident[:, :])
                ins.then_inc(sm.w_turned, 1)
                up(g, 1)
                pe.wait_ge(sm.w_out, upto(g + 1))
                pe.wait_ge(sm.acc, upto(g))
                for j in range(GROUP):
                    ins = pe.matmul(m.ps[1][:, P * j:P * (j + 1)], m.weight_t[:, P * j:P * (j + 1)], m.b2_sb[:, :], start=True, stop=True)
                ins.then_inc(sm.bias_done, 1)
                down(g, 0)
                for e in range(1, EXPERTS):
                    if e + 1 < EXPERTS:
                        up(g, e + 1)
                    down(g, e)

        @block.sync
        def _(sp):
            with sp.Fori(0, GROUPS) as g:
                sp.wait_ge(sm.combined, upto(32 * g + 32))
                hold(sp, m)
                sp.dma_start(m.out_tiles[:, cols(g, GROUP), :], m.acc[:, :, :]).then_inc(sm.saved, 16)
            sp.wait_ge(sm.saved, upto(16 * GROUPS))


def build(nc, ins, out):
    m = Names(dict(ins))
    m.credited, m.reused = [], []
    with ExitStack() as ctx:
        m.scope = ctx

        def sb(name, shape, dt=F32):
            return ctx.enter_context(nc.sbuf_tensor(name, shape, dt))

        def sems(name, *names, **lists):
            table = {}
            for n in names:
                table[n] = m.scope.enter_context(nc.semaphore(f"{name}_{n}"))
            for n, k in lists.items():
                table[n] = [m.scope.enter_context(nc.semaphore(f"{name}_{n}{i}")) for i in range(k)]
            for s in table.values():
                m.reused.extend(s if isinstance(s, list) else [s])
            return Names(table)

        def counted(name, *names, **lists):
            ns = sems(name, *names, **lists)
            for s in ns.table.values():
                m.credited.extend(s if isinstance(s, list) else [s])
            return ns

        m.table.update(sems("io", "x_loaded", "ctx_loaded", "gates_loaded", "scales_loaded", "tanh_ready",
                               "const_step", "stored", "ffn0_loaded", "clips_loaded",
                               "proj_loaded", "proj_bias_loaded", "pos_loaded", "moe_loaded", "moe_small_loaded",
                               "mo_split", "b1_turned", "held").table)
        m.stat_sems = [sems(f"stats{k}", "dve", "variance") for k in range(4)]
        m.wide = [ctx.enter_context(nc.psum_tensor(f"banks{k}", [P, 1024], F32)) for k in range(3)]
        m.ps6, m.ps7 = (ctx.enter_context(nc.psum_tensor(f"bank{k}", [P, 512], F32)) for k in (6, 7))
        m.ps = [m.wide[k // 2][:, 512 * (k % 2):512 * (k % 2 + 1)] for k in range(6)] + [m.ps6[:, :], m.ps7[:, :]]

        m.X = sb("X", [P, TILES, E])
        m.C = sb("C", [P, TILES, E])
        m.CT = sb("CT", [P, TILES * P])
        m.XT = sb("XT", [P, TILES * P])
        m.ident = sb("ident", [P, P])
        m.ident_bf = sb("ident_bf", [P, P], BF16)
        m.ones = sb("ones", [P, P])
        m.minus_half = sb("minus_half", [P, TILES])
        m.tanh_g = sb("tanh_g", [P, 4])
        m.row_stats = sb("row_stats", [P, TILES, 6])
        m.row_mean = sb("row_mean", [P, TILES])
        m.row_rstd = sb("row_rstd", [P, TILES])
        m.row_tmp = sb("row_tmp", [P, TILES])
        m.head_mask = sb("head_mask", [P, NH0])
        m.cumsum_mat = sb("cumsum_mat", [P, P])

        m.causal_add = sb("causal_add", [P, S])

        m.magic = sb("magic", [P, 1])
        m.clips = sb("clips", [1, 2])
        m.gu_raw_t = sb("gu_raw", [P, 6, E])
        m.proj_raw = sb("proj_raw", [P, 4, E])
        m.proj_bias = sb("proj_bias", [P, 2])
        m.bv_rows, m.bo_rows = sb("bv_rows", [P, E]), sb("bo_rows", [P, E])
        m.pos_k_raw = sb("pos_k_raw", [S, S, DH1])
        m.pos_v = sb("pos_v", [P, S, 2 * DH1])
        m.v_block = sb("v_block", [P, NH1 // 2, 2, 2, DH1 + 1])
        m.strip_mask, m.inner_mask = sb("strip_mask", [P, 4]), sb("inner_mask", [P, 4])
        m.Wr_sb, m.br_rows = sb("Wr_sb", [P, EXPERTS]), sb("br_rows", [P, EXPERTS])
        m.b2_sb, m.b1_cols = sb("b2_sb", [EXPERTS, E]), sb("b1_cols", [P, 4 * EXPERTS])
        m.b1_raw = sb("b1_raw", [4 * EXPERTS, P])
        m.out_tiles = out.rearrange("(i c) s f -> (c s) i f", c=2)
        m.dn_raw_t = sb("dn_raw", [P, 1, 352])
        m.gu_raw, m.dn_raw = m.gu_raw_t[:, :, :], m.dn_raw_t[:, :, :]

        with ExitStack() as l0:
            m.scope = l0
            m.gs = counted("gates", "ctx_turned", "ctx_staged", "xt_out", "ct_out", "stored", "x_turned", "normed",
                           "gates_done", "gates_out")
            m.gw = sems("gates_w", "turned", "ready")
            m.gm = sems("gmath", "act", "dve", "dve2", "log1p", "neg", "logf", "summed", "g", "g_turned", "gmax",
                        "gmax_turned", "saved")
            m.rows = sems("att0_g", rows=2).rows
            m.at = counted("att0", diff=2, qk=2, spread=2, av=2, v=2, causal=2, c=2, exp=2, k=2, out=2)
            m.af = sems("fin0", "dve", "centered", "squared", "var", "rstd")
            start_counts(nc, m)
            def sl(name, shape, dt=F32):
                return l0.enter_context(nc.sbuf_tensor(name, shape, dt))
            m.gate_rows = sl("gate_rows", [16, 3 * E])
            m.gate_bias = sl("gate_bias", [P, 16])
            m.gate_w = sl("gate_w", [P, 3, 16])
            m.out_w_rows = sl("out_w_rows", [P, E])
            m.stage_x = sl("stage_x", [P, GROUP, E])
            m.stage_c = sl("stage_c", [P, GROUP, E])
            m.stage_xt = sl("stage_xt", [P, 512])
            m.stage_ct = sl("stage_ct", [P, 512])
            m.gates = sl("gates", [P, TILES, 16])
            m.softp = sl("softp", [P, TILES, NH0])
            m.logf = sl("logf", [P, TILES, NH0])
            m.exp_neg_max = sl("exp_neg_max", [P, TILES, NH0])
            m.g_nat = sl("g_nat", [P, TILES, NH0])
            m.cumsum = sl("cumsum", [P, TILES * NH0])
            m.g_t = sl("g_t", [P, 2, P])
            m.gmax_t = sl("gmax_t", [P, 2, P])
            m.g_rows = [sl(f"g_rows{j}", [P, NH0 * S]) for j in range(2)]
            m.decay = [sl(f"decay{j}", [P, NH0, S]) for j in range(2)]
            m.c_t = [sl(f"c_t{j}", [P, NH0, S]) for j in range(2)]
            m.q_spread = [sl(f"q_spread{j}", [P, NH0, P]) for j in range(2)]
            m.k_stage = [sl(f"k_stage{j}", [P, P]) for j in range(2)]
            m.v_ones = [sl(f"v_ones{j}", [P, NH0, DH0 + 1]) for j in range(2)]
            m.num = sl("num", [P, TILES, NH0 * (DH0 + 1)])
            m.den = sl("den", [P, TILES * NH0])
            m.hmean = sl("hmean", [P, TILES * NH0])
            m.hvar = sl("hvar", [P, TILES * NH0])
            m.hid = sl("hid", [P, TILES * NH0, DH0])
            m.hsq = sl("hsq", [P, TILES * NH0, DH0])
            m.gmax_dram = nc.dram_tensor("gmax_dram", (2, TILES, NH0, S), F32, kind="Internal").ap()
            load_and_constants(nc, m)
            l0_gates(nc, m)
            l0_gate_math(nc, m)
            l0_attention(nc, m)
            l0_attention_finish(nc, m)

        with ExitStack() as f0:
            m.scope = f0
            m.fw = sems("ffn0_w", "dve", "quantized", "turned")
            m.fn = counted("ffn0_norm", "normed")
            scale_sems = [sems(f"scale{k}", "exp", "dve", "col", "row", "pair", "spread") for k in range(2)]
            m.fu = counted("ffn0_up", "scaled", "shifted", "clipped", "turned", "quantized", "upped", "stood", "silu", "hidden")
            m.fd = counted("ffn0_down", "shifted", "clipped", "downed", "quantized", "out", "added")
            m.fd.dve = sems("ffn0_down", "dve").dve
            start_counts(nc, m)
            def sl(name, shape, dt=F32):
                return f0.enter_context(nc.sbuf_tensor(name, shape, dt))
            m.XN = m.XT[:, :].rearrange("p (i f) -> p i f", f=E)
            gu_q, dn_q = sl("gu_q", [P, 6, E], BF16), sl("dn_q", [P, 1, 352], BF16)
            m.gu_q, m.dn_q = gu_q[:, :, :], dn_q[:, :, :]
            m.gu_top, m.gu_scale = sl("gu_top", [P, 6]), sl("gu_scale", [P, 6])
            m.dn_top, m.dn_scale = sl("dn_top", [P, 1]), sl("dn_scale", [P, 1])
            m.dn_diag = sl("dn_diag", [P, P])
            m.dn_row = sl("dn_row", [P, E])
            m.gu_t = sl("gu_t", [P, 6, P], BF16)
            m.dn_t = sl("dn_t", [P, 3, E], BF16)
            m.x_top = sl("x_top", [P, GROUPS])
            m.h_top = sl("h_top", [P, 3, GROUPS])
            m.clip_exp = sl("clip_exp", [1, 1])
            m.top_col = sl("top_col", [P, 1])
            m.top_one = sl("top_one", [1, 2])
            m.top_pair = sl("top_pair", [1, 2])
            m.x_scale, m.h_scale = sl("x_scale", [P, 2]), sl("h_scale", [P, 2])
            m.round_x, m.xq, m.xq_t = sl("round_x", [P, 512]), sl("xq", [P, 512], BF16), sl("xq_t", [P, 512], BF16)
            m.silu = [sl(f"silu{k}", [P, 512]) for k in range(3)]
            m.HT = sl("HT", [P, 3, TILES * P])
            m.round_h, m.hq = sl("round_h", [P, 3, 512]), sl("hq", [P, 3, 512], BF16)
            m.down = sl("down", [P, GROUP, E])
            finish_stats(nc, m, m.stat_sems[1])
            l0_ffn_weights(nc, m)
            l0_ffn_norm(nc, m)
            activation_scale(nc, m, scale_sems[0], m.x_top[:, :], m.clips[0:1, 0:1], m.x_scale)
            l0_ffn_up(nc, m)
            activation_scale(nc, m, scale_sems[1], m.h_top[:, :, :].rearrange("p k g -> p (k g)"), m.clips[0:1, 1:2], m.h_scale)
            l0_ffn_down(nc, m)

        with ExitStack() as l1:
            m.scope = l1
            m.lw = sems("l1_w", "turned", "stood", "moved")
            m.pj = counted("l1_proj", "turned", "normed", "xt_out", "q_out", "k_out", "q_done", "k_done", "q_back", "q_saved",
                           "rel_out", "rel_done", rel_saved=2)
            m.a1 = counted("l1_att", "added", "masked", "pv_out", "pv_saved", "pv_back", "summed", "v_done", "ct_staged",
                           "scored", "spread", "av_done", "v_out", "exped", "maxed", "shifted", "av_out", "small",
                           "att_turned", "att_done", "wo_done", "p_turned", "pv_done", "pt_out", "att_out")
            m.rel_sem = sems("l1_rel", slot=4).slot
            m.mask_sem = sems("l1_mask", slot=4).slot
            start_counts(nc, m)
            def sl(name, shape, dt=F32):
                return l1.enter_context(nc.sbuf_tensor(name, shape, dt))
            m.proj_t = sl("proj_t", [P, 4, E])
            m.stage_x, m.stage_xt = sl("stage_x1", [P, GROUP, E]), sl("stage_xt1", [P, 512])
            m.KT, m.QT = sl("KT", [P, TILES * P]), m.XT
            m.q_dram = nc.dram_tensor("q_dram", (P, TILES * P), F32, kind="Internal").ap()
            m.rel_dram = nc.dram_tensor("rel_dram", (GROUPS, NH1, 8, S, S), F32, kind="Internal").ap()
            m.pv_dram = nc.dram_tensor("pv_dram", (GROUPS, S, S, 2 * DH1), F32, kind="Internal").ap()
            finish_stats(nc, m, m.stat_sems[2])
            with ExitStack() as part:
                def sl(name, shape, dt=F32):
                    return part.enter_context(nc.sbuf_tensor(name, shape, dt))
                m.pos_k_td = sl("pos_k_td", [P, 4, S])
                m.pos_k8 = sl("pos_k8", [DH1, S, S])
                m.q8 = sl("q8", [DH1, NH1, 512])
                m.rel = [sl(f"rel{k}", [P, 2048]) for k in range(2)]
                l1_weights(nc, m)
                l1_project(nc, m)
            with ExitStack() as part:
                def sl(name, shape, dt=F32):
                    return part.enter_context(nc.sbuf_tensor(name, shape, dt))
                m.rel_in = [sl(f"rel_in{k}", [P, NH1, S]) for k in range(2)]
                m.mask_in = [sl(f"mask_in{k}", [P, S], I32) for k in range(2)]
                m.mask_add = [sl(f"mask_add{k}", [P, S], BF16) for k in range(2)]
                m.ct_twice = sl("ct_twice", [P, 2, 2, S])
                m.q_strip = [sl(f"q_strip{k}", [P, 4, P]) for k in range(2)]
                m.k_inner = [sl(f"k_inner{k}", [P, 4, P]) for k in range(2)]
                m.soft = [sl(f"soft{k}", [P, NH1, S]) for k in range(2)]
                m.expd = [sl(f"expd{k}", [P, NH1, S]) for k in range(2)]
                m.row_max = sl("row_max", [P, NH1])
                m.p_t = sl("p_t", [P, GROUP, 1024])
                m.av = sl("av", [P, GROUP, NH1 * (DH1 + 1)])
                m.pv, m.pv_in = sl("pv", [S, 1024]), sl("pv_in", [P, 32, 2 * DH1])
                m.row_sum = sl("row_sum", [P, GROUP * NH1])
                m.att, m.att_t, m.res = sl("att", [P, GROUP, E]), sl("att_t", [P, 512]), sl("res", [P, GROUP, E])
                l1_attention(nc, m)

        with ExitStack() as f1:
            m.scope = f1
            m.ro = counted("route", turned=2, normed=2, xt_out=2, logits=2, taken=2)
            m.rt = sems("route1", "dve", "shifted", "exp")
            m.mo = counted("moe", "up_done", "w_staged", "x_high", "x_low", "w_turned", "w_out", "bias_done", "saved", "acc",
                           "gelu", "down_done", "h_high", "h_high2", "h_split", "combined")
            start_counts(nc, m)
            def sl(name, shape, dt=F32):
                return f1.enter_context(nc.sbuf_tensor(name, shape, dt))
            m.W1_sb = m.CT[:, :].rearrange("p (e h) -> p e h", e=EXPERTS)
            m.W2_sb = m.XT[:, :].rearrange("p (e c d) -> p e c d", e=EXPERTS, c=4)
            m.W1_h, m.W1_l = (sl(f"W1_{k}", [P, EXPERTS, HID], F32R)[:, :, :] for k in "hl")
            m.W2_h, m.W2_l = (sl(f"W2_{k}", [P, EXPERTS, 4, E], F32R)[:, :, :, :] for k in "hl")
            m.XR = m.C[:, :, :].rearrange("p i f -> p (i f)")
            m.stage_x = [sl(f"stage_x2{k}", [P, GROUP, E]) for k in range(2)]
            m.stage_xt = [sl(f"stage_xt2{k}", [P, 512]) for k in range(2)]
            m.xt_h, m.xt_l = sl("xt_h", [P, 512], F32R), sl("xt_l", [P, 512], F32R)
            m.h = [sl(f"h{k}", [P, 512]) for k in range(4)]
            m.h_h = [sl(f"h_h{k}", [P, 4, 512], F32R) for k in range(2)]
            m.h_l = [sl(f"h_l{k}", [P, 4, 512], F32R) for k in range(2)]
            m.logit, m.best, m.chosen, m.weight = (sl(k, [P, TILES, EXPERTS]) for k in ("logit", "best", "chosen", "weight"))
            m.wsum, m.weight_t, m.w_stage = sl("wsum", [P, TILES]), sl("weight_t", [EXPERTS, 512]), sl("w_stage", [P, GROUP, EXPERTS])
            m.acc = sl("acc", [P, GROUP, E])
            with nc.Block() as block:

                @block.sync
                def _(sp):
                    sp.dma_start(m.W1_sb, m.W1.rearrange("e d h -> d e h")).then_inc(m.moe_loaded, 16)
                    for e0 in (0, 4):
                        sp.dma_start(m.W2_sb[:, e0:e0 + 4], m.W2[e0:e0 + 4].rearrange("e (c p) d -> p e c d", p=P)).then_inc(m.moe_loaded, 16)
            finish_stats(nc, m, m.stat_sems[3])
            expert_weights(nc, m)
            router(nc, m)
            experts(nc, m)


_INS = {'x': 'x', 'ctx_1024': 'ctx', 'mask_BxSxS2_ik0': 'mask', 'g_xattn': 'g_xattn', 'g_ffn': 'g_ffn',
        'L0_xattn_igate_w': 'igate_w', 'L0_xattn_igate_b': 'igate_b', 'L0_xattn_fgate_w': 'fgate_w',
        'L0_xattn_fgate_b': 'fgate_b', 'L0_xattn_out_w': 'out_w', 'L0_ffn_clip_x': 'clip_x',
        'L0_ffn_clip_down': 'clip_down', 'L0_ffn_w_gate': 'w_gate', 'L0_ffn_w_up': 'w_up', 'L0_ffn_w_down': 'w_down',
        'L1_xattn_pos_k': 'pos_k', 'L1_xattn_pos_v': 'pos_v_in', 'L1_xattn_Wq': 'Wq', 'L1_xattn_bq': 'bq',
        'L1_xattn_Wk': 'Wk', 'L1_xattn_bk': 'bk', 'L1_xattn_Wv': 'Wv', 'L1_xattn_bv': 'bv', 'L1_xattn_Wo': 'Wo',
        'L1_xattn_bo': 'bo', 'L1_ffn_W1': 'W1', 'L1_ffn_b1': 'b1', 'L1_ffn_W2': 'W2', 'L1_ffn_b2': 'b2',
        'L1_ffn_Wr': 'Wr', 'L1_ffn_br': 'br'}


def kernel(**inputs):
    import numpy as _np
    import concourse.bacc as _bacc
    from concourse import mybir as _mybir
    from concourse.bass_utils import run_bass_kernel_spmd as _run

    nc = _bacc.Bacc("TRN2", target_bir_lowering=False, num_devices=1)
    arrays, args = {}, {}
    for name, short in _INS.items():
        a = _np.ascontiguousarray(inputs[name])
        arrays[f"in_{name}_dram"] = a
        args[short] = nc.dram_tensor(f"in_{name}_dram", a.shape, _mybir.dt.from_np(a.dtype), kind="ExternalInput").ap()
    out = nc.dram_tensor("out_0_dram", (B, S, E), _mybir.dt.float32, kind="ExternalOutput").ap()
    build(nc, args, out)
    r = _run(nc, [arrays], core_ids=[0])
    return r.results[0]["out_0_dram"]
```

```python
from contextlib import ExitStack

import concourse.bass as bass
from concourse import mybir

P = 128
B, S, E = 64, 64, 128
TILES = B * S // P
GROUP = 4
GROUPS = TILES // GROUP
NH0, DH0 = 8, 16
LN_EPS = 1e-5
NORM_EPS = 1e-6
QMAX = 127.0
MAGIC = 1.5 * 2 ** 23
NH1, DH1 = 16, 8
EXPERTS, HID = 8, 512
CHUNKS = (128, 128, 96)
FAR = -1e30

F32 = mybir.dt.float32
F32R = mybir.dt.float32r
BF16 = mybir.dt.bfloat16
I32 = mybir.dt.int32
ALU = mybir.AluOpType
ACT = mybir.ActivationFunctionType
AX = mybir.AxisListType.X


class Names:

    def __init__(self, table):
        self.table = table

    def __getattr__(self, name):
        return self.table[name]


def cols(i, n):
    return bass.ds(i * n, n)


def upto(n):
    return n + 1


class Chain:

    def __init__(self, eng, sem):
        self.eng, self.sem, self.n = eng, sem, 0

    def link(self, ins):
        self.n += 1
        ins.then_inc(self.sem, 1)
        self.eng.wait_ge(self.sem, self.n)


def hold(eng, m):
    eng.sem_inc(m.held, 1)


def start_counts(nc, m):
    reused, credited = m.reused, m.credited
    m.reused, m.credited = [], []
    with nc.Block() as block:

        @block.sync
        def _(sp):
            for sem in reused:
                sp.sem_clear(sem)
            for sem in credited:
                sp.sem_inc(sem, 1)


def load_and_constants(nc, m):
    with nc.Block() as block:

        @block.sync
        def _(sp):
            sp.dma_start(m.X[:, :, :], m.x.rearrange("(i c) s f -> (c s) i f", c=2)).then_inc(m.x_loaded, 16)
            sp.dma_start(m.C[:, :, :], m.ctx.rearrange("(i c) s f -> (c s) i f", c=2)).then_inc(m.ctx_loaded, 16)

        @block.scalar
        def _(act):
            act.dma_start(m.gate_rows[0:NH0, :], m.igate_w).then_inc(m.gates_loaded, 16)
            act.dma_start(m.gate_rows[NH0:2 * NH0, :], m.fgate_w).then_inc(m.gates_loaded, 16)
            act.dma_start(m.gate_bias[:, 0:NH0], m.igate_b.partition_broadcast(P)).then_inc(m.gates_loaded, 16)
            act.dma_start(m.gate_bias[:, NH0:2 * NH0], m.fgate_b.partition_broadcast(P)).then_inc(m.gates_loaded, 16)
            act.dma_start(m.out_w_rows[:, :], m.out_w.partition_broadcast(P)).then_inc(m.scales_loaded, 16)
            act.dma_start(m.tanh_g[:, 0:2], m.g_xattn.partition_broadcast(P)).then_inc(m.scales_loaded, 16)
            act.dma_start(m.tanh_g[:, 2:4], m.g_ffn.partition_broadcast(P)).then_inc(m.scales_loaded, 16)
            for k, w in enumerate((m.w_gate, m.w_up)):
                act.dma_start(m.gu_raw[:, 3 * k:3 * k + 2, :], w[0:2 * P].rearrange("(c p) f -> p c f", p=P)).then_inc(m.ffn0_loaded, 16)
                act.dma_start(m.gu_raw[0:96, 3 * k + 2, :], w[2 * P:]).then_inc(m.ffn0_loaded, 16)
            act.dma_start(m.dn_raw[:, 0, :], m.w_down).then_inc(m.ffn0_loaded, 16)
            act.dma_start(m.clips[:, 0:1], m.clip_x.unsqueeze(0)).then_inc(m.clips_loaded, 16)
            act.dma_start(m.clips[:, 1:2], m.clip_down.unsqueeze(0)).then_inc(m.clips_loaded, 16)
            for k, w in enumerate((m.Wq, m.Wk, m.Wv, m.Wo)):
                act.dma_start(m.proj_raw[:, k, :], w).then_inc(m.proj_loaded, 16)
            act.dma_start(m.proj_bias[:, 0:1], m.bq.unsqueeze(1)).then_inc(m.proj_bias_loaded, 16)
            act.dma_start(m.proj_bias[:, 1:2], m.bk.unsqueeze(1)).then_inc(m.proj_bias_loaded, 16)
            act.dma_start(m.bv_rows[:, :], m.bv.partition_broadcast(P)).then_inc(m.proj_bias_loaded, 16)
            act.dma_start(m.bo_rows[:, :], m.bo.partition_broadcast(P)).then_inc(m.proj_bias_loaded, 16)
            act.dma_start(m.pos_k_raw[:, :, :], m.pos_k.rearrange("t s d -> s t d")).then_inc(m.pos_loaded, 16)
            act.wait_ge(m.const_step, 4)
            for p in range(2):
                act.dma_start(m.pos_v[p * S:(p + 1) * S, :, p * DH1:(p + 1) * DH1], m.pos_v_in.rearrange("t s d -> s t d")).then_inc(m.pos_loaded, 16)
            act.dma_start(m.Wr_sb[:, :], m.Wr).then_inc(m.moe_small_loaded, 16)
            act.dma_start(m.br_rows[:, :], m.br.partition_broadcast(P)).then_inc(m.moe_small_loaded, 16)
            act.dma_start(m.b2_sb[:, :], m.b2).then_inc(m.moe_small_loaded, 16)
            act.dma_start(m.b1_raw[:, :], m.b1.rearrange("e (c p) -> (e c) p", p=P)).then_inc(m.moe_small_loaded, 16)
            act.wait_ge(m.scales_loaded, 48)
            act.activation(m.tanh_g[:, :], m.tanh_g[:, :], ACT.Tanh).then_inc(m.tanh_ready, 1)

        @block.gpsimd
        def _(pool):
            step = Chain(pool, m.const_step)
            step.link(pool.memset(m.pos_v[:, :, :], 0.0))
            step.link(pool.memset(m.v_block[:, :, :, :, :], 0.0))
            for p in range(2):
                step.link(pool.memset(m.v_block[p * S:(p + 1) * S, :, :, p, DH1:DH1 + 1], 1.0))
            step.link(pool.memset(m.ident[:, :], 0.0))
            step.link(pool.affine_select(out=m.ident[:, :], in_=m.ident[:, :], compare_op=ALU.not_equal, fill=1.0,
                                         base=0, pattern=[[-1, P]], channel_multiplier=1))
            step.link(pool.tensor_copy(m.ident_bf[:, :], m.ident[:, :]))
            step.link(pool.memset(m.ones[:, :], 1.0))
            step.link(pool.affine_select(out=m.cumsum_mat[:, :], in_=m.ones[:, :], compare_op=ALU.is_ge, fill=0.0,
                                         base=0, pattern=[[1, P]], channel_multiplier=-1))
            step.link(pool.memset(m.cumsum_mat[0:S, S:P], 0.0))
            step.link(pool.affine_select(out=m.head_mask[:, :], in_=m.ones[:, 0:NH0], compare_op=ALU.is_ge, fill=0.0,
                                         base=0, pattern=[[-DH0, NH0]], channel_multiplier=1))
            step.link(pool.affine_select(out=m.head_mask[:, :], in_=m.head_mask[:, :], compare_op=ALU.is_ge, fill=0.0,
                                         base=DH0 - 1, pattern=[[DH0, NH0]], channel_multiplier=-1))
            step.link(pool.memset(m.causal_add[:, :], 0.0))
            for c in range(2):
                half = m.causal_add[c * S:(c + 1) * S, :]
                step.link(pool.affine_select(out=half, in_=half, compare_op=ALU.is_ge, fill=FAR, base=0,
                                             pattern=[[1, S]], channel_multiplier=-1))
            for j in range(2):
                step.link(pool.memset(m.v_ones[j][:, :, DH0:DH0 + 1], 1.0))
            for k in (2, 5):
                step.link(pool.memset(m.gu_raw[96:P, k, :], 1.0))
            step.link(pool.memset(m.magic[:, :], MAGIC))
            step.link(pool.memset(m.minus_half[:, :], -0.5))


def stats_of(eng, m, tile):
    return eng.bn_stats(m.row_stats[:, tile, :], m.X[:, tile, :])


def finish_stats(nc, m, sm):
    stats = m.row_stats
    with nc.Block() as block:

        @block.vector
        def _(dve):
            step = Chain(dve, sm.dve)
            step.link(dve.tensor_tensor(m.row_mean[:, :], stats[:, :, 1], stats[:, :, 4], ALU.add))
            step.link(dve.tensor_scalar(m.row_mean[:, :], m.row_mean[:, :], 0.5, None, ALU.mult))
            step.link(dve.tensor_tensor(m.row_tmp[:, :], stats[:, :, 1], stats[:, :, 4], ALU.subtract))
            step.link(dve.scalar_tensor_tensor(m.row_tmp[:, :], m.row_tmp[:, :], 0.25, m.row_tmp[:, :], ALU.mult, ALU.mult))
            step.link(dve.tensor_tensor(m.row_rstd[:, :], stats[:, :, 2], stats[:, :, 5], ALU.add))
            step.link(dve.scalar_tensor_tensor(m.row_tmp[:, :], m.row_rstd[:, :], 1.0 / E, m.row_tmp[:, :], ALU.mult, ALU.add))
            step.link(dve.tensor_scalar(m.row_tmp[:, :], m.row_tmp[:, :], LN_EPS, None, ALU.add))
            dve.sem_inc(sm.variance, 1)

        @block.gpsimd
        def _(pool):
            pool.wait_ge(sm.variance, 1)
            pool.tensor_tensor(m.row_rstd[:, :], m.row_tmp[:, :], m.minus_half[:, 0:TILES], ALU.pow)


def normalize(eng, m, out, tile):
    return eng.tensor_scalar(out, m.X[:, tile, :], m.row_mean[:, cols(tile, 1)], m.row_rstd[:, cols(tile, 1)],
                             ALU.subtract, ALU.mult)


def l0_gates(nc, m):
    sm = m.gs
    with nc.Block() as block:

        @block.vector
        def _(dve):
            dve.wait_ge(m.x_loaded, 16)
            with dve.Fori(0, GROUPS) as g:
                for j in range(GROUP):
                    stats_of(dve, m, g * GROUP + j)
    finish_stats(nc, m, m.stat_sems[0])

    with nc.Block() as block:

        @block.gpsimd
        def _(pool):
            pool.wait_ge(m.ctx_loaded, 16)
            with pool.Fori(0, GROUPS) as g:
                pool.wait_ge(sm.ctx_turned, upto(g))
                pool.tensor_copy(m.stage_c[:, :, :], m.C[:, cols(g, GROUP), :]).then_inc(sm.ctx_staged, 1)
                pool.wait_ge(sm.xt_out, upto(g + 1))
                pool.tensor_copy(m.XT[:, cols(g, 512)], m.stage_xt[:, :]).then_inc(sm.stored, 1)
                pool.wait_ge(sm.ct_out, upto(g + 1))
                pool.tensor_copy(m.CT[:, cols(g, 512)], m.stage_ct[:, :]).then_inc(sm.stored, 1)

        @block.vector
        def _(dve):
            dve.wait_ge(m.gates_loaded, 64)
            dve.wait_ge(m.gw.turned, 3)
            for k in range(3):
                dve.tensor_copy(m.gate_w[:, k, :], m.ps[0][:, 16 * k:16 * k + 16]).then_inc(m.gw.ready, 1)
            with dve.Fori(0, GROUPS) as g:
                dve.wait_ge(sm.x_turned, upto(g))
                for j in range(GROUP):
                    normalize(dve, m, m.stage_x[:, j, :], g * GROUP + j).then_inc(sm.normed, 1)
                dve.wait_ge(sm.gates_done, upto(g + 1))
                dve.tensor_tensor(m.gates[:, cols(g, GROUP), :],
                                  m.ps[4][:, 0:64].rearrange("p (j n) -> p j n", j=GROUP),
                                  m.gate_bias[:, :].unsqueeze(1).to_broadcast([P, GROUP, 16]),
                                  ALU.add).then_inc(sm.gates_out, 1)

        @block.tensor
        def _(pe):
            pe.wait_ge(m.gates_loaded, 64)
            for k in range(3):
                pe.transpose(m.ps[0][:, 16 * k:16 * k + 16], m.gate_rows[0:16, k * P:(k + 1) * P],
                             m.ident[0:16, 0:16]).then_inc(m.gw.turned, 1)
            pe.wait_ge(m.gw.ready, 3)
            with pe.Fori(0, GROUPS) as g:
                pe.wait_ge(sm.normed, upto(g * GROUP + GROUP))
                pe.wait_ge(sm.xt_out, upto(g))
                for j in range(GROUP):
                    ins = pe.transpose(m.ps[1][:, j * P:(j + 1) * P], m.stage_x[:, j, :], m.ident[:, :])
                ins.then_inc(sm.x_turned, 1)
                pe.wait_ge(sm.ctx_staged, upto(g + 1))
                pe.wait_ge(sm.ct_out, upto(g))
                for j in range(GROUP):
                    ins = pe.transpose(m.ps[2][:, j * P:(j + 1) * P], m.stage_c[:, j, :], m.ident[:, :])
                ins.then_inc(sm.ctx_turned, 1)
                pe.wait_ge(sm.xt_out, upto(g + 1))
                pe.wait_ge(sm.ct_out, upto(g + 1))
                pe.wait_ge(sm.gates_out, upto(g))
                for j in range(GROUP):
                    tok = slice(j * P, (j + 1) * P)
                    out = m.ps[4][:, 16 * j:16 * j + 16]
                    pe.matmul(out, m.stage_xt[:, tok], m.gate_w[:, 0, :], start=True, stop=False)
                    pe.matmul(out, m.stage_ct[:, tok], m.gate_w[:, 1, :], start=False, stop=False)
                    ins = pe.matmul(out, m.stage_ct[:, tok], m.gate_w[:, 2, :], start=False, stop=True)
                ins.then_inc(sm.gates_done, 1)

        @block.scalar
        def _(act):
            with act.Fori(0, GROUPS) as g:
                act.wait_ge(sm.x_turned, upto(g + 1))
                act.wait_ge(sm.gates_done, upto(g))
                act.wait_ge(sm.stored, upto(2 * g))
                act.copy(m.stage_xt[:, :], m.ps[1][:, :]).then_inc(sm.xt_out, 1)
                act.wait_ge(sm.ctx_turned, upto(g + 1))
                act.copy(m.stage_ct[:, :], m.ps[2][:, :]).then_inc(sm.ct_out, 1)


def l0_gate_math(nc, m):
    sm = m.gm
    ig, fg = m.gates[:, :, 0:NH0], m.gates[:, :, NH0:2 * NH0]
    flat = m.logf[:, :, :].rearrange("p i h -> p (i h)")
    with nc.Block() as block:

        @block.scalar
        def _(act):
            step = Chain(act, sm.act)
            step.link(act.activation(m.softp[:, :, :], fg, ACT.Abs))
            step.link(act.activation(m.softp[:, :, :], m.softp[:, :, :], ACT.Exp, scale=-1.0))
            act.activation(m.softp[:, :, :], m.softp[:, :, :], ACT.Ln, bias=1.0).then_inc(sm.log1p, 1)
            act.wait_ge(sm.neg, 1)
            act.activation(m.exp_neg_max[:, :, :], m.exp_neg_max[:, :, :], ACT.Exp, scale=-1.0)

        @block.vector
        def _(dve):
            step = Chain(dve, sm.dve)
            step.link(dve.tensor_scalar(m.logf[:, :, :], fg, 0.0, None, ALU.min))
            dve.wait_ge(sm.log1p, 1)
            dve.tensor_tensor(m.logf[:, :, :], m.logf[:, :, :], m.softp[:, :, :], ALU.subtract).then_inc(sm.logf, 1)
            dve.wait_ge(sm.summed, 1)
            dve.tensor_copy(m.cumsum[:, :], m.ps[0][:, 0:256]).then_inc(sm.dve2, 1)
            dve.wait_ge(sm.dve2, 1)
            dve.tensor_tensor(m.g_nat[:, :, :], ig, m.cumsum[:, :].rearrange("p (i h) -> p i h", h=NH0),
                              ALU.subtract).then_inc(sm.g, 1)
            dve.wait_ge(sm.g_turned, 1)
            dve.tensor_copy(m.g_t[:, :, :], m.ps[1][:, 0:256].rearrange("p (u t) -> p u t", u=2)).then_inc(sm.dve2, 1)
            dve.wait_ge(sm.dve2, 2)
            for u in range(2):
                for c in range(2):
                    part = m.g_t[:, u, c * S:(c + 1) * S]
                    dve.tensor_tensor_scan(m.gmax_t[:, u, c * S:(c + 1) * S], part, part, -3e38,
                                           ALU.max, ALU.max).then_inc(sm.gmax, 1)
            dve.wait_ge(sm.gmax_turned, 1)
            dve.tensor_tensor(m.exp_neg_max[:, :, :].rearrange("p i h -> p (i h)"), m.ps[2][:, 0:256],
                              m.cumsum[:, :], ALU.add).then_inc(sm.neg, 1)

        @block.tensor
        def _(pe):
            pe.wait_ge(sm.logf, 1)
            pe.matmul(m.ps[0][:, 0:256], m.cumsum_mat[:, :], flat, start=True, stop=True).then_inc(sm.summed, 1)
            pe.wait_ge(sm.g, 1)
            g = m.g_nat[:, :, :].rearrange("p i h -> p (i h)")
            pe.transpose(m.ps[1][:, 0:P], g[:, 0:P], m.ident[:, :])
            pe.transpose(m.ps[1][:, P:2 * P], g[:, P:2 * P], m.ident[:, :]).then_inc(sm.g_turned, 1)
            pe.wait_ge(sm.gmax, 4)
            pe.transpose(m.ps[2][:, 0:P], m.gmax_t[:, 0, :], m.ident[:, :])
            pe.transpose(m.ps[2][:, P:2 * P], m.gmax_t[:, 1, :], m.ident[:, :]).then_inc(sm.gmax_turned, 1)

        @block.sync
        def _(sp):
            sp.wait_ge(sm.gmax, 4)
            for u in range(2):
                for c in range(2):
                    rows = m.gmax_dram[c, u * 16:(u + 1) * 16].rearrange("i h s -> (i h) s")
                    sp.dma_start(rows, m.gmax_t[:, u, c * S:(c + 1) * S]).then_inc(sm.saved, 16)
            sp.wait_ge(sm.saved, 64)


def l0_attention(nc, m):
    sm = m.at
    W = DH0 + 1
    with nc.Block() as block:

        @block.sync
        def _(sp):
            with sp.Fori(0, TILES // 2) as g:
                for j in range(2):
                    i = g * 2 + j
                    sp.wait_ge(sm.diff[j], upto(g))
                    for c in range(2):
                        row = m.gmax_dram[c, cols(i, 1)].rearrange("i h s -> (i h s)")
                        sp.dma_start(m.g_rows[j][c * S:(c + 1) * S, :], row.partition_broadcast(S)).then_inc(m.rows[j], 16)

        @block.gpsimd
        def _(pool):
            mask = m.head_mask[:, :].unsqueeze(2).to_broadcast([P, NH0, P])
            causal = m.causal_add[:, :].unsqueeze(1).to_broadcast([P, NH0, S])
            with pool.Fori(0, TILES // 2) as g:
                for j in range(2):
                    i = g * 2 + j
                    pool.wait_ge(sm.qk[j], upto(g))
                    q = m.XT[:, cols(i, P)].unsqueeze(1).to_broadcast([P, NH0, P])
                    pool.tensor_tensor(m.q_spread[j][:, :, :], q, mask, ALU.mult).then_inc(sm.spread[j], 1)
                    pool.wait_ge(sm.av[j], upto(g))
                    pool.tensor_copy(m.v_ones[j][:, :, 0:DH0],
                                     m.C[:, cols(i, 1), :].rearrange("p i (h d) -> p (i h) d", h=NH0)).then_inc(sm.v[j], 1)
                    pool.wait_ge(sm.diff[j], upto(g + 1))
                    pool.tensor_tensor(m.decay[j][:, :, :], m.decay[j][:, :, :], causal, ALU.add).then_inc(sm.causal[j], 1)

        @block.vector
        def _(dve):
            def difference(g, j):
                dve.wait_ge(m.rows[j], 32 * g + 32)
                own = m.g_nat[:, cols(g * 2 + j, 1), :].rearrange("p i h -> p (i h)").unsqueeze(2).to_broadcast([P, NH0, S])
                dve.tensor_tensor(m.decay[j][:, :, :], own, m.g_rows[j][:, :].rearrange("p (h s) -> p h s", h=NH0),
                                  ALU.subtract).then_inc(sm.diff[j], 1)

            with dve.Fori(0, TILES // 2) as g:
                for j in range(2):
                    dve.wait_ge(sm.c[j], upto(g))
                    difference(g, j)
                for j in range(2):
                    dve.wait_ge(sm.exp[j], upto(g + 1))
                    dve.wait_ge(sm.qk[j], upto(g + 1))
                    dve.wait_ge(sm.av[j], upto(g))
                    dve.tensor_tensor(m.c_t[j][:, :, :], m.ps[j][:, :].rearrange("p (h s) -> p h s", h=NH0),
                                      m.decay[j][:, :, :], ALU.mult).then_inc(sm.c[j], 1)

        @block.scalar
        def _(act):
            with act.Fori(0, TILES // 2) as g:
                for j in range(2):
                    act.wait_ge(sm.qk[j], upto(g))
                    act.activation(m.k_stage[j][:, :], m.CT[:, cols(g * 2 + j, P)], ACT.Copy, scale=DH0 ** -0.5).then_inc(sm.k[j], 1)
                for j in range(2):
                    act.wait_ge(sm.causal[j], upto(g + 1))
                    act.activation(m.decay[j][:, :, :], m.decay[j][:, :, :], ACT.Exp).then_inc(sm.exp[j], 1)
                for j in range(2):
                    act.wait_ge(sm.av[j], upto(g + 1))
                    for c in range(2):
                        act.copy(m.num[c * S:(c + 1) * S, cols(g * 2 + j, 1), :],
                                 m.ps[2 + 2 * j + c][c * S:(c + 1) * S, 0:NH0 * W].unsqueeze(1)).then_inc(sm.out[j], 1)

        @block.tensor
        def _(pe):
            with pe.Fori(0, TILES // 2) as g:
                for j in range(2):
                    pe.wait_ge(sm.k[j], upto(g + 1))
                    pe.wait_ge(sm.spread[j], upto(g + 1))
                    pe.wait_ge(sm.c[j], upto(g))
                    for c in range(2):
                        half = slice(c * S, (c + 1) * S)
                        ins = pe.matmul(m.ps[j][half, :], m.k_stage[j][:, half], m.q_spread[j][:, :, half],
                                        start=True, stop=True)
                    ins.then_inc(sm.qk[j], 1)
                for j in range(2):
                    pe.wait_ge(sm.c[j], upto(g + 1))
                    pe.wait_ge(sm.v[j], upto(g + 1))
                    pe.wait_ge(sm.out[j], upto(2 * g))
                    hold(pe, m)
                    for h in range(NH0):
                        for c in range(2):
                            half = slice(c * S, (c + 1) * S)
                            ins = pe.matmul(m.ps[2 + 2 * j + c][half, h * W:(h + 1) * W], m.c_t[j][half, h, :],
                                            m.v_ones[j][half, h, :], start=True, stop=True)
                    ins.then_inc(sm.av[j], 1)


def l0_attention_finish(nc, m):
    sm = m.af
    W = DH0 + 1
    num = m.num[:, :, :].rearrange("p i (h w) -> p (i h) w", w=W)
    hid = m.hid[:, :, :]
    N = TILES * NH0
    wide = [P, N, DH0]
    with nc.Block() as block:

        @block.vector
        def _(dve):
            step = Chain(dve, sm.dve)
            step.link(dve.scalar_tensor_tensor(m.den[:, :], num[:, :, DH0], -1.0, num[:, :, DH0], ALU.mult, ALU.max))
            step.link(dve.tensor_tensor(m.den[:, :], m.den[:, :], m.exp_neg_max[:, :, :].rearrange("p i h -> p (i h)"), ALU.max))
            step.link(dve.tensor_scalar(m.den[:, :], m.den[:, :], NORM_EPS, None, ALU.add))
            step.link(dve.reciprocal(m.den[:, :], m.den[:, :]))
            step.link(dve.tensor_tensor(hid, num[:, :, 0:DH0], m.den[:, :].unsqueeze(2).to_broadcast(wide), ALU.mult))
            step.link(dve.tensor_reduce(m.hmean[:, :], hid, AX, ALU.add))
            step.link(dve.tensor_scalar(m.hmean[:, :], m.hmean[:, :], 1.0 / DH0, None, ALU.mult))
            step.link(dve.tensor_tensor(hid, hid, m.hmean[:, :].unsqueeze(2).to_broadcast(wide), ALU.subtract))
            dve.sem_inc(sm.centered, 1)
            dve.wait_ge(sm.squared, 1)
            step.link(dve.tensor_reduce(m.hvar[:, :], m.hsq[:, :, :], AX, ALU.add))
            step.link(dve.tensor_scalar(m.hvar[:, :], m.hvar[:, :], 1.0 / DH0, LN_EPS, ALU.mult, ALU.add))
            dve.sem_inc(sm.var, 1)
            dve.wait_ge(m.tanh_ready, 1)
            step.link(dve.tensor_scalar(m.out_w_rows[:, :], m.out_w_rows[:, :], m.tanh_g[:, 0:1], None, ALU.mult))
            dve.wait_ge(sm.rstd, 1)
            step.link(dve.tensor_tensor(hid, hid, m.hvar[:, :].unsqueeze(2).to_broadcast(wide), ALU.mult))
            tiles = hid.rearrange("p (i h) d -> p i (h d)", h=NH0)
            step.link(dve.tensor_tensor(tiles, tiles, m.out_w_rows[:, :].unsqueeze(1).to_broadcast([P, TILES, E]), ALU.mult))
            step.link(dve.tensor_tensor(m.X[:, :, :], m.X[:, :, :], tiles, ALU.add))
            with dve.Fori(0, GROUPS) as g:
                for j in range(GROUP):
                    stats_of(dve, m, g * GROUP + j)

        @block.scalar
        def _(act):
            act.wait_ge(sm.centered, 1)
            act.activation(m.hsq[:, :, :], hid, ACT.Square).then_inc(sm.squared, 1)

        @block.gpsimd
        def _(pool):
            pool.wait_ge(sm.var, 1)
            half = m.minus_half[:, 0:1].to_broadcast([P, N])
            pool.tensor_tensor(m.hvar[:, :], m.hvar[:, :], half, ALU.pow).then_inc(sm.rstd, 1)


def l0_ffn_weights(nc, m):
    sm = m.fw
    with nc.Block() as block:

        @block.vector
        def _(dve):
            step = Chain(dve, sm.dve)
            dve.wait_ge(m.ffn0_loaded, 80)
            for raw, q, top, scale, n in ((m.gu_raw, m.gu_q, m.gu_top, m.gu_scale, 6), (m.dn_raw, m.dn_q, m.dn_top, m.dn_scale, 1)):
                wide = list(raw.shape)
                step.link(dve.tensor_reduce(top[:, :], raw, AX, ALU.max, apply_absolute_value=True))
                step.link(dve.tensor_scalar(scale[:, :], top[:, :], 1.0 / QMAX, None, ALU.mult))
                step.link(dve.reciprocal(top[:, :], scale[:, :]))
                step.link(dve.tensor_tensor(raw, raw, top[:, :].unsqueeze(2).to_broadcast(wide), ALU.mult))
                step.link(dve.tensor_scalar(raw, raw, MAGIC, None, ALU.add))
                step.link(dve.tensor_scalar(raw, raw, MAGIC + QMAX, MAGIC - QMAX - 1, ALU.min, ALU.max))
                step.link(dve.tensor_scalar(q, raw, MAGIC, None, ALU.subtract))
            step.link(dve.tensor_scalar(m.dn_diag[:, :], m.ident[:, :], m.dn_scale[:, 0:1], None, ALU.mult))
            dve.sem_inc(sm.quantized, 1)
            dve.wait_ge(sm.turned, 1)
            dve.tensor_copy(m.gu_t[:, :, :], m.ps[0][:, :].bitcast(BF16)[:, 0:6 * P].rearrange("p (k n) -> p k n", k=6)).then_inc(sm.dve, 1)
            dve.tensor_copy(m.dn_t[:, 0:2, :], m.ps[1][:, :].bitcast(BF16)[:, 0:2 * P].rearrange("p (k n) -> p k n", k=2))
            dve.tensor_copy(m.dn_t[0:96, 2, :], m.ps[1][0:96, :].bitcast(BF16)[:, 2 * P:3 * P])
            dve.tensor_copy(m.dn_row[:, :], m.ps[2][:, 0:P])

        @block.gpsimd
        def _(pool):
            pool.memset(m.dn_t[96:P, 2, :], 0.0)

        @block.tensor
        def _(pe):
            pe.wait_ge(sm.quantized, 1)
            for k in range(6):
                pe.transpose(m.ps[0][:, :].bitcast(BF16)[:, k * P:(k + 1) * P], m.gu_q[:, k, :], m.ident_bf[:, :])
            for k, n in enumerate((P, P, 96)):
                pe.transpose(m.ps[1][0:n, :].bitcast(BF16)[:, k * P:(k + 1) * P], m.dn_q[:, 0, k * P:k * P + n], m.ident_bf[:, :])
            pe.matmul(m.ps[2][:, 0:P], m.ones[:, :], m.dn_diag[:, :], start=True, stop=True).then_inc(sm.turned, 1)


def l0_ffn_norm(nc, m):
    with nc.Block() as block:

        @block.vector
        def _(dve):
            with dve.Fori(0, GROUPS) as g:
                for j in range(GROUP):
                    normalize(dve, m, m.XN[:, cols(g * GROUP + j, 1), :].rearrange("p i f -> p (i f)"),
                              g * GROUP + j).then_inc(m.fn.normed, 1)
                dve.wait_ge(m.fn.normed, upto(g * GROUP + GROUP))
                dve.tensor_reduce(m.x_top[:, cols(g, 1)], m.XN[:, cols(g, GROUP), :].rearrange("p i f -> p (i f)"),
                                  AX, ALU.max, apply_absolute_value=True)


def activation_scale(nc, m, sm, tops, clip, scales):
    with nc.Block() as block:

        @block.scalar
        def _(act):
            act.wait_ge(m.clips_loaded, 32)
            act.activation(m.clip_exp[0:1, :], clip, ACT.Exp, scale=-1.0).then_inc(sm.exp, 1)

        @block.vector
        def _(dve):
            step = Chain(dve, sm.dve)
            step.link(dve.tensor_reduce(m.top_col[:, :], tops, AX, ALU.max))
            dve.sem_inc(sm.col, 1)
            dve.wait_ge(sm.row, 1)
            step.link(dve.tensor_reduce(m.top_one[:, 0:1], m.ps[0][0:1, 0:P], AX, ALU.max))
            dve.wait_ge(sm.exp, 1)
            step.link(dve.tensor_scalar(m.top_one[:, 1:2], m.clip_exp[0:1, :], 1.0, None, ALU.add))
            step.link(dve.reciprocal(m.top_one[:, 1:2], m.top_one[:, 1:2]))
            step.link(dve.scalar_tensor_tensor(m.top_pair[:, 0:1], m.top_one[:, 0:1], 1.0 / QMAX, m.top_one[:, 1:2], ALU.mult, ALU.mult))
            step.link(dve.reciprocal(m.top_pair[:, 1:2], m.top_pair[:, 0:1]))
            dve.sem_inc(sm.pair, 1)
            dve.wait_ge(sm.spread, 1)
            dve.tensor_copy(scales[:, :], m.ps[1][:, 0:2])

        @block.tensor
        def _(pe):
            pe.wait_ge(sm.col, 1)
            pe.transpose(m.ps[0][0:1, 0:P], m.top_col[:, :], m.ident[:, :]).then_inc(sm.row, 1)
            pe.wait_ge(sm.pair, 1)
            pe.matmul(m.ps[1][:, 0:2], m.ones[0:1, :], m.top_pair[:, :], start=True, stop=True).then_inc(sm.spread, 1)


def l0_ffn_up(nc, m):
    sm = m.fu
    with nc.Block() as block:

        @block.vector
        def _(dve):
            dve.tensor_scalar(m.gu_scale[:, :], m.gu_scale[:, :], m.x_scale[:, 0:1], None, ALU.mult).then_inc(sm.scaled, 1)
            dve.wait_ge(sm.scaled, upto(1))
            with dve.Fori(0, GROUPS) as g:
                dve.wait_ge(sm.shifted, upto(g + 1))
                dve.tensor_scalar(m.round_x[:, :], m.round_x[:, :], MAGIC + QMAX, MAGIC - QMAX - 1, ALU.min, ALU.max).then_inc(sm.clipped, 1)
                dve.wait_ge(sm.clipped, upto(g + 1))
                dve.wait_ge(sm.turned, upto(g))
                dve.tensor_scalar(m.xq[:, :], m.round_x[:, :], MAGIC, None, ALU.subtract).then_inc(sm.quantized, 1)
                dve.wait_ge(sm.turned, upto(g + 1))
                dve.wait_ge(sm.upped, upto(3 * g))
                dve.tensor_copy(m.xq_t[:, :], m.ps[0][:, :].bitcast(BF16)[:, 0:512]).then_inc(sm.stood, 1)
                for k, n in enumerate(CHUNKS):
                    dve.wait_ge(sm.silu, upto(3 * g + k + 1))
                    h = m.HT[0:n, k, cols(g, 512)]
                    dve.scalar_tensor_tensor(h, m.ps[2 + 2 * k][0:n, :], m.gu_scale[0:n, 3 + k:4 + k],
                                             m.silu[k][0:n, :], ALU.mult, ALU.mult).then_inc(sm.hidden, 1)
                    dve.wait_ge(sm.hidden, upto(3 * g + k + 1))
                    dve.tensor_reduce(m.h_top[0:n, k, cols(g, 1)], h, AX, ALU.max, apply_absolute_value=True)

        @block.scalar
        def _(act):
            act.wait_ge(sm.scaled, upto(1))
            with act.Fori(0, GROUPS) as g:
                act.wait_ge(sm.quantized, upto(g))
                act.activation(m.round_x[:, :], m.XN[:, cols(g, GROUP), :].rearrange("p i f -> p (i f)"), ACT.Identity,
                               bias=m.magic[:, 0:1], scale=m.x_scale[:, 1:2]).then_inc(sm.shifted, 1)
                for k, n in enumerate(CHUNKS):
                    act.wait_ge(sm.upped, upto(3 * g + k + 1))
                    act.wait_ge(sm.hidden, upto(3 * g))
                    act.activation(m.silu[k][0:n, :], m.ps[1 + 2 * k][0:n, :], ACT.Silu, scale=m.gu_scale[0:n, k:k + 1]).then_inc(sm.silu, 1)

        @block.gpsimd
        def _(pool):
            pool.memset(m.HT[96:P, 2, :], 0.0)
            pool.memset(m.h_top[96:P, 2, :], 0.0)

        @block.tensor
        def _(pe):
            with pe.Fori(0, GROUPS) as g:
                pe.wait_ge(sm.quantized, upto(g + 1))
                pe.wait_ge(sm.stood, upto(g))
                for j in range(GROUP):
                    ins = pe.transpose(m.ps[0][:, :].bitcast(BF16)[:, j * P:(j + 1) * P], m.xq[:, j * P:(j + 1) * P], m.ident_bf[:, :])
                ins.then_inc(sm.turned, 1)
                pe.wait_ge(sm.stood, upto(g + 1))
                for k, n in enumerate(CHUNKS):
                    pe.wait_ge(sm.hidden, upto(3 * g))
                    pe.matmul(m.ps[1 + 2 * k][0:n, :], m.gu_t[:, k, 0:n], m.xq_t[:, :], start=True, stop=True)
                    pe.matmul(m.ps[2 + 2 * k][0:n, :], m.gu_t[:, 3 + k, 0:n], m.xq_t[:, :], start=True, stop=True).then_inc(sm.upped, 1)


def l0_ffn_down(nc, m):
    sm = m.fd
    with nc.Block() as block:

        @block.vector
        def _(dve):
            step = Chain(dve, sm.dve)
            step.link(dve.tensor_scalar(m.dn_row[:, :], m.dn_row[:, :], m.h_scale[:, 0:1], m.tanh_g[:, 2:3], ALU.mult, ALU.mult))
            scale = m.dn_row[:, :].unsqueeze(1).to_broadcast([P, GROUP, E])
            with dve.Fori(0, GROUPS) as g:
                dve.wait_ge(sm.shifted, upto(g + 1))
                dve.tensor_scalar(m.round_h[:, :, :], m.round_h[:, :, :], MAGIC + QMAX, MAGIC - QMAX - 1, ALU.min, ALU.max).then_inc(sm.clipped, 1)
                dve.wait_ge(sm.clipped, upto(g + 1))
                dve.wait_ge(sm.downed, upto(g))
                dve.tensor_scalar(m.hq[:, :, :], m.round_h[:, :, :], MAGIC, None, ALU.subtract).then_inc(sm.quantized, 1)
                dve.wait_ge(sm.downed, upto(g + 1))
                dve.tensor_tensor(m.down[:, :, :], m.ps[0][:, :].rearrange("p (j f) -> p j f", j=GROUP), scale, ALU.mult).then_inc(sm.out, 1)
                dve.wait_ge(sm.out, upto(g + 1))
                x = m.X[:, cols(g, GROUP), :]
                dve.tensor_tensor(x, x, m.down[:, :, :], ALU.add).then_inc(sm.added, 1)
                dve.wait_ge(sm.added, upto(g + 1))
                for j in range(GROUP):
                    stats_of(dve, m, g * GROUP + j)

        @block.scalar
        def _(act):
            with act.Fori(0, GROUPS) as g:
                act.wait_ge(sm.quantized, upto(g))
                act.activation(m.round_h[:, :, :], m.HT[:, :, cols(g, 512)], ACT.Identity, bias=m.magic[:, 0:1],
                               scale=m.h_scale[:, 1:2]).then_inc(sm.shifted, 1)

        @block.tensor
        def _(pe):
            with pe.Fori(0, GROUPS) as g:
                pe.wait_ge(sm.quantized, upto(g + 1))
                pe.wait_ge(sm.out, upto(g))
                for j in range(GROUP):
                    for k in range(3):
                        ins = pe.matmul(m.ps[0][:, j * P:(j + 1) * P], m.hq[:, k, j * P:(j + 1) * P], m.dn_t[:, k, :],
                                        start=(k == 0), stop=(k == 2))
                ins.then_inc(sm.downed, 1)


def split_parts(eng, step, out, exact):
    step.link(eng.tensor_tensor(exact, exact, out[:, 0], ALU.subtract))
    step.link(eng.tensor_copy(out[:, 1], exact))
    return eng.tensor_tensor(out[:, 2], exact, out[:, 1], ALU.subtract)


LEFT_PARTS = (0, 1, 2, 0, 1, 0)
RIGHT_PARTS = (0, 0, 0, 1, 1, 2)
STACK = len(LEFT_PARTS) * DH1


def load_left(eng, out, parts, sem):
    row = 0
    for n in (3, 2, 1):
        eng.dma_start(out[row:row + n * DH1], parts[:, 0:n].rearrange("h k d t -> (k d) h t")).then_inc(sem, 16)
        row += n * DH1


def load_right(eng, out, parts, sem):
    for r, part in enumerate(RIGHT_PARTS):
        eng.dma_start(out[r * DH1:(r + 1) * DH1], parts[:, part].rearrange("h d t -> d h t")).then_inc(sem, 16)


def l1_weights(nc, m):
    sm = m.lw
    with nc.Block() as block:

        @block.tensor
        def _(pe):
            pe.wait_ge(m.proj_loaded, 64)
            for k in range(4):
                ins = pe.transpose(m.ps[0][:, k * P:(k + 1) * P], m.proj_raw[:, k, :], m.ident[:, :])
            pe.wait_ge(m.pos_loaded, 48)
            for k in range(4):
                ins = pe.transpose(m.ps[1][:, k * S:(k + 1) * S],
                                   m.pos_k_raw[:, :, :].rearrange("s t d -> s (t d)")[:, k * P:(k + 1) * P], m.ident[0:S, 0:S])
            ins.then_inc(sm.turned, 1)

        @block.vector
        def _(dve):
            step = Chain(dve, sm.dve)
            dve.wait_ge(sm.turned, 1)
            pos = m.ps[1][:, 0:4 * S]
            dve.tensor_copy(m.pos_parts[:, 0], pos)
            step.link(dve.tensor_copy(m.pos_exact[:, :], pos))
            split_parts(dve, step, m.pos_parts, m.pos_exact[:, :]).then_inc(sm.stood, 1)
            dve.tensor_copy(m.proj_t[:, :, :], m.ps[0][:, :].rearrange("p (k n) -> p k n", k=4))
            dve.wait_ge(m.proj_bias_loaded, 64)
            dve.tensor_scalar(m.bo_rows[:, :], m.bo_rows[:, :], m.tanh_g[:, 1:2], None, ALU.mult)

        @block.sync
        def _(sp):
            sp.wait_ge(sm.stood, 1)
            sp.dma_start(m.pos_dram, m.pos_parts[:, :, :]).then_inc(sm.moved, 16)
            sp.wait_ge(sm.moved, 16)
            for r, part in enumerate(RIGHT_PARTS):
                src = m.pos_dram[:, part].rearrange("(t d) k -> d t k", d=DH1)
                sp.dma_start(m.pos_right[r * DH1:(r + 1) * DH1], src).then_inc(sm.moved, 16)
            sp.wait_ge(sm.moved, 16 + 16 * len(RIGHT_PARTS))


def l1_project(nc, m):
    sm = m.pj
    with nc.Block() as block:

        @block.vector
        def _(dve):
            def norm(g):
                dve.wait_ge(sm.turned, upto(g))
                for j in range(GROUP):
                    normalize(dve, m, m.stage_x[:, j, :], g * GROUP + j).then_inc(sm.normed, 1)

            def split(g):
                for w in range(2):
                    exact, parts = m.qk_exact[:, w, :], m.qk_parts[:, w]
                    dve.wait_ge(sm.exact_out, upto(2 * g + w + 1))
                    dve.tensor_tensor(exact, exact, parts[:, 0], ALU.subtract).then_inc(sm.rest, 1)
                    dve.wait_ge(sm.rest, upto(2 * g + w + 1))
                    dve.tensor_copy(parts[:, 1], exact).then_inc(sm.middle, 1)
                    dve.wait_ge(sm.middle, upto(2 * g + w + 1))
                    dve.tensor_tensor(parts[:, 2], exact, parts[:, 1], ALU.subtract).then_inc(sm.low, 1)

            norm(0)
            with dve.Fori(0, GROUPS - 1) as g:
                norm(g + 1)
                split(g)
            split(GROUPS - 1)

        @block.tensor
        def _(pe):
            with pe.Fori(0, GROUPS) as g:
                pe.wait_ge(sm.xt_out, upto(g))
                pe.wait_ge(sm.normed, upto(g * GROUP + GROUP))
                for j in range(GROUP):
                    ins = pe.transpose(m.ps[0][:, j * P:(j + 1) * P], m.stage_x[:, j, :], m.ident[:, :])
                ins.then_inc(sm.turned, 1)
                pe.wait_ge(sm.exact_out, upto(2 * g))
                pe.matmul(m.ps[2][:, :], m.proj_t[:, 1, :], m.CT[:, cols(g, 512)], start=True, stop=True).then_inc(sm.k_done, 1)
                pe.wait_ge(sm.xt_out, upto(g + 1))
                pe.matmul(m.ps[1][:, :], m.proj_t[:, 0, :], m.stage_xt[:, :], start=True, stop=True).then_inc(sm.q_done, 1)

        @block.scalar
        def _(act):
            with act.Fori(0, GROUPS) as g:
                act.wait_ge(sm.turned, upto(g + 1))
                act.wait_ge(sm.q_done, upto(g))
                act.copy(m.stage_xt[:, :], m.ps[0][:, :]).then_inc(sm.xt_out, 1)
                for w, done in enumerate((sm.q_done, sm.k_done)):
                    src, bias = m.ps[1 + w][:, :], m.proj_bias[:, w:w + 1]
                    act.wait_ge(done, upto(g + 1))
                    act.wait_ge(sm.low, upto(2 * g))
                    act.wait_ge(sm.parts_saved[w], upto(48 * g))
                    act.activation(m.qk_parts[:, w, 0, :], src, ACT.Identity, bias=bias)
                    act.activation(m.qk_exact[:, w, :], src, ACT.Identity, bias=bias).then_inc(sm.exact_out, 1)

        @block.sync
        def _(sp):
            with sp.Fori(0, GROUPS) as g:
                for w in range(2):
                    sp.wait_ge(sm.low, upto(2 * g + w + 1))
                    hold(sp, m)
                    for part in range(3):
                        dst = m.qk_dram[w][cols(g, 1), :, part].rearrange("g h d t -> (g h) d t")
                        sp.dma_start(dst, m.qk_parts[:, w, part, :]).then_inc(sm.parts_saved[w], 16)
            for w in range(2):
                sp.wait_ge(sm.parts_saved[w], upto(48 * GROUPS))


def l1_relative(nc, m):
    sm = m.rl
    with nc.Block() as block:

        @block.tensor
        def _(pe):
            with pe.Fori(0, GROUPS // 2) as pair:
                for z in range(2):
                    g = 2 * pair + z
                    q = m.q_left[z][:, :, :].rearrange("k h (b t) -> k (h b) t", t=S)
                    pe.wait_ge(sm.loaded[z], upto(48 * pair + 48))
                    for n in range(8):
                        pe.wait_ge(sm.out[n % 4], upto(2 * g + n // 4))
                        for k in range(8):
                            t = 8 * n + k
                            ins = pe.matmul(m.ps[n % 4][:, k * S:(k + 1) * S], q[:, :, t],
                                            m.pos_right[:, t % 16, (t // 16) * S:(t // 16 + 1) * S], start=True, stop=True)
                        ins.then_inc(sm.done, 1)

        def take(eng, copy, mine):
            with eng.Fori(0, GROUPS) as g:
                for n in mine:
                    half = n // 4
                    eng.wait_ge(sm.done, upto(8 * g + n + 1))
                    if n in (mine[0], mine[2]):
                        eng.wait_ge(sm.saved[half], upto(16 * g))
                    copy(m.rel[half][:, 512 * (n % 4):512 * (n % 4 + 1)], m.ps[n % 4][:, :]).then_inc(sm.out[n % 4], 1)

        @block.scalar
        def _(act):
            take(act, act.copy, (0, 2, 4, 6))

        @block.vector
        def _(dve):
            take(dve, dve.tensor_copy, (1, 3, 5, 7))

        @block.sync
        def _(sp):
            def load(g, z):
                load_left(sp, m.q_left[z], m.qk_dram[0][cols(g, 1)].rearrange("g h k d t -> (g h) k d t"), sm.loaded[z])

            def save(g):
                rows = m.rel_dram[cols(g, 1)].rearrange("g h b t s -> (g h b) (t s)")
                for half in range(2):
                    for bank in range(4):
                        sp.wait_ge(sm.out[bank], upto(2 * g + half + 1))
                        hold(sp, m)
                    sp.dma_start(rows[:, 2048 * half:2048 * (half + 1)], m.rel[half][:, :]).then_inc(sm.saved[half], 16)

            load(0, 0)
            load(1, 1)
            with sp.Fori(0, GROUPS // 2 - 1) as pair:
                for z in range(2):
                    save(2 * pair + z)
                    load(2 * pair + z + 2, z)
            for z in range(2):
                save(GROUPS - 2 + z)
            for half in range(2):
                sp.wait_ge(sm.saved[half], upto(16 * GROUPS))


def load_mask(nc, m):
    sm = m.a1
    with nc.Block() as block:

        @block.sync
        def _(sp):
            sp.dma_start(m.mask_in[:, :, :], m.mask.rearrange("(i c) t s -> (c t) i s", c=2)).then_inc(sm.mask_in, 16)

        @block.vector
        def _(dve):
            dve.wait_ge(sm.mask_in, 16)
            dve.tensor_scalar(m.mask_add[:, :, :], m.mask_in[:, :, :], 0.0, FAR, ALU.is_equal, ALU.mult)


def l1_attention(nc, m):
    sm = m.a1
    W = DH1 + 1
    LAST = GROUPS - 1
    scores = m.wide[0][:, :]
    turned = m.wide[1][:, :]
    rel_v = m.wide[2][0:S, :]
    values = m.ps[4]

    def groups(eng, body):
        body(0, first=True, last=False)
        with eng.Fori(1, LAST) as g:
            body(g, first=False, last=False)
        body(LAST, first=False, last=True)

    with nc.Block() as block:

        @block.sync
        def _(sp):
            def load_rel(g, j, filled=True):
                n = g * GROUP + j
                if filled:
                    sp.wait_ge(sm.added, upto(n - 3))
                    hold(sp, m)
                for c in range(2):
                    sp.dma_start(m.rel_in[j][c * S:(c + 1) * S, :, :],
                                 m.rel_dram[cols(g, 1), :, 2 * j + c].rearrange("g h t s -> (g t) h s")).then_inc(m.rel_sem[j], 16)

            def load_qk(g, u, filled=True):
                if filled:
                    sp.wait_ge(sm.scored, upto(g * GROUP + 2 * u - 2))
                    hold(sp, m)
                q, k = (d[cols(g, 1), :, :, :, 256 * u:256 * (u + 1)].rearrange("g h k d t -> (g h) k d t") for d in m.qk_dram)
                load_left(sp, m.q_left[u], q, sm.qk_in[u])
                load_right(sp, m.k_right[u], k, sm.qk_in[u])

            def turn_pos(g):
                sp.wait_ge(sm.pv_out, upto(g + 1))
                hold(sp, m)
                sp.dma_start(m.pv_dram[cols(g, 1)].rearrange("g n t e -> (g n) (t e)"), m.pv[:, :]).then_inc(sm.pv_saved, 16)
                sp.wait_ge(sm.pv_saved, upto(16 * g + 16))
                hold(sp, m)
                sp.wait_ge(sm.summed, upto(g))
                hold(sp, m)
                sp.dma_start(m.pv_in[:, :, :], m.pv_dram[cols(g, 1)].rearrange("g (n c) t e -> (g c t) n e", c=2)).then_inc(sm.pv_back, 16)

            for u in range(2):
                load_qk(0, u, False)
                for j in (2 * u, 2 * u + 1):
                    load_rel(0, j, False)
            with sp.Fori(0, LAST) as g:
                load_qk(g + 1, 0)
                load_rel(g + 1, 0)
                load_rel(g + 1, 1)
                load_qk(g + 1, 1)
                load_rel(g + 1, 2)
                load_rel(g + 1, 3)
                turn_pos(g)
            turn_pos(LAST)

        @block.gpsimd
        def _(pool):
            def stage(n):
                src = m.CT[:, cols(n, P)].rearrange("p (c s) -> p c s", c=2)
                for twice in range(2):
                    pool.tensor_copy(m.ct_twice[:, :, twice, :], src).then_inc(sm.ct_staged, 1)

            def mask(g, j):
                n, slot = g * GROUP + j, j % GROUP
                pool.wait_ge(m.rel_sem[slot], 32 * (g + j // GROUP) + 32)
                rel = m.rel_in[slot][:, :, :]
                pool.tensor_tensor(rel, rel, m.mask_add[:, cols(n, 1), :].to_broadcast([P, NH1, S]), ALU.add).then_inc(sm.masked, 1)

            def body(g, first, last):
                for j in range(GROUP):
                    if not last or j + 2 < GROUP:
                        mask(g, j + 2)
                    if not last or j + 1 < GROUP:
                        pool.wait_ge(sm.v_done, upto(g * GROUP + j + 1))
                        stage(g * GROUP + j + 1)

            stage(0)
            mask(0, 0)
            mask(0, 1)
            groups(pool, body)

        @block.vector
        def _(dve):
            def place_values(g, j):
                n = g * GROUP + j
                dve.wait_ge(sm.v_done, upto(n + 1))
                dve.wait_ge(sm.av_done, upto(n))
                for c in range(2):
                    for p in range(2):
                        half = slice(p * S, (p + 1) * S)
                        src = values[half, c * P:(c + 1) * P].rearrange("s (n p d) -> s n p d", p=2, d=DH1)[:, :, p, :]
                        bias = m.bv_rows[half, :].rearrange("s (n p d) -> s n p d", p=2, d=DH1)[:, :, p, :]
                        dve.tensor_tensor(m.v_block[half, :, c, p, 0:DH1], src, bias, ALU.add).then_inc(sm.v_out, 1)

            def shift(g, j, filled=True):
                n, z = g * GROUP + j, j % 2
                dve.wait_ge(sm.masked, upto(n + 1))
                dve.wait_ge(sm.scored, upto(n + 1))
                if filled:
                    dve.wait_ge(sm.exped, upto(n - 1))
                t = m.soft[z][:, :, :]
                dve.tensor_tensor(t, scores.rearrange("p (h s) -> p h s", s=S), m.rel_in[j % GROUP][:, :, :], ALU.add).then_inc(sm.added, 1)
                dve.wait_ge(sm.added, upto(n + 1))
                dve.tensor_reduce(m.row_max[:, :], t, AX, ALU.max).then_inc(sm.maxed, 1)
                dve.wait_ge(sm.maxed, upto(2 * n + 1))
                dve.tensor_scalar(m.row_max[:, :], m.row_max[:, :], FAR / 10, None, ALU.max).then_inc(sm.maxed, 1)
                dve.wait_ge(sm.maxed, upto(2 * n + 2))
                dve.tensor_tensor(t, t, m.row_max[:, :].unsqueeze(2).to_broadcast([P, NH1, S]), ALU.subtract).then_inc(sm.shifted, 1)

            def weigh(g):
                dve.wait_ge(sm.pv_back, upto(16 * g + 16))
                dve.wait_ge(sm.av_out, upto(8 * g + 8))
                av = m.av[:, cols(g, GROUP), :].rearrange("p i (h w) -> p (i h) w", w=W)
                dve.tensor_scalar(m.row_sum[:, :], av[:, :, DH1], 1e-30, None, ALU.max).then_inc(sm.small, 1)
                dve.wait_ge(sm.small, upto(4 * g + 1))
                dve.reciprocal(m.row_sum[:, :], m.row_sum[:, :]).then_inc(sm.small, 1)
                att = m.att[:, :, :].rearrange("p i (h d) -> p (i h) d", d=DH1)
                pv = m.pv_in[:, :, :].rearrange("p n (q d) -> p (n q) d", d=DH1)
                dve.wait_ge(sm.att_turned, upto(g))
                dve.tensor_tensor(att, av[:, :, 0:DH1], pv, ALU.add).then_inc(sm.summed, 1)
                dve.wait_ge(sm.summed, upto(g + 1))
                dve.wait_ge(sm.small, upto(4 * g + 2))
                dve.tensor_tensor(att, att, m.row_sum[:, :].unsqueeze(2).to_broadcast([P, GROUP * NH1, DH1]), ALU.mult).then_inc(sm.att_done, 1)

            def add_to_x(g):
                dve.wait_ge(sm.wo_done, upto(g + 1))
                bo = m.bo_rows[:, :].unsqueeze(1).to_broadcast([P, GROUP, E])
                dve.scalar_tensor_tensor(m.res[:, :, :], m.ps7[:, :].rearrange("p (i f) -> p i f", f=E), m.tanh_g[:, 1:2],
                                         bo, ALU.mult, ALU.add).then_inc(sm.small, 1)
                dve.wait_ge(sm.small, upto(4 * g + 3))
                x = m.X[:, cols(g, GROUP), :]
                dve.tensor_tensor(x, x, m.res[:, :, :], ALU.add).then_inc(sm.small, 1)
                dve.wait_ge(sm.small, upto(4 * g + 4))
                for j in range(GROUP):
                    stats_of(dve, m, g * GROUP + j)

            def body(g, first, last):
                for j in range(GROUP):
                    place_values(g, j)
                    if not last or j + 2 < GROUP:
                        shift(g, j + 2)
                    if j == 1 and not first:
                        weigh(g - 1)
                    if j == 3 and not first:
                        add_to_x(g - 1)

            shift(0, 0, False)
            shift(0, 1, False)
            groups(dve, body)
            weigh(LAST)
            add_to_x(LAST)

        @block.scalar
        def _(act):
            def exp(g, j, filled=True):
                n, z = g * GROUP + j, j % 2
                act.wait_ge(sm.shifted, upto(n + 1))
                if filled:
                    act.wait_ge(sm.p_turned, upto(n - 1))
                act.activation(m.expd[z][:, :, :], m.soft[z][:, :, :], ACT.Exp, scale=DH1 ** -0.5).then_inc(sm.exped, 1)

            def att_out(g):
                act.wait_ge(sm.att_turned, upto(g + 1))
                act.wait_ge(sm.wo_done, upto(g))
                act.copy(m.att_t[:, :], m.ps7[:, :]).then_inc(sm.att_out, 1)

            def body(g, first, last):
                for j in range(GROUP):
                    n = g * GROUP + j
                    if j == 2 and not first:
                        att_out(g - 1)
                    act.wait_ge(sm.p_turned, upto(n + 1))
                    if j == 0 and not first:
                        act.wait_ge(sm.pv_done, upto(g))
                    act.copy(m.p_t[:, j, :], turned).then_inc(sm.pt_out, 1)
                    act.wait_ge(sm.av_done, upto(n + 1))
                    for c in range(2):
                        half = slice(c * S, (c + 1) * S)
                        src = m.ps6[half, 0:288].rearrange("t (n c q) -> t n c q", c=2, n=8)[:, :, c, :]
                        dst = m.av[half, cols(n, 1), :].rearrange("t i (n q) -> t (i n) q", n=8)
                        act.copy(dst, src).then_inc(sm.av_out, 1)
                    if j == GROUP - 1:
                        act.wait_ge(sm.pv_done, upto(g + 1))
                        if not first:
                            act.wait_ge(sm.pv_saved, upto(16 * g))
                        act.copy(m.pv[:, :], rel_v).then_inc(sm.pv_out, 1)
                    if not last or j + 2 < GROUP:
                        exp(g, j + 2)

            exp(0, 0, False)
            exp(0, 1, False)
            groups(act, body)
            att_out(LAST)

        @block.tensor
        def _(pe):
            def scores_of(g, j):
                n, u = g * GROUP + j, (j // 2) % 2
                if j % 2 == 0:
                    pe.wait_ge(sm.qk_in[u], 144 * (g + j // GROUP) + 144)
                pe.wait_ge(sm.added, upto(n))
                hold(pe, m)
                for c in range(2):
                    tok = slice(P * (j % 2) + c * S, P * (j % 2) + (c + 1) * S)
                    for h in range(NH1):
                        ins = pe.matmul(scores[c * S:(c + 1) * S, h * S:(h + 1) * S], m.q_left[u][:, h, tok],
                                        m.k_right[u][:, h, tok], start=True, stop=True)
                ins.then_inc(sm.scored, 1)

            def values_of(g, j):
                n = g * GROUP + j
                pe.wait_ge(sm.ct_staged, upto(2 * n + 2))
                pe.wait_ge(sm.v_out, upto(4 * n))
                if j == 0:
                    pe.wait_ge(sm.pv_out, upto(g))
                for c in range(2):
                    ins = pe.matmul(values[:, c * P:(c + 1) * P], m.ct_twice[:, c, :, :].rearrange("p a s -> p (a s)"),
                                    m.proj_t[:, 2, :], start=True, stop=True)
                ins.then_inc(sm.v_done, 1)

            def turn(g, j):
                n, z = g * GROUP + j, j % 2
                pe.wait_ge(sm.exped, upto(n + 1))
                pe.wait_ge(sm.pt_out, upto(n))
                for pair in range(8):
                    ins = pe.transpose(turned[:, P * pair:P * (pair + 1)],
                                       m.expd[z][:, 2 * pair:2 * pair + 2, :].rearrange("p h s -> p (h s)"), m.ident[:, :])
                ins.then_inc(sm.p_turned, 1)

            def sum_values(g, j):
                n = g * GROUP + j
                pe.wait_ge(sm.pt_out, upto(n + 1))
                pe.wait_ge(sm.v_out, upto(4 * n + 4))
                pe.wait_ge(sm.av_out, upto(2 * n))
                for pair in range(8):
                    ins = pe.matmul(m.ps6[:, 36 * pair:36 * (pair + 1)], m.p_t[:, j, P * pair:P * (pair + 1)],
                                    m.v_block[:, pair, :, :, :].rearrange("p c q w -> p (c q w)"), start=True, stop=True)
                ins.then_inc(sm.av_done, 1)

            def sum_pos(g):
                p = m.p_t[:, :, :].rearrange("p i (n t) -> p (i n) t", t=S)
                for t in range(S):
                    ins = pe.matmul(rel_v[:, 16 * t:16 * (t + 1)], p[:, :, t], m.pos_v[:, t, :], start=True, stop=True)
                ins.then_inc(sm.pv_done, 1)

            def turn_att(g):
                pe.wait_ge(sm.att_done, upto(g + 1))
                pe.wait_ge(sm.small, upto(4 * g + 2))
                for j in range(GROUP):
                    ins = pe.transpose(m.ps7[:, P * j:P * (j + 1)], m.att[:, j, :], m.ident[:, :])
                ins.then_inc(sm.att_turned, 1)

            def project_out(g):
                pe.wait_ge(sm.att_out, upto(g + 1))
                for j in range(GROUP):
                    ins = pe.matmul(m.ps7[:, P * j:P * (j + 1)], m.att_t[:, P * j:P * (j + 1)], m.proj_t[:, 3, :], start=True, stop=True)
                ins.then_inc(sm.wo_done, 1)

            def body(g, first, last):
                for j in range(GROUP):
                    ahead = not last or j + 2 < GROUP
                    if j > 0:
                        values_of(g, j)
                    if ahead:
                        scores_of(g, j + 2)
                    if j == 0:
                        values_of(g, j)
                    if j == 2 and not first:
                        turn_att(g - 1)
                    turn(g, j)
                    if j == 3 and not first:
                        project_out(g - 1)
                    sum_values(g, j)
                sum_pos(g)

            scores_of(0, 0)
            scores_of(0, 1)
            groups(pe, body)
            turn_att(LAST)
            project_out(LAST)


def expert_weights(nc, m):
    with nc.Block() as block:

        @block.vector
        def _(dve):
            dve.wait_ge(m.moe_loaded, 48)
            for raw, high, low in ((m.W1_sb, m.W1_h, m.W1_l), (m.W2_sb, m.W2_h, m.W2_l)):
                dve.tensor_copy(high, raw).then_inc(m.mo_split, 1)
            for k, (raw, high, low) in enumerate(((m.W1_sb, m.W1_h, m.W1_l), (m.W2_sb, m.W2_h, m.W2_l))):
                dve.wait_ge(m.mo_split, k + 1)
                dve.tensor_tensor(low, raw, high.bitcast(F32), ALU.subtract)
            dve.wait_ge(m.b1_turned, 1)
            dve.tensor_copy(m.b1_cols[:, :], m.ps[0][:, 0:4 * EXPERTS])

        @block.tensor
        def _(pe):
            pe.wait_ge(m.moe_small_loaded, 64)
            pe.transpose(m.ps[0][:, 0:4 * EXPERTS], m.b1_raw[:, :], m.ident[0:4 * EXPERTS, 0:4 * EXPERTS]).then_inc(m.b1_turned, 1)


def router(nc, m):
    sm = m.ro
    wide = [P, TILES, EXPERTS]
    with nc.Block() as block:

        @block.vector
        def _(dve):
            dve.wait_ge(m.moe_small_loaded, 64)
            with dve.Fori(0, GROUPS // 2) as g2:
                for z in range(2):
                    g = g2 * 2 + z
                    dve.wait_ge(sm.turned[z], upto(g2))
                    for j in range(GROUP):
                        ins = normalize(dve, m, m.stage_x[z][:, j, :], g * GROUP + j)
                    ins.then_inc(sm.normed[z], 1)
                for z in range(2):
                    g = g2 * 2 + z
                    dve.wait_ge(sm.logits[z], upto(g2 + 1))
                    dve.tensor_tensor(m.logit[:, cols(g, GROUP), :], m.ps[2 + z][:, 0:32].rearrange("p (j e) -> p j e", e=EXPERTS),
                                      m.br_rows[:, :].unsqueeze(1).to_broadcast([P, GROUP, EXPERTS]), ALU.add).then_inc(sm.taken[z], 1)

        @block.tensor
        def _(pe):
            with pe.Fori(0, GROUPS // 2) as g2:
                for z in range(2):
                    pe.wait_ge(sm.normed[z], upto(g2 + 1))
                    pe.wait_ge(sm.xt_out[z], upto(g2))
                    for j in range(GROUP):
                        ins = pe.transpose(m.ps[z][:, P * j:P * (j + 1)], m.stage_x[z][:, j, :], m.ident[:, :])
                    ins.then_inc(sm.turned[z], 1)
                for z in range(2):
                    pe.wait_ge(sm.xt_out[z], upto(g2 + 1))
                    pe.wait_ge(sm.taken[z], upto(g2))
                    for j in range(GROUP):
                        ins = pe.matmul(m.ps[2 + z][:, EXPERTS * j:EXPERTS * (j + 1)], m.stage_xt[z][:, P * j:P * (j + 1)],
                                        m.Wr_sb[:, :], start=True, stop=True)
                    ins.then_inc(sm.logits[z], 1)

        @block.scalar
        def _(act):
            with act.Fori(0, GROUPS // 2) as g2:
                for z in range(2):
                    act.wait_ge(sm.turned[z], upto(g2 + 1))
                    act.wait_ge(sm.logits[z], upto(g2))
                    act.copy(m.stage_xt[z][:, :], m.ps[z][:, :]).then_inc(sm.xt_out[z], 1)
                    act.wait_ge(sm.xt_out[z], upto(g2 + 1))
                    act.copy(m.XR[:, cols(g2 * 2 + z, 512)], m.stage_xt[z][:, :])

    with nc.Block() as block:

        @block.vector
        def _(dve):
            step = Chain(dve, m.rt.dve)
            for i in range(TILES):
                ins = dve.max(m.best[:, i, :], m.logit[:, i, :])
            step.link(ins)
            step.link(dve.tensor_tensor(m.chosen[:, :, :], m.logit[:, :, :], m.best[:, :, 1:2].to_broadcast(wide), ALU.is_ge))
            step.link(dve.tensor_tensor(m.logit[:, :, :], m.logit[:, :, :], m.best[:, :, 0:1].to_broadcast(wide), ALU.subtract))
            dve.sem_inc(m.rt.shifted, 1)
            dve.wait_ge(m.rt.exp, 1)
            step.link(dve.tensor_tensor(m.weight[:, :, :], m.weight[:, :, :], m.chosen[:, :, :], ALU.mult))
            step.link(dve.tensor_reduce(m.wsum[:, :], m.weight[:, :, :], AX, ALU.add))
            step.link(dve.reciprocal(m.wsum[:, :], m.wsum[:, :]))
            step.link(dve.tensor_scalar(m.wsum[:, :], m.wsum[:, :], m.tanh_g[:, 3:4], None, ALU.mult))
            dve.tensor_tensor(m.weight[:, :, :], m.weight[:, :, :], m.wsum[:, :].unsqueeze(2).to_broadcast(wide), ALU.mult)

        @block.scalar
        def _(act):
            act.wait_ge(m.rt.shifted, 1)
            act.activation(m.weight[:, :, :], m.logit[:, :, :], ACT.Exp).then_inc(m.rt.exp, 1)


def experts(nc, m):
    sm = m.mo
    UP = (2, 3, 6, 7)
    with nc.Block() as block:

        @block.gpsimd
        def _(pool):
            with pool.Fori(0, GROUPS) as g:
                pool.wait_ge(sm.w_turned, upto(g))
                pool.tensor_copy(m.w_stage[:, :, :], m.weight[:, cols(g, GROUP), :]).then_inc(sm.w_staged, 1)
                pool.wait_ge(sm.x_high, upto(g + 1))
                pool.tensor_tensor(m.xt_l[:, :], m.XR[:, cols(g, 512)], m.xt_h[:, :].bitcast(F32), ALU.subtract).then_inc(sm.x_low, 1)

        @block.vector
        def _(dve):
            def split(g, e):
                z = e % 2
                for c in range(4):
                    if c % 2:
                        dve.wait_ge(sm.gelu, upto(32 * g + 4 * e + c + 1))
                        dve.wait_ge(sm.down_done, upto(8 * g + max(e - 1, 0)))
                        dve.tensor_copy(m.h_h[z][:, c, :], m.h[c][:, :]).then_inc(sm.h_high, 1)
                for c in (0, 2, 1, 3):
                    if c % 2:
                        dve.wait_ge(sm.h_high, upto(16 * g + 2 * e + (c + 1) // 2))
                    else:
                        dve.wait_ge(sm.h_high2, upto(16 * g + 2 * e + c // 2 + 1))
                    dve.tensor_tensor(m.h_l[z][:, c, :], m.h[c][:, :], m.h_h[z][:, c, :].bitcast(F32), ALU.subtract).then_inc(sm.h_split, 1)

            def combine(g, e):
                dve.wait_ge(sm.down_done, upto(8 * g + e + 1))
                for j in range(GROUP):
                    if e == 0:
                        dve.wait_ge(sm.acc, upto(g + 1))
                    else:
                        dve.wait_ge(sm.combined, upto(32 * g + 4 * (e - 1) + j + 1))
                    dve.scalar_tensor_tensor(m.acc[:, j, :], m.ps[4 + e % 2][:, P * j:P * (j + 1)], m.weight[:, g * GROUP + j, e:e + 1],
                                             m.acc[:, j, :], ALU.mult, ALU.add).then_inc(sm.combined, 1)

            with dve.Fori(0, GROUPS) as g:
                for e in range(EXPERTS):
                    split(g, e)
                    if e == 0:
                        dve.wait_ge(sm.bias_done, upto(g + 1))
                        dve.wait_ge(sm.saved, upto(16 * g))
                        dve.tensor_tensor(m.acc[:, :, :], m.ps[1].rearrange("p (j f) -> p j f", f=E), m.X[:, cols(g, GROUP), :],
                                          ALU.add).then_inc(sm.acc, 1)
                    else:
                        combine(g, e - 1)
                combine(g, EXPERTS - 1)

        @block.scalar
        def _(act):
            with act.Fori(0, GROUPS) as g:
                act.wait_ge(sm.up_done, upto(32 * g))
                act.copy(m.xt_h[:, :], m.XR[:, cols(g, 512)]).then_inc(sm.x_high, 1)
                for e in range(EXPERTS):
                    for c in range(4):
                        n = 32 * g + 4 * e + c
                        act.wait_ge(sm.up_done, upto(n + 1))
                        act.wait_ge(sm.h_split, upto(32 * g + 4 * max(e, 0)))
                        act.activation(m.h[c][:, :], m.ps[UP[c]], ACT.Gelu, bias=m.b1_cols[:, 4 * e + c:4 * e + c + 1]).then_inc(sm.gelu, 1)
                        if c % 2 == 0:
                            act.wait_ge(sm.gelu, upto(n + 1))
                            act.wait_ge(sm.down_done, upto(8 * g + max(e - 1, 0)))
                            act.copy(m.h_h[e % 2][:, c, :], m.h[c][:, :]).then_inc(sm.h_high2, 1)
                    if e == 0:
                        act.wait_ge(sm.w_turned, upto(g + 1))
                        act.copy(m.weight_t[:, :], m.ps[0][0:EXPERTS, :]).then_inc(sm.w_out, 1)

        @block.tensor
        def _(pe):
            def up(g, e):
                for c in range(4):
                    pe.wait_ge(sm.gelu, upto(32 * g + 4 * max(e - 1, 0) + c + (1 if e else 0)) if e else upto(32 * g))
                    out, cs = m.ps[UP[c]], slice(c * P, (c + 1) * P)
                    pe.matmul(out, m.W1_h[:, e, cs], m.xt_h[:, :], start=True, stop=False)
                    pe.matmul(out, m.W1_l[:, e, cs], m.xt_h[:, :], start=False, stop=False)
                    if e == 0 and c == 0:
                        pe.wait_ge(sm.x_low, upto(g + 1))
                    pe.matmul(out, m.W1_h[:, e, cs], m.xt_l[:, :], start=False, stop=True).then_inc(sm.up_done, 1)

            def down(g, e):
                bank, z = m.ps[4 + e % 2], e % 2
                pe.wait_ge(sm.h_split, upto(32 * g + 4 * e + 4))
                pe.wait_ge(sm.combined, upto(32 * g + 4 * max(e - 1, 0)))
                for j in range(GROUP):
                    out, tok = bank[:, P * j:P * (j + 1)], slice(P * j, P * (j + 1))
                    for c in range(4):
                        pe.matmul(out, m.h_h[z][:, c, tok], m.W2_h[:, e, c, :], start=(c == 0), stop=False)
                        pe.matmul(out, m.h_h[z][:, c, tok], m.W2_l[:, e, c, :], start=False, stop=False)
                        ins = pe.matmul(out, m.h_l[z][:, c, tok], m.W2_h[:, e, c, :], start=False, stop=(c == 3))
                ins.then_inc(sm.down_done, 1)

            with pe.Fori(0, GROUPS) as g:
                pe.wait_ge(sm.x_high, upto(g + 1))
                up(g, 0)
                pe.wait_ge(sm.w_staged, upto(g + 1))
                pe.wait_ge(sm.w_out, upto(g))
                for j in range(GROUP):
                    ins = pe.transpose(m.ps[0][0:EXPERTS, P * j:P * (j + 1)], m.w_stage[:, j, :], m.ident[:, :])
                ins.then_inc(sm.w_turned, 1)
                up(g, 1)
                pe.wait_ge(sm.w_out, upto(g + 1))
                pe.wait_ge(sm.acc, upto(g))
                for j in range(GROUP):
                    ins = pe.matmul(m.ps[1][:, P * j:P * (j + 1)], m.weight_t[:, P * j:P * (j + 1)], m.b2_sb[:, :], start=True, stop=True)
                ins.then_inc(sm.bias_done, 1)
                down(g, 0)
                for e in range(1, EXPERTS):
                    if e + 1 < EXPERTS:
                        up(g, e + 1)
                    down(g, e)

        @block.sync
        def _(sp):
            with sp.Fori(0, GROUPS) as g:
                sp.wait_ge(sm.combined, upto(32 * g + 32))
                hold(sp, m)
                sp.dma_start(m.out_tiles[:, cols(g, GROUP), :], m.acc[:, :, :]).then_inc(sm.saved, 16)
            sp.wait_ge(sm.saved, upto(16 * GROUPS))


def build(nc, ins, out):
    m = Names(dict(ins))
    m.credited, m.reused = [], []
    with ExitStack() as ctx:
        m.scope = ctx

        def sb(name, shape, dt=F32):
            return ctx.enter_context(nc.sbuf_tensor(name, shape, dt))

        def sems(name, *names, **lists):
            table = {}
            for n in names:
                table[n] = m.scope.enter_context(nc.semaphore(f"{name}_{n}"))
            for n, k in lists.items():
                table[n] = [m.scope.enter_context(nc.semaphore(f"{name}_{n}{i}")) for i in range(k)]
            for s in table.values():
                m.reused.extend(s if isinstance(s, list) else [s])
            return Names(table)

        def counted(name, *names, **lists):
            ns = sems(name, *names, **lists)
            for s in ns.table.values():
                m.credited.extend(s if isinstance(s, list) else [s])
            return ns

        m.table.update(sems("io", "x_loaded", "ctx_loaded", "gates_loaded", "scales_loaded", "tanh_ready",
                               "const_step", "stored", "ffn0_loaded", "clips_loaded",
                               "proj_loaded", "proj_bias_loaded", "pos_loaded", "moe_loaded", "moe_small_loaded",
                               "mo_split", "b1_turned", "held").table)
        m.stat_sems = [sems(f"stats{k}", "dve", "variance") for k in range(4)]
        m.wide = [ctx.enter_context(nc.psum_tensor(f"banks{k}", [P, 1024], F32)) for k in range(3)]
        m.ps6, m.ps7 = (ctx.enter_context(nc.psum_tensor(f"bank{k}", [P, 512], F32)) for k in (6, 7))
        m.ps = [m.wide[k // 2][:, 512 * (k % 2):512 * (k % 2 + 1)] for k in range(6)] + [m.ps6[:, :], m.ps7[:, :]]

        m.X = sb("X", [P, TILES, E])
        m.C = sb("C", [P, TILES, E])
        m.CT = sb("CT", [P, TILES * P])
        m.XT = sb("XT", [P, TILES * P])
        m.ident = sb("ident", [P, P])
        m.ident_bf = sb("ident_bf", [P, P], BF16)
        m.ones = sb("ones", [P, P])
        m.minus_half = sb("minus_half", [P, TILES])
        m.tanh_g = sb("tanh_g", [P, 4])
        m.row_stats = sb("row_stats", [P, TILES, 6])
        m.row_mean = sb("row_mean", [P, TILES])
        m.row_rstd = sb("row_rstd", [P, TILES])
        m.row_tmp = sb("row_tmp", [P, TILES])
        m.head_mask = sb("head_mask", [P, NH0])
        m.cumsum_mat = sb("cumsum_mat", [P, P])

        m.causal_add = sb("causal_add", [P, S])

        m.magic = sb("magic", [P, 1])
        m.clips = sb("clips", [1, 2])
        m.gu_raw_t = sb("gu_raw", [P, 6, E])
        m.proj_raw = sb("proj_raw", [P, 4, E])
        m.proj_bias = sb("proj_bias", [P, 2])
        m.bv_rows, m.bo_rows = sb("bv_rows", [P, E]), sb("bo_rows", [P, E])
        m.pos_k_raw = sb("pos_k_raw", [S, S, DH1])
        m.pos_v = sb("pos_v", [P, S, 2 * DH1])
        m.v_block = sb("v_block", [P, NH1 // 2, 2, 2, DH1 + 1])
        m.Wr_sb, m.br_rows = sb("Wr_sb", [P, EXPERTS]), sb("br_rows", [P, EXPERTS])
        m.b2_sb, m.b1_cols = sb("b2_sb", [EXPERTS, E]), sb("b1_cols", [P, 4 * EXPERTS])
        m.b1_raw = sb("b1_raw", [4 * EXPERTS, P])
        m.out_tiles = out.rearrange("(i c) s f -> (c s) i f", c=2)
        m.dn_raw_t = sb("dn_raw", [P, 1, 352])
        m.gu_raw, m.dn_raw = m.gu_raw_t[:, :, :], m.dn_raw_t[:, :, :]

        with ExitStack() as l0:
            m.scope = l0
            m.gs = counted("gates", "ctx_turned", "ctx_staged", "xt_out", "ct_out", "stored", "x_turned", "normed",
                           "gates_done", "gates_out")
            m.gw = sems("gates_w", "turned", "ready")
            m.gm = sems("gmath", "act", "dve", "dve2", "log1p", "neg", "logf", "summed", "g", "g_turned", "gmax",
                        "gmax_turned", "saved")
            m.rows = sems("att0_g", rows=2).rows
            m.at = counted("att0", diff=2, qk=2, spread=2, av=2, v=2, causal=2, c=2, exp=2, k=2, out=2)
            m.af = sems("fin0", "dve", "centered", "squared", "var", "rstd")
            start_counts(nc, m)
            def sl(name, shape, dt=F32):
                return l0.enter_context(nc.sbuf_tensor(name, shape, dt))
            m.gate_rows = sl("gate_rows", [16, 3 * E])
            m.gate_bias = sl("gate_bias", [P, 16])
            m.gate_w = sl("gate_w", [P, 3, 16])
            m.out_w_rows = sl("out_w_rows", [P, E])
            m.stage_x = sl("stage_x", [P, GROUP, E])
            m.stage_c = sl("stage_c", [P, GROUP, E])
            m.stage_xt = sl("stage_xt", [P, 512])
            m.stage_ct = sl("stage_ct", [P, 512])
            m.gates = sl("gates", [P, TILES, 16])
            m.softp = sl("softp", [P, TILES, NH0])
            m.logf = sl("logf", [P, TILES, NH0])
            m.exp_neg_max = sl("exp_neg_max", [P, TILES, NH0])
            m.g_nat = sl("g_nat", [P, TILES, NH0])
            m.cumsum = sl("cumsum", [P, TILES * NH0])
            m.g_t = sl("g_t", [P, 2, P])
            m.gmax_t = sl("gmax_t", [P, 2, P])
            m.g_rows = [sl(f"g_rows{j}", [P, NH0 * S]) for j in range(2)]
            m.decay = [sl(f"decay{j}", [P, NH0, S]) for j in range(2)]
            m.c_t = [sl(f"c_t{j}", [P, NH0, S]) for j in range(2)]
            m.q_spread = [sl(f"q_spread{j}", [P, NH0, P]) for j in range(2)]
            m.k_stage = [sl(f"k_stage{j}", [P, P]) for j in range(2)]
            m.v_ones = [sl(f"v_ones{j}", [P, NH0, DH0 + 1]) for j in range(2)]
            m.num = sl("num", [P, TILES, NH0 * (DH0 + 1)])
            m.den = sl("den", [P, TILES * NH0])
            m.hmean = sl("hmean", [P, TILES * NH0])
            m.hvar = sl("hvar", [P, TILES * NH0])
            m.hid = sl("hid", [P, TILES * NH0, DH0])
            m.hsq = sl("hsq", [P, TILES * NH0, DH0])
            m.gmax_dram = nc.dram_tensor("gmax_dram", (2, TILES, NH0, S), F32, kind="Internal").ap()
            load_and_constants(nc, m)
            l0_gates(nc, m)
            l0_gate_math(nc, m)
            l0_attention(nc, m)
            l0_attention_finish(nc, m)

        with ExitStack() as f0:
            m.scope = f0
            m.fw = sems("ffn0_w", "dve", "quantized", "turned")
            m.fn = counted("ffn0_norm", "normed")
            scale_sems = [sems(f"scale{k}", "exp", "dve", "col", "row", "pair", "spread") for k in range(2)]
            m.fu = counted("ffn0_up", "scaled", "shifted", "clipped", "turned", "quantized", "upped", "stood", "silu", "hidden")
            m.fd = counted("ffn0_down", "shifted", "clipped", "downed", "quantized", "out", "added")
            m.fd.dve = sems("ffn0_down", "dve").dve
            start_counts(nc, m)
            def sl(name, shape, dt=F32):
                return f0.enter_context(nc.sbuf_tensor(name, shape, dt))
            m.XN = m.XT[:, :].rearrange("p (i f) -> p i f", f=E)
            gu_q, dn_q = sl("gu_q", [P, 6, E], BF16), sl("dn_q", [P, 1, 352], BF16)
            m.gu_q, m.dn_q = gu_q[:, :, :], dn_q[:, :, :]
            m.gu_top, m.gu_scale = sl("gu_top", [P, 6]), sl("gu_scale", [P, 6])
            m.dn_top, m.dn_scale = sl("dn_top", [P, 1]), sl("dn_scale", [P, 1])
            m.dn_diag = sl("dn_diag", [P, P])
            m.dn_row = sl("dn_row", [P, E])
            m.gu_t = sl("gu_t", [P, 6, P], BF16)
            m.dn_t = sl("dn_t", [P, 3, E], BF16)
            m.x_top = sl("x_top", [P, GROUPS])
            m.h_top = sl("h_top", [P, 3, GROUPS])
            m.clip_exp = sl("clip_exp", [1, 1])
            m.top_col = sl("top_col", [P, 1])
            m.top_one = sl("top_one", [1, 2])
            m.top_pair = sl("top_pair", [1, 2])
            m.x_scale, m.h_scale = sl("x_scale", [P, 2]), sl("h_scale", [P, 2])
            m.round_x, m.xq, m.xq_t = sl("round_x", [P, 512]), sl("xq", [P, 512], BF16), sl("xq_t", [P, 512], BF16)
            m.silu = [sl(f"silu{k}", [P, 512]) for k in range(3)]
            m.HT = sl("HT", [P, 3, TILES * P])
            m.round_h, m.hq = sl("round_h", [P, 3, 512]), sl("hq", [P, 3, 512], BF16)
            m.down = sl("down", [P, GROUP, E])
            finish_stats(nc, m, m.stat_sems[1])
            l0_ffn_weights(nc, m)
            l0_ffn_norm(nc, m)
            activation_scale(nc, m, scale_sems[0], m.x_top[:, :], m.clips[0:1, 0:1], m.x_scale)
            l0_ffn_up(nc, m)
            activation_scale(nc, m, scale_sems[1], m.h_top[:, :, :].rearrange("p k g -> p (k g)"), m.clips[0:1, 1:2], m.h_scale)
            l0_ffn_down(nc, m)

        with ExitStack() as l1:
            m.scope = l1
            m.lw = sems("l1_w", "dve", "turned", "stood", "moved")
            m.pj = counted("l1_proj", "turned", "normed", "xt_out", "q_done", "k_done", "exact_out", "rest", "middle", "low",
                           parts_saved=2)
            m.rl = counted("l1_rel", "done", loaded=2, saved=2, out=4)
            m.a1 = counted("l1_att", "added", "masked", "pv_out", "pv_saved", "pv_back", "summed", "v_done", "ct_staged",
                           "scored", "av_done", "v_out", "exped", "maxed", "shifted", "av_out", "small",
                           "att_turned", "att_done", "wo_done", "p_turned", "pv_done", "pt_out", "att_out")
            m.rel_sem = sems("l1_rel_in", slot=4).slot
            m.a1.table.update(sems("l1_att", "mask_in", qk_in=2).table)
            start_counts(nc, m)
            def sl(name, shape, dt=F32):
                return l1.enter_context(nc.sbuf_tensor(name, shape, dt))
            m.proj_t = sl("proj_t", [P, 4, E])
            m.stage_x, m.stage_xt = sl("stage_x1", [P, GROUP, E]), sl("stage_xt1", [P, 512])
            m.qk_dram = [nc.dram_tensor(f"{w}_dram", (GROUPS, NH1, 3, DH1, 512), BF16, kind="Internal").ap() for w in "qk"]
            m.pos_dram = nc.dram_tensor("pos_dram", (P, 3, 4 * S), BF16, kind="Internal").ap()
            m.rel_dram = nc.dram_tensor("rel_dram", (GROUPS, NH1, 8, S, S), F32, kind="Internal").ap()
            m.pv_dram = nc.dram_tensor("pv_dram", (GROUPS, S, S, 2 * DH1), F32, kind="Internal").ap()
            finish_stats(nc, m, m.stat_sems[2])
            with ExitStack() as part:
                def sl(name, shape, dt=F32):
                    return part.enter_context(nc.sbuf_tensor(name, shape, dt))
                m.pos_parts, m.pos_exact = sl("pos_parts", [P, 3, 4 * S], BF16), sl("pos_exact", [P, 4 * S])
                m.pos_right = sl("pos_right", [STACK, 16, 4 * S], BF16)
                m.qk_exact, m.qk_parts = sl("qk_exact", [P, 2, 512]), sl("qk_parts", [P, 2, 3, 512], BF16)
                m.q_left = [sl(f"q_left{k}", [STACK, NH1, 512], BF16) for k in range(2)]
                m.rel = [sl(f"rel{k}", [P, 2048]) for k in range(2)]
                l1_weights(nc, m)
                l1_project(nc, m)
                l1_relative(nc, m)
            with ExitStack() as part:
                def sl(name, shape, dt=F32):
                    return part.enter_context(nc.sbuf_tensor(name, shape, dt))
                m.rel_in = [sl(f"rel_in{k}", [P, NH1, S]) for k in range(4)]
                m.mask_in, m.mask_add = sl("mask_in", [P, TILES, S], I32), sl("mask_add", [P, TILES, S])
                m.ct_twice = sl("ct_twice", [P, 2, 2, S])
                m.q_left = [sl(f"q_left_tiles{k}", [STACK, NH1, 256], BF16) for k in range(2)]
                m.k_right = [sl(f"k_right{k}", [STACK, NH1, 256], BF16) for k in range(2)]
                m.soft = [sl(f"soft{k}", [P, NH1, S]) for k in range(2)]
                m.expd = [sl(f"expd{k}", [P, NH1, S]) for k in range(2)]
                m.row_max = sl("row_max", [P, NH1])
                m.p_t = m.C[:, :, :].rearrange("p i f -> p (i f)").rearrange("p (i k) -> p i k", k=1024)
                m.av = sl("av", [P, TILES, NH1 * (DH1 + 1)])
                m.pv, m.pv_in = sl("pv", [S, 1024]), sl("pv_in", [P, 32, 2 * DH1])
                m.row_sum = sl("row_sum", [P, GROUP * NH1])
                m.att, m.att_t, m.res = sl("att", [P, GROUP, E]), sl("att_t", [P, 512]), sl("res", [P, GROUP, E])
                load_mask(nc, m)
                l1_attention(nc, m)

        with ExitStack() as f1:
            m.scope = f1
            m.ro = counted("route", turned=2, normed=2, xt_out=2, logits=2, taken=2)
            m.rt = sems("route1", "dve", "shifted", "exp")
            m.mo = counted("moe", "up_done", "w_staged", "x_high", "x_low", "w_turned", "w_out", "bias_done", "saved", "acc",
                           "gelu", "down_done", "h_high", "h_high2", "h_split", "combined")
            start_counts(nc, m)
            def sl(name, shape, dt=F32):
                return f1.enter_context(nc.sbuf_tensor(name, shape, dt))
            m.W1_sb = m.CT[:, :].rearrange("p (e h) -> p e h", e=EXPERTS)
            m.W2_sb = m.XT[:, :].rearrange("p (e c d) -> p e c d", e=EXPERTS, c=4)
            m.W1_h, m.W1_l = (sl(f"W1_{k}", [P, EXPERTS, HID], F32R)[:, :, :] for k in "hl")
            m.W2_h, m.W2_l = (sl(f"W2_{k}", [P, EXPERTS, 4, E], F32R)[:, :, :, :] for k in "hl")
            m.XR = m.C[:, :, :].rearrange("p i f -> p (i f)")
            m.stage_x = [sl(f"stage_x2{k}", [P, GROUP, E]) for k in range(2)]
            m.stage_xt = [sl(f"stage_xt2{k}", [P, 512]) for k in range(2)]
            m.xt_h, m.xt_l = sl("xt_h", [P, 512], F32R), sl("xt_l", [P, 512], F32R)
            m.h = [sl(f"h{k}", [P, 512]) for k in range(4)]
            m.h_h = [sl(f"h_h{k}", [P, 4, 512], F32R) for k in range(2)]
            m.h_l = [sl(f"h_l{k}", [P, 4, 512], F32R) for k in range(2)]
            m.logit, m.best, m.chosen, m.weight = (sl(k, [P, TILES, EXPERTS]) for k in ("logit", "best", "chosen", "weight"))
            m.wsum, m.weight_t, m.w_stage = sl("wsum", [P, TILES]), sl("weight_t", [EXPERTS, 512]), sl("w_stage", [P, GROUP, EXPERTS])
            m.acc = sl("acc", [P, GROUP, E])
            with nc.Block() as block:

                @block.sync
                def _(sp):
                    sp.dma_start(m.W1_sb, m.W1.rearrange("e d h -> d e h")).then_inc(m.moe_loaded, 16)
                    for e0 in (0, 4):
                        sp.dma_start(m.W2_sb[:, e0:e0 + 4], m.W2[e0:e0 + 4].rearrange("e (c p) d -> p e c d", p=P)).then_inc(m.moe_loaded, 16)
            finish_stats(nc, m, m.stat_sems[3])
            expert_weights(nc, m)
            router(nc, m)
            experts(nc, m)


_INS = {'x': 'x', 'ctx_1024': 'ctx', 'mask_BxSxS2_ik0': 'mask', 'g_xattn': 'g_xattn', 'g_ffn': 'g_ffn',
        'L0_xattn_igate_w': 'igate_w', 'L0_xattn_igate_b': 'igate_b', 'L0_xattn_fgate_w': 'fgate_w',
        'L0_xattn_fgate_b': 'fgate_b', 'L0_xattn_out_w': 'out_w', 'L0_ffn_clip_x': 'clip_x',
        'L0_ffn_clip_down': 'clip_down', 'L0_ffn_w_gate': 'w_gate', 'L0_ffn_w_up': 'w_up', 'L0_ffn_w_down': 'w_down',
        'L1_xattn_pos_k': 'pos_k', 'L1_xattn_pos_v': 'pos_v_in', 'L1_xattn_Wq': 'Wq', 'L1_xattn_bq': 'bq',
        'L1_xattn_Wk': 'Wk', 'L1_xattn_bk': 'bk', 'L1_xattn_Wv': 'Wv', 'L1_xattn_bv': 'bv', 'L1_xattn_Wo': 'Wo',
        'L1_xattn_bo': 'bo', 'L1_ffn_W1': 'W1', 'L1_ffn_b1': 'b1', 'L1_ffn_W2': 'W2', 'L1_ffn_b2': 'b2',
        'L1_ffn_Wr': 'Wr', 'L1_ffn_br': 'br'}


def kernel(**inputs):
    import numpy as _np
    import concourse.bacc as _bacc
    from concourse import mybir as _mybir
    from concourse.bass_utils import run_bass_kernel_spmd as _run

    nc = _bacc.Bacc("TRN2", target_bir_lowering=False, num_devices=1)
    arrays, args = {}, {}
    for name, short in _INS.items():
        a = _np.ascontiguousarray(inputs[name])
        arrays[f"in_{name}_dram"] = a
        args[short] = nc.dram_tensor(f"in_{name}_dram", a.shape, _mybir.dt.from_np(a.dtype), kind="ExternalInput").ap()
    out = nc.dram_tensor("out_0_dram", (B, S, E), _mybir.dt.float32, kind="ExternalOutput").ap()
    build(nc, args, out)
    r = _run(nc, [arrays], core_ids=[0])
    return r.results[0]["out_0_dram"]
```

```python
from contextlib import ExitStack

import concourse.bass as bass
from concourse import mybir

P = 128
B, S, E = 64, 64, 128
TILES = B * S // P
GROUP = 4
GROUPS = TILES // GROUP
NH0, DH0 = 8, 16
LN_EPS = 1e-5
NORM_EPS = 1e-6
QMAX = 127.0
MAGIC = 1.5 * 2 ** 23
NH1, DH1 = 16, 8
EXPERTS, HID = 8, 512
CHUNKS = (128, 128, 96)
FAR = -1e30

F32 = mybir.dt.float32
F32R = mybir.dt.float32r
BF16 = mybir.dt.bfloat16
I32 = mybir.dt.int32
ALU = mybir.AluOpType
ACT = mybir.ActivationFunctionType
AX = mybir.AxisListType.X


class Names:

    def __init__(self, table):
        self.table = table

    def __getattr__(self, name):
        return self.table[name]


def cols(i, n):
    return bass.ds(i * n, n)


def upto(n):
    return n + 1


class Chain:

    def __init__(self, eng, sem):
        self.eng, self.sem, self.n = eng, sem, 0

    def link(self, ins):
        self.n += 1
        ins.then_inc(self.sem, 1)
        self.eng.wait_ge(self.sem, self.n)


def hold(eng, m):
    eng.sem_inc(m.held, 1)


def groups(eng, body):
    body(0, first=True, last=False)
    with eng.Fori(1, GROUPS - 1) as g:
        body(g, first=False, last=False)
    body(GROUPS - 1, first=False, last=True)


def paired_groups(eng, body):
    body(0, 0, True, False, False)
    body(1, 1, False, True, False)
    with eng.Fori(1, GROUPS // 2 - 1) as pair:
        for u in range(2):
            body(2 * pair + u, u, False, False, False)
    body(GROUPS - 2, 0, False, False, False)
    body(GROUPS - 1, 1, False, False, True)


def start_counts(block, m):
    reused, credited = m.reused, m.credited
    m.reused, m.credited = [], []

    @block.sync
    def _(sp):
        for sem in reused:
            sp.sem_clear(sem)
        for sem in credited:
            sp.sem_inc(sem, 1)


def load_and_constants(nc, m):
    with nc.Block() as block:

        @block.sync
        def _(sp):
            sp.dma_start(m.X[:, :, :], m.x.rearrange("(i c) s f -> (c s) i f", c=2)).then_inc(m.x_loaded, 16)
            sp.dma_start(m.C[:, :, :], m.ctx.rearrange("(i c) s f -> (c s) i f", c=2)).then_inc(m.ctx_loaded, 16)

        @block.scalar
        def _(act):
            act.dma_start(m.gate_rows[0:NH0, :], m.igate_w).then_inc(m.gates_loaded, 16)
            act.dma_start(m.gate_rows[NH0:2 * NH0, :], m.fgate_w).then_inc(m.gates_loaded, 16)
            act.dma_start(m.gate_bias[0:NH0, :], m.igate_b.unsqueeze(1)).then_inc(m.gates_loaded, 16)
            act.dma_start(m.gate_bias[NH0:2 * NH0, :], m.fgate_b.unsqueeze(1)).then_inc(m.gates_loaded, 16)
            act.dma_start(m.out_w_rows[:, :], m.out_w.partition_broadcast(P)).then_inc(m.scales_loaded, 16)
            act.dma_start(m.tanh_g[:, 0:2], m.g_xattn.partition_broadcast(P)).then_inc(m.scales_loaded, 16)
            act.dma_start(m.tanh_g[:, 2:4], m.g_ffn.partition_broadcast(P)).then_inc(m.scales_loaded, 16)
            for k, w in enumerate((m.w_gate, m.w_up)):
                act.dma_start(m.gu_raw[:, 3 * k:3 * k + 2, :], w[0:2 * P].rearrange("(c p) f -> p c f", p=P)).then_inc(m.ffn0_loaded, 16)
                act.dma_start(m.gu_raw[0:96, 3 * k + 2, :], w[2 * P:]).then_inc(m.ffn0_loaded, 16)
            act.dma_start(m.dn_raw[:, 0, :], m.w_down).then_inc(m.ffn0_loaded, 16)
            act.dma_start(m.clips[:, 0:1], m.clip_x.unsqueeze(0)).then_inc(m.clips_loaded, 16)
            act.dma_start(m.clips[:, 1:2], m.clip_down.unsqueeze(0)).then_inc(m.clips_loaded, 16)
            for k, w in enumerate((m.Wq, m.Wk, m.Wv, m.Wo)):
                act.dma_start(m.proj_raw[:, k, :], w).then_inc(m.proj_loaded, 16)
            act.dma_start(m.proj_bias[:, 0:1], m.bq.unsqueeze(1)).then_inc(m.proj_bias_loaded, 16)
            act.dma_start(m.proj_bias[:, 1:2], m.bk.unsqueeze(1)).then_inc(m.proj_bias_loaded, 16)
            act.dma_start(m.bv_rows[:, :], m.bv.partition_broadcast(P)).then_inc(m.proj_bias_loaded, 16)
            act.dma_start(m.bo_rows[:, :], m.bo.partition_broadcast(P)).then_inc(m.proj_bias_loaded, 16)
            act.dma_start(m.pos_k_raw[:, :, :], m.pos_k.rearrange("t s d -> s t d")).then_inc(m.pos_loaded, 16)
            act.wait_ge(m.const_step, 4)
            for p in range(2):
                act.dma_start(m.pos_v[p * S:(p + 1) * S, :, p * DH1:(p + 1) * DH1], m.pos_v_in.rearrange("t s d -> s t d")).then_inc(m.pos_loaded, 16)
            act.dma_start(m.Wr_sb[:, :], m.Wr).then_inc(m.moe_small_loaded, 16)
            act.dma_start(m.br_rows[:, :], m.br.partition_broadcast(P)).then_inc(m.moe_small_loaded, 16)
            act.dma_start(m.b2_sb[:, :], m.b2).then_inc(m.moe_small_loaded, 16)
            act.dma_start(m.b1_raw[:, :], m.b1.rearrange("e (c p) -> (e c) p", p=P)).then_inc(m.moe_small_loaded, 16)
            act.wait_ge(m.scales_loaded, 48)
            act.activation(m.tanh_g[:, :], m.tanh_g[:, :], ACT.Tanh).then_inc(m.tanh_ready, 1)

        @block.vector
        def _(dve):
            dve.wait_ge(m.x_loaded, 16)
            all_stats(dve, m)

        @block.gpsimd
        def _(pool):
            step = Chain(pool, m.const_step)
            step.link(pool.memset(m.pos_v[:, :, :], 0.0))
            step.link(pool.memset(m.v_block[:, :, :, :, :], 0.0))
            for p in range(2):
                step.link(pool.memset(m.v_block[p * S:(p + 1) * S, :, :, p, DH1:DH1 + 1], 1.0))
            for mask, width in ((m.strip_mask, 32), (m.inner_mask, DH1)):
                for lo in range(0, P, P if width == 32 else 32):
                    rows = mask[lo:lo + (P if width == 32 else 32), :]
                    step.link(pool.memset(rows, 1.0))
                    step.link(pool.affine_select(out=rows, in_=rows, compare_op=ALU.is_ge, fill=0.0, base=0,
                                                 pattern=[[-width, 4]], channel_multiplier=1))
                    step.link(pool.affine_select(out=rows, in_=rows, compare_op=ALU.is_ge, fill=0.0, base=width - 1,
                                                 pattern=[[width, 4]], channel_multiplier=-1))
            step.link(pool.memset(m.ident[:, :], 0.0))
            step.link(pool.affine_select(out=m.ident[:, :], in_=m.ident[:, :], compare_op=ALU.not_equal, fill=1.0,
                                         base=0, pattern=[[-1, P]], channel_multiplier=1))
            step.link(pool.tensor_copy(m.ident_bf[:, :], m.ident[:, :]))
            step.link(pool.memset(m.ones[:, :], 1.0))
            step.link(pool.affine_select(out=m.cumsum_mat[:, :], in_=m.ones[:, :], compare_op=ALU.is_ge, fill=0.0,
                                         base=0, pattern=[[1, P]], channel_multiplier=-1))
            step.link(pool.memset(m.cumsum_mat[0:S, S:P], 0.0))
            step.link(pool.affine_select(out=m.head_mask[:, :], in_=m.ones[:, 0:NH0], compare_op=ALU.is_ge, fill=0.0,
                                         base=0, pattern=[[-DH0, NH0]], channel_multiplier=1))
            step.link(pool.affine_select(out=m.head_mask[:, :], in_=m.head_mask[:, :], compare_op=ALU.is_ge, fill=0.0,
                                         base=DH0 - 1, pattern=[[DH0, NH0]], channel_multiplier=-1))
            step.link(pool.memset(m.causal_add[:, :], 0.0))
            for c in range(2):
                half = m.causal_add[c * S:(c + 1) * S, :]
                step.link(pool.affine_select(out=half, in_=half, compare_op=ALU.is_ge, fill=FAR, base=0,
                                             pattern=[[1, S]], channel_multiplier=-1))
            for j in range(2):
                step.link(pool.memset(m.v_ones[j][:, :, :, :], 0.0))
                for c in range(2):
                    step.link(pool.memset(m.v_ones[j][c * S:(c + 1) * S, :, c, DH0:DH0 + 1], 1.0))
            for k in (2, 5):
                step.link(pool.memset(m.gu_raw[96:P, k, :], 1.0))
            step.link(pool.memset(m.magic[:, :], MAGIC))


def stats_of(eng, m, tile):
    return eng.bn_stats(m.row_stats[:, tile, :], m.X[:, tile, :])


def all_stats(dve, m):
    with dve.Fori(0, GROUPS // 2) as pair:
        for j in range(2 * GROUP):
            stats_of(dve, m, pair * 2 * GROUP + j)


def inverse_root(dve, step, var, root, tmp):
    step.link(dve.reciprocal(root, root))
    step.link(dve.tensor_tensor(tmp, root, root, ALU.mult))
    step.link(dve.tensor_tensor(tmp, tmp, var, ALU.mult))
    step.link(dve.tensor_scalar(tmp, tmp, -0.5, 1.5, ALU.mult, ALU.add))
    step.link(dve.tensor_tensor(root, root, tmp, ALU.mult))


def finish_stats(nc, m, sm):
    stats = m.row_stats
    with nc.Block() as block:
        start_counts(block, m)

        @block.vector
        def _(dve):
            step = Chain(dve, sm.dve)
            step.link(dve.tensor_tensor(m.row_mean[:, :], stats[:, :, 1], stats[:, :, 4], ALU.add))
            step.link(dve.tensor_scalar(m.row_mean[:, :], m.row_mean[:, :], 0.5, None, ALU.mult))
            step.link(dve.tensor_tensor(m.row_tmp[:, :], stats[:, :, 1], stats[:, :, 4], ALU.subtract))
            step.link(dve.scalar_tensor_tensor(m.row_tmp[:, :], m.row_tmp[:, :], 0.25, m.row_tmp[:, :], ALU.mult, ALU.mult))
            step.link(dve.tensor_tensor(m.row_rstd[:, :], stats[:, :, 2], stats[:, :, 5], ALU.add))
            step.link(dve.scalar_tensor_tensor(m.row_tmp[:, :], m.row_rstd[:, :], 1.0 / E, m.row_tmp[:, :], ALU.mult, ALU.add))
            step.link(dve.tensor_scalar(m.row_tmp[:, :], m.row_tmp[:, :], LN_EPS, None, ALU.add))
            dve.sem_inc(sm.variance, 1)
            dve.wait_ge(sm.root, 1)
            inverse_root(dve, step, m.row_tmp[:, :], m.row_rstd[:, :], m.row_tmp2[:, :])

        @block.scalar
        def _(act):
            act.wait_ge(sm.variance, 1)
            act.activation(m.row_rstd[:, :], m.row_tmp[:, :], ACT.Sqrt).then_inc(sm.root, 1)


def normalize(eng, m, out, tile):
    return eng.tensor_scalar(out, m.X[:, tile, :], m.row_mean[:, cols(tile, 1)], m.row_rstd[:, cols(tile, 1)],
                             ALU.subtract, ALU.mult)


def l0_gates(nc, m):
    sm = m.gs
    finish_stats(nc, m, m.stat_sems[0])

    with nc.Block() as block:

        @block.sync
        def _(sp):
            def load(g, z):
                sp.dma_start(m.stage_c[z][:, :, :], m.ctx_tiles[:, cols(g, GROUP), :]).then_inc(sm.ctx_in[z], 16)

            def store(pair, z):
                g = 2 * pair + z
                for src, dst, out in ((m.stage_xt[z], m.XT, sm.xt_out), (m.stage_ct[z], m.CT, sm.ct_out)):
                    sp.wait_ge(out, upto(g + 1))
                    hold(sp, m)
                    sp.dma_start(dst[:, cols(g, 512)], src[:, :]).then_inc(sm.stored[z], 16)

            load(0, 0)
            load(1, 1)
            with sp.Fori(0, GROUPS // 2 - 1) as pair:
                for z in range(2):
                    store(pair, z)
                    load(2 * pair + z + 2, z)
            for z in range(2):
                store(GROUPS // 2 - 1, z)
            for z in range(2):
                sp.wait_ge(sm.stored[z], upto(16 * GROUPS))

        @block.vector
        def _(dve):
            dve.wait_ge(m.gates_loaded, 64)
            dve.wait_ge(m.gw.turned, 3)
            for k in range(2):
                dve.tensor_copy(m.gate_w[:, k, :], m.ps[0][:, 16 * k:16 * k + 16]).then_inc(m.gw.ready, 1)
            dve.wait_ge(m.gw.ready, 2)
            dve.tensor_tensor(m.gate_w[:, 1, :], m.gate_w[:, 1, :], m.ps[0][:, 32:48], ALU.add).then_inc(m.gw.ready, 1)

            def norm(g, z):
                dve.wait_ge(sm.x_turned, upto(g - 1))
                for j in range(GROUP):
                    normalize(dve, m, m.stage_x[z][:, j, :], g * GROUP + j).then_inc(sm.normed, 1)

            def add_bias(g, z):
                dve.wait_ge(sm.gates_done, upto(g + 1))
                if not isinstance(g, int) or g >= 2:
                    dve.wait_ge(sm.gates_turned, upto(g - 1))
                dve.tensor_scalar(m.gates_t[z][:, :], m.ps[5 + z][0:2 * NH0, :], m.gate_bias[:, 0:1], None, ALU.add).then_inc(sm.biased, 1)

            def take(g, z):
                dve.wait_ge(sm.gates_turned, upto(g + 1))
                dve.tensor_copy(m.gates[:, cols(g, GROUP), :],
                                m.ps[7][:, 64 * z:64 * z + 64].rearrange("p (j n) -> p j n", j=GROUP)).then_inc(sm.gates_out, 1)

            for z in range(2):
                for j in range(GROUP):
                    normalize(dve, m, m.stage_x[z][:, j, :], z * GROUP + j).then_inc(sm.normed, 1)
            norm(2, 0)
            add_bias(0, 0)
            norm(3, 1)
            add_bias(1, 1)
            take(0, 0)
            with dve.Fori(1, GROUPS // 2 - 1) as pair:
                for z in range(2):
                    norm(2 * pair + z + 2, z)
                    add_bias(2 * pair + z, z)
                    take(2 * pair + z - 1, 1 - z)
            for z in range(2):
                add_bias(GROUPS - 2 + z, z)
                take(GROUPS - 3 + z, 1 - z)
            take(GROUPS - 1, 1)

        @block.tensor
        def _(pe):
            pe.wait_ge(m.gates_loaded, 64)
            for k in range(3):
                pe.transpose(m.ps[0][:, 16 * k:16 * k + 16], m.gate_rows[0:16, k * P:(k + 1) * P],
                             m.ident[0:16, 0:16]).then_inc(m.gw.turned, 1)
            pe.wait_ge(m.gw.ready, 3)

            def turn(pair, z, first=False):
                g = 2 * pair + z
                pe.wait_ge(sm.normed, upto(g * GROUP + GROUP))
                if not first:
                    pe.wait_ge(sm.xt_out, upto(g - 1))
                    pe.wait_ge(sm.ct_out, upto(g - 1))
                for j in range(GROUP):
                    ins = pe.transpose(m.ps[1 + z][:, j * P:(j + 1) * P], m.stage_x[z][:, j, :], m.ident[:, :])
                ins.then_inc(sm.x_turned, 1)
                pe.wait_ge(sm.ctx_in[z], upto(16 * pair + 16))
                for j in range(GROUP):
                    ins = pe.transpose(m.ps[3 + z][:, j * P:(j + 1) * P], m.stage_c[z][:, j, :], m.ident[:, :])
                ins.then_inc(sm.ctx_turned, 1)

            def gates(pair, z):
                g = 2 * pair + z
                pe.wait_ge(sm.xt_out, upto(g + 1))
                pe.wait_ge(sm.ct_out, upto(g + 1))
                if not isinstance(g, int) or g >= 2:
                    pe.wait_ge(sm.biased, upto(g - 1))
                out = m.ps[5 + z][0:2 * NH0, :]
                pe.matmul(out, m.gate_w[:, 0, :], m.stage_xt[z][:, :], start=True, stop=False)
                pe.matmul(out, m.gate_w[:, 1, :], m.stage_ct[z][:, :], start=False, stop=True).then_inc(sm.gates_done, 1)

            def turn_gates(pair, z):
                g = 2 * pair + z
                pe.wait_ge(sm.biased, upto(g + 1))
                pe.wait_ge(sm.gates_out, upto(g))
                hold(pe, m)
                for j in range(GROUP):
                    ins = pe.transpose(m.ps[7][:, 64 * z + 16 * j:64 * z + 16 * (j + 1)], m.gates_t[z][:, j * P:(j + 1) * P],
                                       m.ident[0:2 * NH0, 0:2 * NH0])
                ins.then_inc(sm.gates_turned, 1)

            turn(0, 0, True)
            turn(0, 1)
            gates(0, 0)
            turn(1, 0)
            gates(0, 1)
            turn_gates(0, 0)
            with pe.Fori(1, GROUPS // 2 - 1) as pair:
                turn(pair, 1)
                gates(pair, 0)
                turn_gates(pair - 1, 1)
                turn(pair + 1, 0)
                gates(pair, 1)
                turn_gates(pair, 0)
            last = GROUPS // 2 - 1
            turn(last, 1)
            gates(last, 0)
            turn_gates(last - 1, 1)
            gates(last, 1)
            turn_gates(last, 0)
            turn_gates(last, 1)

        @block.scalar
        def _(act):
            def body(pair, first):
                for z in range(2):
                    g = 2 * pair + z
                    act.wait_ge(sm.x_turned, upto(g + 1))
                    if not first:
                        act.wait_ge(sm.gates_done, upto(g - 1))
                        act.wait_ge(sm.stored[z], upto(32 * pair))
                    act.copy(m.stage_xt[z][:, :], m.ps[1 + z][:, :]).then_inc(sm.xt_out, 1)
                    act.wait_ge(sm.ctx_turned, upto(g + 1))
                    act.copy(m.stage_ct[z][:, :], m.ps[3 + z][:, :]).then_inc(sm.ct_out, 1)

            body(0, True)
            with act.Fori(1, GROUPS // 2) as pair:
                body(pair, False)


def l0_gate_math(nc, m):
    sm = m.gm
    ig, fg = m.gates[:, :, 0:NH0], m.gates[:, :, NH0:2 * NH0]
    flat = m.logf[:, :, :].rearrange("p i h -> p (i h)")
    with nc.Block() as block:

        @block.scalar
        def _(act):
            step = Chain(act, sm.act)
            step.link(act.activation(m.softp[:, :, :], fg, ACT.Abs))
            step.link(act.activation(m.softp[:, :, :], m.softp[:, :, :], ACT.Exp, scale=-1.0))
            act.activation(m.softp[:, :, :], m.softp[:, :, :], ACT.Ln, bias=1.0).then_inc(sm.log1p, 1)
            act.wait_ge(sm.neg, 1)
            act.activation(m.exp_neg_max[:, :, :], m.exp_neg_max[:, :, :], ACT.Exp, scale=-1.0)

        @block.vector
        def _(dve):
            step = Chain(dve, sm.dve)
            step.link(dve.tensor_scalar(m.logf[:, :, :], fg, 0.0, None, ALU.min))
            dve.wait_ge(sm.log1p, 1)
            dve.tensor_tensor(m.logf[:, :, :], m.logf[:, :, :], m.softp[:, :, :], ALU.subtract).then_inc(sm.logf, 1)
            dve.wait_ge(sm.summed, 1)
            dve.tensor_copy(m.cumsum[:, :], m.ps[0][:, 0:256]).then_inc(sm.dve2, 1)
            dve.wait_ge(sm.dve2, 1)
            dve.tensor_tensor(m.g_nat[:, :, :], ig, m.cumsum[:, :].rearrange("p (i h) -> p i h", h=NH0),
                              ALU.subtract).then_inc(sm.g, 1)
            dve.wait_ge(sm.g_turned, 1)
            dve.tensor_copy(m.g_t[:, :, :], m.ps[1][:, 0:256].rearrange("p (u t) -> p u t", u=2)).then_inc(sm.dve2, 1)
            dve.wait_ge(sm.dve2, 2)
            for u in range(2):
                for c in range(2):
                    part = m.g_t[:, u, c * S:(c + 1) * S]
                    dve.tensor_tensor_scan(m.gmax_t[:, u, c * S:(c + 1) * S], part, part, -3e38,
                                           ALU.max, ALU.max).then_inc(sm.gmax, 1)
            dve.wait_ge(sm.gmax_turned, 1)
            dve.tensor_tensor(m.exp_neg_max[:, :, :].rearrange("p i h -> p (i h)"), m.ps[2][:, 0:256],
                              m.cumsum[:, :], ALU.add).then_inc(sm.neg, 1)

        @block.tensor
        def _(pe):
            pe.wait_ge(sm.logf, 1)
            pe.matmul(m.ps[0][:, 0:256], m.cumsum_mat[:, :], flat, start=True, stop=True).then_inc(sm.summed, 1)
            pe.wait_ge(sm.g, 1)
            g = m.g_nat[:, :, :].rearrange("p i h -> p (i h)")
            pe.transpose(m.ps[1][:, 0:P], g[:, 0:P], m.ident[:, :])
            pe.transpose(m.ps[1][:, P:2 * P], g[:, P:2 * P], m.ident[:, :]).then_inc(sm.g_turned, 1)
            pe.wait_ge(sm.gmax, 4)
            pe.transpose(m.ps[2][:, 0:P], m.gmax_t[:, 0, :], m.ident[:, :])
            pe.transpose(m.ps[2][:, P:2 * P], m.gmax_t[:, 1, :], m.ident[:, :]).then_inc(sm.gmax_turned, 1)

        @block.sync
        def _(sp):
            sp.wait_ge(sm.gmax, 4)
            for u in range(2):
                for c in range(2):
                    rows = m.gmax_dram[c, u * 16:(u + 1) * 16].rearrange("i h s -> (i h) s")
                    sp.dma_start(rows, m.gmax_t[:, u, c * S:(c + 1) * S]).then_inc(sm.saved, 16)
            sp.wait_ge(sm.saved, 64)


def l0_attention(nc, m):
    sm = m.at
    W = DH0 + 1
    DVE_HEADS = 6
    with nc.Block() as block:

        @block.sync
        def _(sp):
            def load(g, j, filled=True):
                n = g * GROUP + j
                if filled:
                    sp.wait_ge(sm.diff, upto(n - 1))
                for c in range(2):
                    row = m.gmax_dram[c, cols(n, 1)].rearrange("i h s -> (i h s)")
                    sp.dma_start(m.g_rows[j % 2][c * S:(c + 1) * S, :], row.partition_broadcast(S)).then_inc(m.rows[j], 16)

            for j in range(GROUP):
                load(0, j, j >= 2)
            with sp.Fori(1, GROUPS) as g:
                for j in range(GROUP):
                    load(g, j)

        @block.gpsimd
        def _(pool):
            causal = m.causal_add[:, :].unsqueeze(1).to_broadcast([P, NH0, S])

            def mask(n, j):
                pool.wait_ge(sm.diff, upto(n + 1))
                d = m.decay[j % GROUP][:, :, :]
                pool.tensor_tensor(d, d, causal, ALU.add).then_inc(sm.causal, 1)

            def body(g, first, last):
                for j in range(GROUP):
                    n = g * GROUP + j
                    if not last or j + 2 < GROUP:
                        mask(n + 2, j + 2)

            mask(0, 0)
            mask(1, 1)
            groups(pool, body)

        @block.vector
        def _(dve):
            heads = m.head_mask[:, 0:DVE_HEADS].unsqueeze(2).to_broadcast([P, DVE_HEADS, P])

            def begin(g, j, filled=True):
                n = g * GROUP + j
                dve.wait_ge(m.rows[j % GROUP], 32 * (g + j // GROUP) + 32)
                if filled:
                    dve.wait_ge(sm.c, upto(n - 2))
                own = m.g_nat[:, cols(n, 1), :].rearrange("p i h -> p (i h)").unsqueeze(2).to_broadcast([P, NH0, S])
                dve.tensor_tensor(m.decay[j % GROUP][:, :, :], own, m.g_rows[j % 2][:, :].rearrange("p (h s) -> p h s", h=NH0),
                                  ALU.subtract).then_inc(sm.diff, 1)
                if filled:
                    dve.wait_ge(sm.qk, upto(n - 1))
                q = m.XT[:, cols(n, P)].unsqueeze(1).to_broadcast([P, DVE_HEADS, P])
                dve.tensor_tensor(m.q_spread[j % 2][:, 0:DVE_HEADS, :], q, heads, ALU.mult).then_inc(sm.spread, 1)

            def end(g, j, filled):
                n = g * GROUP + j
                dve.wait_ge(sm.exp, upto(n + 1))
                dve.wait_ge(sm.qk, upto(n + 1))
                if filled:
                    dve.wait_ge(sm.av, upto(n - 1))
                dve.tensor_tensor(m.c_t[j % 2][:, :, :], m.ps[j % 2][:, :].rearrange("p (h s) -> p h s", h=NH0),
                                  m.decay[j][:, :, :], ALU.mult).then_inc(sm.c, 1)

            def body(g, first, last):
                for j in range(GROUP):
                    if not last or j + 2 < GROUP:
                        begin(g, j + 2)
                    end(g, j, not first or j > 1)

            begin(0, 0, False)
            begin(0, 1, False)
            groups(dve, body)

        @block.scalar
        def _(act):
            def keys(n, j, filled=True):
                if filled:
                    act.wait_ge(sm.qk, upto(n - 1))
                act.activation(m.k_stage[j % 2][:, :], m.CT[:, cols(n, P)], ACT.Copy, scale=DH0 ** -0.5).then_inc(sm.k, 1)
                for h in range(DVE_HEADS, NH0):
                    act.activation(m.q_spread[j % 2][:, h, :], m.XT[:, cols(n, P)], ACT.Copy,
                                   scale=m.head_mask[:, h:h + 1]).then_inc(sm.k, 1)

            def values(n, j, filled=True):
                if filled:
                    act.wait_ge(sm.av, upto(n - 1))
                for c in range(2):
                    half = slice(c * S, (c + 1) * S)
                    act.copy(m.v_ones[j % 2][half, :, c, 0:DH0],
                                     m.C[half, cols(n, 1), :].rearrange("p i (h d) -> p (i h) d", h=NH0)).then_inc(sm.v, 1)

            def exp(n, j):
                act.wait_ge(sm.causal, upto(n + 1))
                d = m.decay[j % GROUP][:, :, :]
                act.activation(d, d, ACT.Exp).then_inc(sm.exp, 1)

            def body(g, first, last):
                for j in range(GROUP):
                    n = g * GROUP + j
                    if not last or j + 2 < GROUP:
                        keys(n + 2, j + 2)
                    if not last or j + 1 < GROUP:
                        exp(n + 1, j + 1)
                        values(n + 1, j + 1, not first or j > 0)
                    act.wait_ge(sm.av, upto(n + 1))
                    for c in range(2):
                        sums = m.ps[2 + j % 2][0:S, 0:2 * NH0 * W].rearrange("s (h c w) -> s h c w", c=2, w=W)[:, :, c, :]
                        dst = m.num[c * S:(c + 1) * S, cols(n, 1), :].rearrange("p i (h w) -> p (i h) w", w=W)
                        act.copy(dst, sums).then_inc(sm.out, 1)

            act.wait_ge(m.ctx_loaded, 16)
            values(0, 0, False)
            keys(0, 0, False)
            keys(1, 1, False)
            exp(0, 0)
            groups(act, body)

        @block.tensor
        def _(pe):
            def scores(n, j, filled=True):
                pe.wait_ge(sm.k, upto((1 + NH0 - DVE_HEADS) * (n + 1)))
                pe.wait_ge(sm.spread, upto(n + 1))
                if filled:
                    pe.wait_ge(sm.c, upto(n - 1))
                for c in range(2):
                    half = slice(c * S, (c + 1) * S)
                    ins = pe.matmul(m.ps[j % 2][half, :], m.k_stage[j % 2][:, half], m.q_spread[j % 2][:, :, half],
                                    start=True, stop=True)
                ins.then_inc(sm.qk, 1)

            def body(g, first, last):
                for j in range(GROUP):
                    n = g * GROUP + j
                    if not last or j + 1 < GROUP:
                        scores(n + 1, j + 1, not first or j > 0)
                    pe.wait_ge(sm.c, upto(n + 1))
                    pe.wait_ge(sm.v, upto(2 * n + 2))
                    if not first or j > 1:
                        pe.wait_ge(sm.out, upto(2 * n - 2))
                    hold(pe, m)
                    for h in range(NH0):
                        ins = pe.matmul(m.ps[2 + j % 2][0:S, 2 * W * h:2 * W * (h + 1)], m.c_t[j % 2][:, h, :],
                                        m.v_ones[j % 2][:, h, :, :].rearrange("p c w -> p (c w)"), start=True, stop=True)
                    ins.then_inc(sm.av, 1)

            scores(0, 0, False)
            groups(pe, body)


def l0_attention_finish(nc, m):
    sm = m.af
    W = DH0 + 1
    num = m.num[:, :, :].rearrange("p i (h w) -> p (i h) w", w=W)
    hid = m.hid[:, :, :]
    N = TILES * NH0
    wide = [P, N, DH0]
    halves = (slice(0, N // 2), slice(N // 2, N))
    with nc.Block() as block:

        @block.vector
        def _(dve):
            step = Chain(dve, sm.dve)
            step.link(dve.scalar_tensor_tensor(m.den[:, :], num[:, :, DH0], -1.0, num[:, :, DH0], ALU.mult, ALU.max))
            step.link(dve.tensor_tensor(m.den[:, :], m.den[:, :], m.exp_neg_max[:, :, :].rearrange("p i h -> p (i h)"), ALU.max))
            step.link(dve.tensor_scalar(m.den[:, :], m.den[:, :], NORM_EPS, None, ALU.add))
            step.link(dve.reciprocal(m.den[:, :], m.den[:, :]))
            step.link(dve.tensor_tensor(hid, num[:, :, 0:DH0], m.den[:, :].unsqueeze(2).to_broadcast(wide), ALU.mult))
            step.link(dve.tensor_reduce(m.hmean[:, :], hid, AX, ALU.add))
            step.link(dve.tensor_scalar(m.hmean[:, :], m.hmean[:, :], 1.0 / DH0, None, ALU.mult))
            for rows in halves:
                h = m.hid[:, rows, :]
                dve.tensor_tensor(h, h, m.hmean[:, rows].unsqueeze(2).to_broadcast([P, N // 2, DH0]), ALU.subtract).then_inc(sm.centered, 1)
            for k, rows in enumerate(halves):
                dve.wait_ge(sm.squared, k + 1)
                step.link(dve.tensor_reduce(m.hvar[:, rows], m.hsq[:, rows, :], AX, ALU.add))
            step.link(dve.tensor_scalar(m.hvar[:, :], m.hvar[:, :], 1.0 / DH0, LN_EPS, ALU.mult, ALU.add))
            dve.sem_inc(sm.var, 1)
            dve.wait_ge(m.tanh_ready, 1)
            step.link(dve.tensor_scalar(m.out_w_rows[:, :], m.out_w_rows[:, :], m.tanh_g[:, 0:1], None, ALU.mult))
            dve.wait_ge(sm.root, 1)
            inverse_root(dve, step, m.hvar[:, :], m.hmean[:, :], m.den[:, :])
            step.link(dve.tensor_tensor(hid, hid, m.hmean[:, :].unsqueeze(2).to_broadcast(wide), ALU.mult))
            tiles = hid.rearrange("p (i h) d -> p i (h d)", h=NH0)
            step.link(dve.tensor_tensor(tiles, tiles, m.out_w_rows[:, :].unsqueeze(1).to_broadcast([P, TILES, E]), ALU.mult))
            step.link(dve.tensor_tensor(m.X[:, :, :], m.X[:, :, :], tiles, ALU.add))
            all_stats(dve, m)

        @block.scalar
        def _(act):
            for k, rows in enumerate(halves):
                act.wait_ge(sm.centered, k + 1)
                act.activation(m.hsq[:, rows, :], m.hid[:, rows, :], ACT.Square).then_inc(sm.squared, 1)
            act.wait_ge(sm.var, 1)
            act.activation(m.hmean[:, :], m.hvar[:, :], ACT.Sqrt).then_inc(sm.root, 1)


def l0_ffn_weights(nc, m):
    sm = m.fw
    with nc.Block() as block:

        @block.vector
        def _(dve):
            step = Chain(dve, sm.dve)
            dve.wait_ge(m.ffn0_loaded, 80)
            for raw, q, top, scale, n in ((m.gu_raw, m.gu_q, m.gu_top, m.gu_scale, 6), (m.dn_raw, m.dn_q, m.dn_top, m.dn_scale, 1)):
                wide = list(raw.shape)
                step.link(dve.tensor_reduce(top[:, :], raw, AX, ALU.max, apply_absolute_value=True))
                step.link(dve.tensor_scalar(scale[:, :], top[:, :], 1.0 / QMAX, None, ALU.mult))
                step.link(dve.reciprocal(top[:, :], scale[:, :]))
                step.link(dve.tensor_tensor(raw, raw, top[:, :].unsqueeze(2).to_broadcast(wide), ALU.mult))
                step.link(dve.tensor_scalar(raw, raw, MAGIC, None, ALU.add))
                step.link(dve.tensor_scalar(raw, raw, MAGIC + QMAX, MAGIC - QMAX - 1, ALU.min, ALU.max))
                step.link(dve.tensor_scalar(q, raw, MAGIC, None, ALU.subtract))
            step.link(dve.tensor_scalar(m.dn_diag[:, :], m.ident[:, :], m.dn_scale[:, 0:1], None, ALU.mult))
            dve.sem_inc(sm.quantized, 1)
            dve.wait_ge(sm.turned, 1)
            dve.tensor_copy(m.gu_t[:, :, :], m.ps[0][:, :].bitcast(BF16)[:, 0:6 * P].rearrange("p (k n) -> p k n", k=6)).then_inc(sm.dve, 1)
            dve.tensor_copy(m.dn_t[:, 0:2, :], m.ps[1][:, :].bitcast(BF16)[:, 0:2 * P].rearrange("p (k n) -> p k n", k=2))
            dve.tensor_copy(m.dn_t[0:96, 2, :], m.ps[1][0:96, :].bitcast(BF16)[:, 2 * P:3 * P])
            dve.tensor_copy(m.dn_row[:, :], m.ps[2][:, 0:P])

        @block.gpsimd
        def _(pool):
            pool.memset(m.dn_t[96:P, 2, :], 0.0)

        @block.tensor
        def _(pe):
            pe.wait_ge(sm.quantized, 1)
            for k in range(6):
                pe.transpose(m.ps[0][:, :].bitcast(BF16)[:, k * P:(k + 1) * P], m.gu_q[:, k, :], m.ident_bf[:, :])
            for k, n in enumerate((P, P, 96)):
                pe.transpose(m.ps[1][0:n, :].bitcast(BF16)[:, k * P:(k + 1) * P], m.dn_q[:, 0, k * P:k * P + n], m.ident_bf[:, :])
            pe.matmul(m.ps[2][:, 0:P], m.ones[:, :], m.dn_diag[:, :], start=True, stop=True).then_inc(sm.turned, 1)


def l0_ffn_norm(nc, m):
    with nc.Block() as block:

        @block.vector
        def _(dve):
            with dve.Fori(0, GROUPS // 2) as pair:
                for u in range(2):
                    for j in range(GROUP):
                        tile = (2 * pair + u) * GROUP + j
                        normalize(dve, m, m.XN[:, cols(tile, 1), :].rearrange("p i f -> p (i f)"), tile).then_inc(m.fn.normed, 1)
                for u in range(2):
                    g = 2 * pair + u
                    dve.wait_ge(m.fn.normed, upto(g * GROUP + GROUP))
                    dve.tensor_reduce(m.x_top[:, cols(g, 1)], m.XN[:, cols(g, GROUP), :].rearrange("p i f -> p (i f)"),
                                      AX, ALU.max, apply_absolute_value=True)


def activation_scale(nc, m, sm, tops, clip, scales):
    with nc.Block() as block:

        @block.scalar
        def _(act):
            act.wait_ge(m.clips_loaded, 32)
            act.activation(m.clip_exp[0:1, :], clip, ACT.Exp, scale=-1.0).then_inc(sm.exp, 1)

        @block.vector
        def _(dve):
            step = Chain(dve, sm.dve)
            step.link(dve.tensor_reduce(m.top_col[:, :], tops, AX, ALU.max))
            dve.sem_inc(sm.col, 1)
            dve.wait_ge(sm.row, 1)
            step.link(dve.tensor_reduce(m.top_one[:, 0:1], m.ps[0][0:1, 0:P], AX, ALU.max))
            dve.wait_ge(sm.exp, 1)
            step.link(dve.tensor_scalar(m.top_one[:, 1:2], m.clip_exp[0:1, :], 1.0, None, ALU.add))
            step.link(dve.reciprocal(m.top_one[:, 1:2], m.top_one[:, 1:2]))
            step.link(dve.scalar_tensor_tensor(m.top_pair[:, 0:1], m.top_one[:, 0:1], 1.0 / QMAX, m.top_one[:, 1:2], ALU.mult, ALU.mult))
            step.link(dve.reciprocal(m.top_pair[:, 1:2], m.top_pair[:, 0:1]))
            dve.sem_inc(sm.pair, 1)
            dve.wait_ge(sm.spread, 1)
            dve.tensor_copy(scales[:, :], m.ps[1][:, 0:2])

        @block.tensor
        def _(pe):
            pe.wait_ge(sm.col, 1)
            pe.transpose(m.ps[0][0:1, 0:P], m.top_col[:, :], m.ident[:, :]).then_inc(sm.row, 1)
            pe.wait_ge(sm.pair, 1)
            pe.matmul(m.ps[1][:, 0:2], m.ones[0:1, :], m.top_pair[:, :], start=True, stop=True).then_inc(sm.spread, 1)


def l0_ffn_up(nc, m):
    sm = m.fu
    with nc.Block() as block:

        @block.vector
        def _(dve):
            dve.tensor_scalar(m.gu_scale[:, :], m.gu_scale[:, :], m.x_scale[:, 0:1], None, ALU.mult).then_inc(sm.scaled, 1)
            dve.wait_ge(sm.scaled, upto(1))

            def quantize(g):
                x = m.XN[:, cols(g, GROUP), :].rearrange("p i f -> p (i f)")
                dve.tensor_scalar(m.round_x[:, :], x, m.x_scale[:, 1:2], MAGIC, ALU.mult, ALU.add).then_inc(sm.shifted, 1)
                dve.wait_ge(sm.shifted, upto(g + 1))
                dve.tensor_scalar(m.round_x[:, :], m.round_x[:, :], MAGIC + QMAX, MAGIC - QMAX - 1, ALU.min, ALU.max).then_inc(sm.clipped, 1)
                dve.wait_ge(sm.clipped, upto(g + 1))
                dve.wait_ge(sm.turned, upto(g))
                dve.tensor_scalar(m.xq[:, :], m.round_x[:, :], MAGIC, None, ALU.subtract).then_inc(sm.quantized, 1)

            def stand(g):
                dve.wait_ge(sm.turned, upto(g + 1))
                dve.wait_ge(sm.upped, upto(3 * g))
                dve.tensor_copy(m.xq_t[:, :], m.ps[0][:, :].bitcast(BF16)[:, 0:512]).then_inc(sm.stood, 1)

            def hidden(g, k):
                n = CHUNKS[k]
                dve.wait_ge(sm.silu, upto(3 * g + k + 1))
                h = m.HT[0:n, k, cols(g, 512)]
                dve.scalar_tensor_tensor(h, m.ps[2 + 2 * k][0:n, :], m.gu_scale[0:n, 3 + k:4 + k],
                                         m.silu[k][0:n, :], ALU.mult, ALU.mult).then_inc(sm.hidden, 1)
                dve.wait_ge(sm.hidden, upto(3 * g + k + 1))
                dve.tensor_reduce(m.h_top[0:n, k, cols(g, 1)], h, AX, ALU.max, apply_absolute_value=True)

            quantize(0)
            stand(0)
            with dve.Fori(0, GROUPS - 1) as g:
                quantize(g + 1)
                hidden(g, 0)
                hidden(g, 1)
                stand(g + 1)
                hidden(g, 2)
            for k in range(3):
                hidden(GROUPS - 1, k)

        @block.scalar
        def _(act):
            act.wait_ge(sm.scaled, upto(1))
            with act.Fori(0, GROUPS) as g:
                for k, n in enumerate(CHUNKS):
                    act.wait_ge(sm.upped, upto(3 * g + k + 1))
                    act.activation(m.silu[k][0:n, :], m.ps[1 + 2 * k][0:n, :], ACT.Silu, scale=m.gu_scale[0:n, k:k + 1]).then_inc(sm.silu, 1)

        @block.gpsimd
        def _(pool):
            pool.memset(m.HT[96:P, 2, :], 0.0)
            pool.memset(m.h_top[96:P, 2, :], 0.0)

        @block.tensor
        def _(pe):
            def turn(g):
                pe.wait_ge(sm.quantized, upto(g + 1))
                pe.wait_ge(sm.stood, upto(g))
                for j in range(GROUP):
                    ins = pe.transpose(m.ps[0][:, :].bitcast(BF16)[:, j * P:(j + 1) * P], m.xq[:, j * P:(j + 1) * P], m.ident_bf[:, :])
                ins.then_inc(sm.turned, 1)

            def up(g, first=False):
                pe.wait_ge(sm.stood, upto(g + 1))
                for k, n in enumerate(CHUNKS):
                    if not first:
                        pe.wait_ge(sm.hidden, upto(3 * g - 3 + k + 1))
                    pe.matmul(m.ps[1 + 2 * k][0:n, :], m.gu_t[:, k, 0:n], m.xq_t[:, :], start=True, stop=True)
                    pe.matmul(m.ps[2 + 2 * k][0:n, :], m.gu_t[:, 3 + k, 0:n], m.xq_t[:, :], start=True, stop=True).then_inc(sm.upped, 1)

            turn(0)
            up(0, True)
            turn(1)
            with pe.Fori(1, GROUPS - 1) as g:
                up(g)
                turn(g + 1)
            up(GROUPS - 1)


def l0_ffn_down(nc, m):
    sm = m.fd
    with nc.Block() as block:

        @block.vector
        def _(dve):
            step = Chain(dve, sm.dve)
            step.link(dve.tensor_scalar(m.dn_row[:, :], m.dn_row[:, :], m.h_scale[:, 0:1], m.tanh_g[:, 2:3], ALU.mult, ALU.mult))
            scale = m.dn_row[:, :].unsqueeze(1).to_broadcast([P, GROUP, E])

            def quantize(g):
                dve.wait_ge(sm.shifted, upto(g + 1))
                dve.tensor_scalar(m.round_h[:, :, :], m.round_h[:, :, :], MAGIC + QMAX, MAGIC - QMAX - 1, ALU.min, ALU.max).then_inc(sm.clipped, 1)
                dve.wait_ge(sm.clipped, upto(g + 1))
                dve.wait_ge(sm.downed, upto(g))
                dve.tensor_scalar(m.hq[:, :, :], m.round_h[:, :, :], MAGIC, None, ALU.subtract).then_inc(sm.quantized, 1)

            def residual(g, u):
                dve.wait_ge(sm.downed, upto(g + 1))
                dve.tensor_tensor(m.down[:, :, :], m.ps[u][:, :].rearrange("p (j f) -> p j f", j=GROUP), scale, ALU.mult).then_inc(sm.out, 1)
                dve.wait_ge(sm.out, upto(g + 1))
                x = m.X[:, cols(g, GROUP), :]
                dve.tensor_tensor(x, x, m.down[:, :, :], ALU.add).then_inc(sm.added, 1)
                dve.wait_ge(sm.added, upto(g + 1))
                for j in range(GROUP):
                    stats_of(dve, m, g * GROUP + j)

            quantize(0)
            quantize(1)
            with dve.Fori(0, GROUPS // 2 - 1) as pair:
                for u in range(2):
                    residual(2 * pair + u, u)
                    quantize(2 * pair + u + 2)
            for u in range(2):
                residual(GROUPS - 2 + u, u)

        @block.scalar
        def _(act):
            with act.Fori(0, GROUPS) as g:
                act.wait_ge(sm.quantized, upto(g))
                act.activation(m.round_h[:, :, :], m.HT[:, :, cols(g, 512)], ACT.Identity, bias=m.magic[:, 0:1],
                               scale=m.h_scale[:, 1:2]).then_inc(sm.shifted, 1)

        @block.tensor
        def _(pe):
            def down(g, u, first=False):
                pe.wait_ge(sm.quantized, upto(g + 1))
                if not first:
                    pe.wait_ge(sm.out, upto(g - 1))
                for j in range(GROUP):
                    for k in range(3):
                        ins = pe.matmul(m.ps[u][:, j * P:(j + 1) * P], m.hq[:, k, j * P:(j + 1) * P], m.dn_t[:, k, :],
                                        start=(k == 0), stop=(k == 2))
                ins.then_inc(sm.downed, 1)

            for u in range(2):
                down(u, u, True)
            with pe.Fori(1, GROUPS // 2) as pair:
                for u in range(2):
                    down(2 * pair + u, u)


def split_parts(eng, step, out, exact):
    step.link(eng.tensor_tensor(exact, exact, out[:, 0], ALU.subtract))
    step.link(eng.tensor_copy(out[:, 1], exact))
    return eng.tensor_tensor(out[:, 2], exact, out[:, 1], ALU.subtract)


LEFT_PARTS = (0, 1, 2, 0, 1, 0)
RIGHT_PARTS = (0, 0, 0, 1, 1, 2)
STACK = len(LEFT_PARTS) * DH1


def load_left(eng, out, parts, sem):
    row = 0
    for n in (3, 2, 1):
        eng.dma_start(out[row:row + n * DH1], parts[:, 0:n].rearrange("h k d t -> (k d) h t")).then_inc(sem, 16)
        row += n * DH1


def l1_weights(nc, m):
    sm = m.lw
    with nc.Block() as block:

        @block.tensor
        def _(pe):
            pe.wait_ge(m.proj_loaded, 64)
            for k in range(4):
                ins = pe.transpose(m.ps[0][:, k * P:(k + 1) * P], m.proj_raw[:, k, :], m.ident[:, :])
            pe.wait_ge(m.pos_loaded, 48)
            for k in range(4):
                ins = pe.transpose(m.ps[1][:, k * S:(k + 1) * S],
                                   m.pos_k_raw[:, :, :].rearrange("s t d -> s (t d)")[:, k * P:(k + 1) * P], m.ident[0:S, 0:S])
            ins.then_inc(sm.turned, 1)

        @block.vector
        def _(dve):
            step = Chain(dve, sm.dve)
            dve.wait_ge(sm.turned, 1)
            pos = m.ps[1][:, 0:4 * S]
            dve.tensor_copy(m.pos_parts[:, 0], pos)
            step.link(dve.tensor_copy(m.pos_exact[:, :], pos))
            split_parts(dve, step, m.pos_parts, m.pos_exact[:, :])
            dve.tensor_copy(m.proj_t[:, :, :], m.ps[0][:, :].rearrange("p (k n) -> p k n", k=4))
            dve.wait_ge(m.proj_bias_loaded, 64)
            dve.tensor_scalar(m.bo_rows[:, :], m.bo_rows[:, :], m.tanh_g[:, 1:2], None, ALU.mult)


def l1_project(nc, m):
    sm, rl = m.pj, m.rl
    REL = (3, 4, 5, 6)

    def pairs(eng, project, relative):
        for u in range(2):
            project(u, u)
        with eng.Fori(1, GROUPS // 2 - 1) as pair:
            for u in range(2):
                project(2 * pair + u, u)
                relative(2 * pair + u - 2, u)
        for u in range(2):
            project(GROUPS - 2 + u, u)
            relative(GROUPS - 4 + u, u)
        for u in range(2):
            relative(GROUPS - 2 + u, u)

    def take(eng, copy, mine):
        def relative(g, u):
            for n in mine:
                half = n // 4
                eng.wait_ge(rl.done, upto(8 * g + n + 1))
                if n in (mine[0], mine[2]):
                    eng.wait_ge(rl.saved[half], upto(16 * g))
                copy(m.rel[half][:, 512 * (n % 4):512 * (n % 4 + 1)], m.ps[REL[n % 4]]).then_inc(rl.out[n % 4], 1)
        return relative

    with nc.Block() as block:

        @block.vector
        def _(dve):
            def norm(g):
                dve.wait_ge(sm.turned, upto(g))
                for j in range(GROUP):
                    normalize(dve, m, m.stage_x[:, j, :], g * GROUP + j).then_inc(sm.normed, 1)

            def project(g, u):
                if not (isinstance(g, int) and g == GROUPS - 1):
                    norm(g + 1)
                q = m.QT[:, cols(g, 512)]
                dve.wait_ge(sm.q_out, upto(2 * g + 2))
                dve.tensor_tensor(m.q_rest[:, :], q, m.q_parts[:, 0], ALU.subtract).then_inc(sm.rest, 1)
                dve.wait_ge(sm.rest, upto(g + 1))
                dve.tensor_copy(m.q_parts[:, 1], m.q_rest[:, :]).then_inc(sm.middle, 1)
                dve.wait_ge(sm.middle, upto(g + 1))
                dve.tensor_tensor(m.q_parts[:, 2], m.q_rest[:, :], m.q_parts[:, 1], ALU.subtract).then_inc(sm.low, 1)

            norm(0)
            pairs(dve, project, take(dve, dve.tensor_copy, (1, 3, 5, 7)))
            dve.wait_ge(m.mask_in_sem, 16)
            dve.tensor_scalar(m.mask_add[:, :, :], m.mask_in[:, :, :], 0.0, FAR, ALU.is_equal, ALU.mult)

        @block.tensor
        def _(pe):
            def project(g, u):
                pe.wait_ge(sm.xt_out, upto(g))
                pe.wait_ge(sm.normed, upto(g * GROUP + GROUP))
                for j in range(GROUP):
                    ins = pe.transpose(m.ps[0][:, j * P:(j + 1) * P], m.stage_x[:, j, :], m.ident[:, :])
                ins.then_inc(sm.turned, 1)
                pe.wait_ge(sm.q_out, upto(2 * g))
                pe.wait_ge(sm.k_out, upto(g))
                pe.matmul(m.ps[2][:, :], m.proj_t[:, 1, :], m.CT[:, cols(g, 512)], start=True, stop=True).then_inc(sm.k_done, 1)
                pe.wait_ge(sm.xt_out, upto(g + 1))
                pe.matmul(m.ps[1][:, :], m.proj_t[:, 0, :], m.stage_xt[:, :], start=True, stop=True).then_inc(sm.q_done, 1)
                if isinstance(g, int) and g == 1:
                    pe.wait_ge(m.lw.moved, 16 + 16 * len(RIGHT_PARTS))

            def relative(g, u):
                q = m.q_left[u][:, :, :].rearrange("k h (b t) -> k (h b) t", t=S)
                pe.wait_ge(rl.loaded[u], upto(24 * (g - u) + 48))
                for n in range(8):
                    pe.wait_ge(rl.out[n % 4], upto(2 * g + n // 4))
                    for k in range(8):
                        t = 8 * n + k
                        ins = pe.matmul(m.ps[REL[n % 4]][:, k * S:(k + 1) * S], q[:, :, t],
                                        m.pos_right[:, t % 16, (t // 16) * S:(t // 16 + 1) * S], start=True, stop=True)
                    ins.then_inc(rl.done, 1)

            pairs(pe, project, relative)

        @block.scalar
        def _(act):
            def project(g, u):
                act.wait_ge(sm.turned, upto(g + 1))
                act.wait_ge(sm.q_done, upto(g))
                act.copy(m.stage_xt[:, :], m.ps[0][:, :]).then_inc(sm.xt_out, 1)
                act.wait_ge(sm.k_done, upto(g + 1))
                act.activation(m.KT[:, cols(g, 512)], m.ps[2][:, :], ACT.Identity, bias=m.proj_bias[:, 1:2]).then_inc(sm.k_out, 1)
                act.wait_ge(sm.q_done, upto(g + 1))
                act.activation(m.QT[:, cols(g, 512)], m.ps[1][:, :], ACT.Identity, bias=m.proj_bias[:, 0:1]).then_inc(sm.q_out, 1)
                act.wait_ge(sm.low, upto(g))
                act.wait_ge(sm.parts_saved, upto(48 * g))
                act.activation(m.q_parts[:, 0], m.ps[1][:, :], ACT.Identity, bias=m.proj_bias[:, 0:1]).then_inc(sm.q_out, 1)

            pairs(act, project, take(act, act.copy, (0, 2, 4, 6)))

        @block.sync
        def _(sp):
            sp.dma_start(m.mask_in[:, :, :], m.mask.rearrange("(i c) t s -> (c t) i s", c=2)).then_inc(m.mask_in_sem, 16)
            sp.dma_start(m.pos_dram, m.pos_parts[:, :, :]).then_inc(m.lw.moved, 16)
            sp.wait_ge(m.lw.moved, 16)
            for r, part in enumerate(RIGHT_PARTS):
                src = m.pos_dram[:, part].rearrange("(t d) k -> d t k", d=DH1)
                sp.dma_start(m.pos_right[r * DH1:(r + 1) * DH1], src).then_inc(m.lw.moved, 16)

            def project(g, u):
                sp.wait_ge(sm.low, upto(g + 1))
                hold(sp, m)
                for part in range(3):
                    dst = m.q_dram[cols(g, 1), :, part].rearrange("g h d t -> (g h) d t")
                    sp.dma_start(dst, m.q_parts[:, part]).then_inc(sm.parts_saved, 16)

            def load(g, u):
                sp.wait_ge(sm.parts_saved, upto(48 * g + 48))
                hold(sp, m)
                load_left(sp, m.q_left[u], m.q_dram[cols(g, 1)].rearrange("g h k d t -> (g h) k d t"), rl.loaded[u])

            def begin(g, u):
                project(g, u)
                if isinstance(g, int) and g < 2:
                    load(g, u)

            def relative(g, u):
                rows = m.rel_dram[cols(g, 1)].rearrange("g h b t s -> (g h b) (t s)")
                for half in range(2):
                    for bank in range(4):
                        sp.wait_ge(rl.out[bank], upto(2 * g + half + 1))
                        hold(sp, m)
                    sp.dma_start(rows[:, 2048 * half:2048 * (half + 1)], m.rel[half][:, :]).then_inc(rl.saved[half], 16)
                if not (isinstance(g, int) and g >= GROUPS - 2):
                    load(g + 2, u)

            pairs(sp, begin, relative)
            for half in range(2):
                sp.wait_ge(rl.saved[half], upto(16 * GROUPS))


def l1_attention(nc, m):
    sm = m.a1
    W = DH1 + 1
    LAST = GROUPS - 1
    scores = m.wide[0][:, :]
    turned = m.wide[1][:, :]
    values = m.ps[4]
    rel_v = m.ps[5]

    with nc.Block() as block:

        @block.sync
        def _(sp):
            def load_rel(g, j, filled=True):
                n = g * GROUP + j
                if filled:
                    sp.wait_ge(sm.added, upto(n - 3))
                    hold(sp, m)
                for c in range(2):
                    sp.dma_start(m.rel_in[j][c * S:(c + 1) * S, :, :],
                                 m.rel_dram[cols(g, 1), :, 2 * j + c].rearrange("g h t s -> (g t) h s")).then_inc(m.rel_sem[j], 16)

            def turn_pos(g):
                sp.wait_ge(sm.pv_out, upto(g + 1))
                hold(sp, m)
                for half in range(2):
                    rows = m.pv_dram[cols(g, 1), :, 32 * half:32 * (half + 1)].rearrange("g n t e -> (g n) (t e)")
                    sp.dma_start(rows, m.pv[half * S:(half + 1) * S, :]).then_inc(sm.pv_saved, 16)
                sp.wait_ge(sm.pv_saved, upto(32 * g + 32))
                hold(sp, m)
                sp.wait_ge(sm.summed, upto(g))
                hold(sp, m)
                sp.dma_start(m.pv_in[:, :, :], m.pv_dram[cols(g, 1)].rearrange("g (n c) t e -> (g c t) n e", c=2)).then_inc(sm.pv_back, 16)

            for j in range(GROUP):
                load_rel(0, j, False)

            def body(g, first, last):
                if not last:
                    for j in range(GROUP):
                        load_rel(g + 1, j)
                if not first:
                    turn_pos(g - 1)

            groups(sp, body)
            turn_pos(LAST)

        @block.gpsimd
        def _(pool):
            def stage(n):
                src = m.CT[:, cols(n, P)].rearrange("p (c s) -> p c s", c=2)
                for twice in range(2):
                    pool.tensor_copy(m.ct_twice[:, :, twice, :], src).then_inc(sm.ct_staged, 1)

            def mask(g, j):
                n, slot = g * GROUP + j, j % GROUP
                pool.wait_ge(m.rel_sem[slot], 32 * (g + j // GROUP) + 32)
                rel = m.rel_in[slot][:, :, :]
                pool.tensor_tensor(rel, rel, m.mask_add[:, cols(n, 1), :].to_broadcast([P, NH1, S]), ALU.add).then_inc(sm.masked, 1)

            def body(g, first, last):
                for j in range(GROUP):
                    if not last or j + 2 < GROUP:
                        mask(g, j + 2)
                    if not last or j + 1 < GROUP:
                        pool.wait_ge(sm.v_done, upto(g * GROUP + j + 1))
                        stage(g * GROUP + j + 1)

            stage(0)
            mask(0, 0)
            mask(0, 1)
            groups(pool, body)

        @block.vector
        def _(dve):
            inner = m.inner_mask[:, :].unsqueeze(2).to_broadcast([P, 4, P])

            def spread(g, j, filled=True):
                n, z = g * GROUP + j, j % 2
                if filled:
                    dve.wait_ge(sm.scored, upto(n - 1))
                k = m.KT[:, cols(n, P)].unsqueeze(1).to_broadcast([P, 4, P])
                dve.tensor_tensor(m.k_inner[z][:, :, :], k, inner, ALU.mult).then_inc(sm.k_spread, 1)

            def place_values(g, j):
                n = g * GROUP + j
                dve.wait_ge(sm.v_done, upto(n + 1))
                dve.wait_ge(sm.av_done, upto(n))
                for c in range(2):
                    for p in range(2):
                        half = slice(p * S, (p + 1) * S)
                        src = values[half, c * P:(c + 1) * P].rearrange("s (n p d) -> s n p d", p=2, d=DH1)[:, :, p, :]
                        bias = m.bv_rows[half, :].rearrange("s (n p d) -> s n p d", p=2, d=DH1)[:, :, p, :]
                        dve.tensor_tensor(m.v_block[half, :, c, p, 0:DH1], src, bias, ALU.add).then_inc(sm.v_out, 1)

            def shift(g, j, filled=True):
                n, z = g * GROUP + j, j % 2
                dve.wait_ge(sm.masked, upto(n + 1))
                dve.wait_ge(sm.scored, upto(n + 1))
                if filled:
                    dve.wait_ge(sm.exped, upto(n - 1))
                t = m.soft[z][:, :, :]
                dve.tensor_tensor(t, scores.rearrange("p (h s) -> p h s", s=S), m.rel_in[j % GROUP][:, :, :], ALU.add).then_inc(sm.added, 1)
                dve.wait_ge(sm.added, upto(n + 1))
                dve.tensor_reduce(m.row_max[:, :], t, AX, ALU.max).then_inc(sm.maxed, 1)
                dve.wait_ge(sm.maxed, upto(2 * n + 1))
                dve.tensor_scalar(m.row_max[:, :], m.row_max[:, :], FAR / 10, None, ALU.max).then_inc(sm.maxed, 1)
                dve.wait_ge(sm.maxed, upto(2 * n + 2))
                dve.tensor_tensor(t, t, m.row_max[:, :].unsqueeze(2).to_broadcast([P, NH1, S]), ALU.subtract).then_inc(sm.shifted, 1)

            def weigh(g):
                dve.wait_ge(sm.pv_back, upto(16 * g + 16))
                dve.wait_ge(sm.av_out, upto(8 * g + 8))
                av = m.av[:, cols(g, GROUP), :].rearrange("p i (h w) -> p (i h) w", w=W)
                dve.tensor_scalar(m.row_sum[:, :], av[:, :, DH1], 1e-30, None, ALU.max).then_inc(sm.small, 1)
                dve.wait_ge(sm.small, upto(4 * g + 1))
                dve.reciprocal(m.row_sum[:, :], m.row_sum[:, :]).then_inc(sm.small, 1)
                att = m.att[:, :, :].rearrange("p i (h d) -> p (i h) d", d=DH1)
                pv = m.pv_in[:, :, :].rearrange("p n (q d) -> p (n q) d", d=DH1)
                dve.wait_ge(sm.att_turned, upto(g))
                dve.tensor_tensor(att, av[:, :, 0:DH1], pv, ALU.add).then_inc(sm.summed, 1)
                dve.wait_ge(sm.summed, upto(g + 1))
                dve.wait_ge(sm.small, upto(4 * g + 2))
                dve.tensor_tensor(att, att, m.row_sum[:, :].unsqueeze(2).to_broadcast([P, GROUP * NH1, DH1]), ALU.mult).then_inc(sm.att_done, 1)

            def add_to_x(g):
                dve.wait_ge(sm.wo_done, upto(g + 1))
                bo = m.bo_rows[:, :].unsqueeze(1).to_broadcast([P, GROUP, E])
                dve.scalar_tensor_tensor(m.res[:, :, :], m.ps7[:, :].rearrange("p (i f) -> p i f", f=E), m.tanh_g[:, 1:2],
                                         bo, ALU.mult, ALU.add).then_inc(sm.small, 1)
                dve.wait_ge(sm.small, upto(4 * g + 3))
                x = m.X[:, cols(g, GROUP), :]
                dve.tensor_tensor(x, x, m.res[:, :, :], ALU.add).then_inc(sm.small, 1)
                dve.wait_ge(sm.small, upto(4 * g + 4))
                for j in range(GROUP):
                    stats_of(dve, m, g * GROUP + j)

            def body(g, u, first, second, last):
                for j in range(GROUP):
                    if not last or j + 3 < GROUP:
                        spread(g, j + 3)
                    place_values(g, j)
                    if not last or j + 2 < GROUP:
                        shift(g, j + 2)
                    if j == 1 and not first and not second:
                        weigh(g - 2)
                    if j == 3 and not first and not second:
                        add_to_x(g - 2)

            spread(0, 0, False)
            spread(0, 1, False)
            shift(0, 0, False)
            spread(0, 2)
            shift(0, 1, False)
            paired_groups(dve, body)
            for g in (LAST - 1, LAST):
                weigh(g)
                add_to_x(g)

        @block.scalar
        def _(act):
            def exp(g, j, filled=True):
                n, z = g * GROUP + j, j % 2
                act.wait_ge(sm.shifted, upto(n + 1))
                if filled:
                    act.wait_ge(sm.p_turned, upto(n - 1))
                act.activation(m.expd[z][:, :, :], m.soft[z][:, :, :], ACT.Exp, scale=DH1 ** -0.5).then_inc(sm.exped, 1)

            def spread(g, j, filled=True):
                n, z = g * GROUP + j, j % 2
                if filled:
                    act.wait_ge(sm.scored, upto(n - 1))
                for strip in range(4):
                    act.activation(m.q_strip[z][:, strip, :], m.QT[:, cols(n, P)], ACT.Copy,
                                   scale=m.strip_mask[:, strip:strip + 1]).then_inc(sm.q_spread, 1)

            def att_out(g):
                act.wait_ge(sm.att_turned, upto(g + 1))
                act.wait_ge(sm.wo_done, upto(g))
                act.copy(m.att_t[:, :], m.ps7[:, :]).then_inc(sm.att_out, 1)

            def pos_out(g, first=False):
                act.wait_ge(sm.pv_done, upto(g + 1))
                if not first:
                    act.wait_ge(sm.pv_saved, upto(32 * g))
                act.copy(m.pv[:, :], rel_v).then_inc(sm.pv_out, 1)

            def body(g, u, first, second, last):
                for j in range(GROUP):
                    n = g * GROUP + j
                    act.wait_ge(sm.p_turned, upto(n + 1))
                    if j == 0 and not first:
                        act.wait_ge(sm.pv_done, upto(g - 1))
                    act.copy(m.p_t[u][:, j, :], turned).then_inc(sm.pt_out, 1)
                    if j == 2 and not first and not second:
                        att_out(g - 2)
                    if not last or j + 3 < GROUP:
                        spread(g, j + 3)
                    act.wait_ge(sm.av_done, upto(n + 1))
                    for c in range(2):
                        half = slice(c * S, (c + 1) * S)
                        src = m.ps6[half, 0:288].rearrange("t (n c q) -> t n c q", c=2, n=8)[:, :, c, :]
                        dst = m.av[half, cols(n, 1), :].rearrange("t i (n q) -> t (i n) q", n=8)
                        act.copy(dst, src).then_inc(sm.av_out, 1)
                    if j == GROUP - 1 and not first:
                        pos_out(g - 1, second)
                    if not last or j + 2 < GROUP:
                        exp(g, j + 2)

            spread(0, 0, False)
            spread(0, 1, False)
            exp(0, 0, False)
            spread(0, 2)
            exp(0, 1, False)
            paired_groups(act, body)
            pos_out(LAST)
            att_out(LAST - 1)
            att_out(LAST)

        @block.tensor
        def _(pe):
            def scores_of(g, j):
                n, z = g * GROUP + j, j % 2
                pe.wait_ge(sm.q_spread, upto(4 * n + 4))
                pe.wait_ge(sm.k_spread, upto(n + 1))
                pe.wait_ge(sm.added, upto(n))
                hold(pe, m)
                for strip in range(4):
                    for c in range(2):
                        ins = pe.matmul(scores[c * S:(c + 1) * S, 256 * strip:256 * (strip + 1)],
                                        m.q_strip[z][:, strip, c * S:(c + 1) * S],
                                        m.k_inner[z][:, :, c * S:(c + 1) * S], start=True, stop=True)
                ins.then_inc(sm.scored, 1)

            def values_of(g, j):
                n = g * GROUP + j
                pe.wait_ge(sm.ct_staged, upto(2 * n + 2))
                pe.wait_ge(sm.v_out, upto(4 * n))
                for c in range(2):
                    ins = pe.matmul(values[:, c * P:(c + 1) * P], m.ct_twice[:, c, :, :].rearrange("p a s -> p (a s)"),
                                    m.proj_t[:, 2, :], start=True, stop=True)
                ins.then_inc(sm.v_done, 1)

            def turn(g, j):
                n, z = g * GROUP + j, j % 2
                pe.wait_ge(sm.exped, upto(n + 1))
                pe.wait_ge(sm.pt_out, upto(n))
                for pair in range(8):
                    ins = pe.transpose(turned[:, P * pair:P * (pair + 1)],
                                       m.expd[z][:, 2 * pair:2 * pair + 2, :].rearrange("p h s -> p (h s)"), m.ident[:, :])
                ins.then_inc(sm.p_turned, 1)

            def sum_values(g, j, u):
                n = g * GROUP + j
                pe.wait_ge(sm.pt_out, upto(n + 1))
                pe.wait_ge(sm.v_out, upto(4 * n + 4))
                pe.wait_ge(sm.av_out, upto(2 * n))
                for pair in range(8):
                    ins = pe.matmul(m.ps6[:, 36 * pair:36 * (pair + 1)], m.p_t[u][:, j, P * pair:P * (pair + 1)],
                                    m.v_block[:, pair, :, :, :].rearrange("p c q w -> p (c q w)"), start=True, stop=True)
                ins.then_inc(sm.av_done, 1)

            def sum_pos(g, u, quarter):
                p = m.p_t[u][:, :, :].rearrange("p i (n t) -> p (i n) t", t=S)
                half = quarter // 2
                if quarter == 0:
                    pe.wait_ge(sm.pv_out, upto(g))
                    hold(pe, m)
                for t in range(16 * quarter, 16 * (quarter + 1)):
                    ins = pe.matmul(rel_v[half * S:(half + 1) * S, 16 * (t % 32):16 * (t % 32 + 1)], p[:, :, t], m.pos_v[:, t, :],
                                    start=True, stop=True)
                if quarter == 3:
                    ins.then_inc(sm.pv_done, 1)

            def turn_att(g):
                pe.wait_ge(sm.att_done, upto(g + 1))
                pe.wait_ge(sm.small, upto(4 * g + 2))
                for j in range(GROUP):
                    ins = pe.transpose(m.ps7[:, P * j:P * (j + 1)], m.att[:, j, :], m.ident[:, :])
                ins.then_inc(sm.att_turned, 1)

            def project_out(g):
                pe.wait_ge(sm.att_out, upto(g + 1))
                for j in range(GROUP):
                    ins = pe.matmul(m.ps7[:, P * j:P * (j + 1)], m.att_t[:, P * j:P * (j + 1)], m.proj_t[:, 3, :], start=True, stop=True)
                ins.then_inc(sm.wo_done, 1)

            def body(g, u, first, second, last):
                for j in range(GROUP):
                    turn(g, j)
                    values_of(g, j)
                    if not last or j + 2 < GROUP:
                        scores_of(g, j + 2)
                    if not first:
                        sum_pos(g - 1, 1 - u, j)
                    if j == 2 and not first and not second:
                        turn_att(g - 2)
                    if j == 3 and not first and not second:
                        project_out(g - 2)
                    sum_values(g, j, u)

            scores_of(0, 0)
            scores_of(0, 1)
            paired_groups(pe, body)
            for quarter in range(4):
                sum_pos(LAST, 1, quarter)
            for g in (LAST - 1, LAST):
                turn_att(g)
                project_out(g)


def load_expert_weights(nc, m):
    with nc.Block() as block:

        @block.sync
        def _(sp):
            sp.dma_start(m.W1_sb, m.W1.rearrange("e d h -> d e h")).then_inc(m.moe_loaded, 16)
            for e in (0, 4):
                sp.dma_start(m.W2_sb[:, e:e + 4], m.W2[e:e + 4].rearrange("e (c p) d -> p e c d", p=P)).then_inc(m.moe_loaded, 16)


def router(nc, m):
    sm = m.ro
    W1, W1_h, W1_l = (w.rearrange("p e h -> p (e h)") for w in (m.W1_sb, m.W1_h, m.W1_l))
    W2, W2_h, W2_l = (w.rearrange("p e c d -> p (e c d)") for w in (m.W2_sb, m.W2_h, m.W2_l))
    with nc.Block() as block:

        @block.vector
        def _(dve):
            dve.wait_ge(m.moe_small_loaded, 64)

            def norm(g2, z, first=False):
                if not first:
                    dve.wait_ge(sm.turned[z], upto(g2))
                for j in range(GROUP):
                    ins = normalize(dve, m, m.stage_x[z][:, j, :], (g2 * 2 + z) * GROUP + j)
                ins.then_inc(sm.normed[z], 1)

            def take(g2, z):
                g = g2 * 2 + z
                dve.wait_ge(sm.high[z], upto(g2 + 1))
                dve.tensor_tensor(m.xt_l[:, cols(g, 512)], m.stage_xt[z][:, :], m.xt_h[:, cols(g, 512)].bitcast(F32),
                                  ALU.subtract).then_inc(sm.low[z], 1)
                dve.wait_ge(sm.logits[z], upto(g2 + 1))
                dve.tensor_tensor(m.logit[:, cols(g, GROUP), :], m.ps[2 + z][:, 0:32].rearrange("p (j e) -> p j e", e=EXPERTS),
                                  m.br_rows[:, :].unsqueeze(1).to_broadcast([P, GROUP, EXPERTS]), ALU.add).then_inc(sm.taken[z], 1)

            def split(k):
                dve.wait_ge(m.moe_loaded, 48)
                part = cols(k, 1024)
                dve.tensor_copy(W1_h[:, part], W1[:, part]).then_inc(sm.w1_high, 1)
                dve.wait_ge(sm.w2_high, upto(k + 1))
                dve.tensor_tensor(W2_l[:, part], W2[:, part], W2_h[:, part].bitcast(F32), ALU.subtract)
                dve.wait_ge(sm.w1_high, upto(k + 1))
                dve.tensor_tensor(W1_l[:, part], W1[:, part], W1_h[:, part].bitcast(F32), ALU.subtract)

            for z in range(2):
                norm(0, z, True)
            with dve.Fori(0, GROUPS // 2 - 1) as g2:
                for z in range(2):
                    norm(g2 + 1, z)
                    take(g2, z)
                split(g2)
            for z in range(2):
                take(GROUPS // 2 - 1, z)
            split(GROUPS // 2 - 1)
            dve.wait_ge(m.b1_turned, 1)
            dve.tensor_copy(m.b1_cols[:, :], m.ps[4][:, 0:4 * EXPERTS])

        @block.tensor
        def _(pe):
            def turn(g2, z):
                pe.wait_ge(sm.normed[z], upto(g2 + 1))
                pe.wait_ge(sm.xt_out[z], upto(g2))
                for j in range(GROUP):
                    ins = pe.transpose(m.ps[z][:, P * j:P * (j + 1)], m.stage_x[z][:, j, :], m.ident[:, :])
                ins.then_inc(sm.turned[z], 1)

            def logits(g2, z):
                pe.wait_ge(sm.xt_out[z], upto(g2 + 1))
                pe.wait_ge(sm.taken[z], upto(g2))
                for j in range(GROUP):
                    ins = pe.matmul(m.ps[2 + z][:, EXPERTS * j:EXPERTS * (j + 1)], m.stage_xt[z][:, P * j:P * (j + 1)],
                                    m.Wr_sb[:, :], start=True, stop=True)
                ins.then_inc(sm.logits[z], 1)

            for z in range(2):
                turn(0, z)
            with pe.Fori(0, GROUPS // 2 - 1) as g2:
                for z in range(2):
                    logits(g2, z)
                    turn(g2 + 1, z)
            for z in range(2):
                logits(GROUPS // 2 - 1, z)
            pe.transpose(m.ps[4][:, 0:4 * EXPERTS], m.b1_raw[:, :], m.ident[0:4 * EXPERTS, 0:4 * EXPERTS]).then_inc(m.b1_turned, 1)

        @block.scalar
        def _(act):
            with act.Fori(0, GROUPS // 2) as g2:
                for z in range(2):
                    act.wait_ge(sm.turned[z], upto(g2 + 1))
                    act.wait_ge(sm.logits[z], upto(g2))
                    act.wait_ge(sm.low[z], upto(g2))
                    act.copy(m.stage_xt[z][:, :], m.ps[z][:, :]).then_inc(sm.xt_out[z], 1)
                    act.wait_ge(sm.xt_out[z], upto(g2 + 1))
                    act.copy(m.xt_h[:, cols(g2 * 2 + z, 512)], m.stage_xt[z][:, :]).then_inc(sm.high[z], 1)
                act.wait_ge(m.moe_loaded, 48)
                act.copy(W2_h[:, cols(g2, 1024)], W2[:, cols(g2, 1024)]).then_inc(sm.w2_high, 1)

def router_weights(nc, m):
    wide = [P, TILES, EXPERTS]
    with nc.Block() as block:

        @block.vector
        def _(dve):
            step = Chain(dve, m.rt.dve)
            for i in range(TILES):
                ins = dve.max(m.best[:, i, :], m.logit[:, i, :])
            step.link(ins)
            step.link(dve.tensor_tensor(m.chosen[:, :, :], m.logit[:, :, :], m.best[:, :, 1:2].to_broadcast(wide), ALU.is_ge))
            step.link(dve.tensor_tensor(m.logit[:, :, :], m.logit[:, :, :], m.best[:, :, 0:1].to_broadcast(wide), ALU.subtract))
            dve.sem_inc(m.rt.shifted, 1)
            dve.wait_ge(m.rt.exp, 1)
            step.link(dve.tensor_tensor(m.weight[:, :, :], m.weight[:, :, :], m.chosen[:, :, :], ALU.mult))
            step.link(dve.tensor_reduce(m.wsum[:, :], m.weight[:, :, :], AX, ALU.add))
            step.link(dve.reciprocal(m.wsum[:, :], m.wsum[:, :]))
            step.link(dve.tensor_scalar(m.wsum[:, :], m.wsum[:, :], m.tanh_g[:, 3:4], None, ALU.mult))
            step.link(dve.tensor_tensor(m.weight[:, :, :], m.weight[:, :, :], m.wsum[:, :].unsqueeze(2).to_broadcast(wide), ALU.mult))
            dve.sem_inc(m.rt.weights, 1)
            for g in range(1, GROUPS, 2):
                dve.wait_ge(m.rt.turned, g + 1)
                dve.tensor_copy(m.weight_rows[:, g * 512:(g + 1) * 512], m.ps[g][0:EXPERTS, :]).then_inc(m.rt.rows, 1)

        @block.tensor
        def _(pe):
            pe.wait_ge(m.rt.weights, 1)
            for g in range(GROUPS):
                for j in range(GROUP):
                    ins = pe.transpose(m.ps[g][0:EXPERTS, P * j:P * (j + 1)], m.weight[:, g * GROUP + j, :], m.ident[:, :])
                ins.then_inc(m.rt.turned, 1)

        @block.scalar
        def _(act):
            act.wait_ge(m.rt.shifted, 1)
            act.activation(m.weight[:, :, :], m.logit[:, :, :], ACT.Exp).then_inc(m.rt.exp, 1)
            for g in range(0, GROUPS, 2):
                act.wait_ge(m.rt.turned, g + 1)
                act.copy(m.weight_rows[:, g * 512:(g + 1) * 512], m.ps[g][0:EXPERTS, :]).then_inc(m.rt.rows, 1)


def experts(nc, m):
    sm = m.mo
    LAST = GROUPS - 1
    UP = (2, 3, 6, 7)
    ORDER = (0, 2, 1, 3)

    def split_count(g, e, c):
        return upto(32 * g + 4 * e + ORDER.index(c) + 1)

    with nc.Block() as block:

        @block.gpsimd
        def _(pool):
            with pool.Fori(0, GROUPS) as g:
                for e in range(1, EXPERTS):
                    pool.wait_ge(sm.weighed, upto(8 * g + e + 1))
                    pool.wait_ge(sm.added, upto(7 * g + e - 1))
                    pool.tensor_tensor(m.acc[:, :], m.acc[:, :], m.weighted[e % 2][:, :], ALU.add).then_inc(sm.added, 1)

        @block.vector
        def _(dve):
            def split(g, e, first):
                z = e % 2
                for c in (1, 3):
                    dve.wait_ge(sm.gelu, upto(32 * g + 4 * e + c + 1))
                    if not first or e > 0:
                        dve.wait_ge(sm.down_done, upto(8 * g + e - 1))
                    dve.tensor_copy(m.h_h[z][:, c, :], m.h[c][:, :]).then_inc(sm.h_high, 1)
                    rest(g, e, c - 1)
                for c in (1, 3):
                    rest(g, e, c)

            def rest(g, e, c):
                if c % 2:
                    dve.wait_ge(sm.h_high, upto(16 * g + 2 * e + (c + 1) // 2))
                else:
                    dve.wait_ge(sm.h_high2, upto(16 * g + 2 * e + c // 2 + 1))
                dve.tensor_tensor(m.h_l[e % 2][:, c, :], m.h[c][:, :], m.h_h[e % 2][:, c, :].bitcast(F32),
                                  ALU.subtract).then_inc(sm.h_split, 1)

            def weigh(g, e):
                out = m.acc if e == 0 else m.weighted[e % 2]
                dve.wait_ge(sm.down_done, upto(8 * g + e + 1))
                if e % 4 == 0:
                    dve.wait_ge(sm.weight_in[e // 4], upto(16 * g + 16))
                if e == 0:
                    dve.wait_ge(sm.out_done, upto(g))
                else:
                    dve.wait_ge(sm.added, upto(7 * g + max(e - 2, 0)))
                dve.tensor_tensor(out[:, :], m.ps[4 + e % 2], m.weight_wide[:, e, :], ALU.mult).then_inc(sm.weighed, 1)

            def residual(g, first=False):
                dve.wait_ge(sm.out_done, upto(g + 1))
                if not first:
                    dve.wait_ge(sm.saved, upto(16 * g))
                dve.tensor_tensor(m.x_out, m.ps[0].rearrange("p (j f) -> p j f", f=E), m.X[:, cols(g, GROUP), :],
                                  ALU.add).then_inc(sm.summed, 1)

            def body(g, first, last):
                for e in range(EXPERTS):
                    if e > 0:
                        split(g, e, first)
                        weigh(g, e - 1)
                        if e == 2 and not first:
                            residual(g - 1)
                if not last:
                    split(g + 1, 0, False)
                weigh(g, EXPERTS - 1)

            split(0, 0, True)
            groups(dve, body)
            residual(LAST)

        @block.scalar
        def _(act):
            def body(g, first, last):
                for e in range(EXPERTS):
                    for c in range(4):
                        n = 32 * g + 4 * e + c
                        act.wait_ge(sm.up_done, upto(n + 1))
                        if not first or e > 0:
                            act.wait_ge(sm.h_split, split_count(g, e - 1, c))
                        act.activation(m.h[c][:, :], m.ps[UP[c]], ACT.Gelu, bias=m.b1_cols[:, 4 * e + c:4 * e + c + 1]).then_inc(sm.gelu, 1)
                        if c % 2 == 0:
                            act.wait_ge(sm.gelu, upto(n + 1))
                            if not first or e > 0:
                                act.wait_ge(sm.down_done, upto(8 * g + e - 1))
                            act.copy(m.h_h[e % 2][:, c, :], m.h[c][:, :]).then_inc(sm.h_high2, 1)

            groups(act, body)

        @block.tensor
        def _(pe):
            def up(g, e, first=False):
                xt_h, xt_l = m.xt_h[:, cols(g, 512)], m.xt_l[:, cols(g, 512)]
                for c in range(4):
                    if not first:
                        pe.wait_ge(sm.gelu, upto(32 * g + 4 * (e - 1) + c + 1))
                    out, cs = m.ps[UP[c]], slice(c * P, (c + 1) * P)
                    pe.matmul(out, m.W1_h[:, e, cs], xt_h, start=True, stop=False)
                    pe.matmul(out, m.W1_l[:, e, cs], xt_h, start=False, stop=False)
                    pe.matmul(out, m.W1_h[:, e, cs], xt_l, start=False, stop=True).then_inc(sm.up_done, 1)

            def down(g, e, first):
                out, z = m.ps[4 + e % 2], e % 2
                if not first or e > 0:
                    pe.wait_ge(sm.weighed, upto(8 * g + e - 1))
                for c in ORDER:
                    pe.wait_ge(sm.h_split, split_count(g, e, c))
                    pe.matmul(out, m.W2_h[:, e, c, :], m.h_h[z][:, c, :], start=(c == ORDER[0]), stop=False)
                    pe.matmul(out, m.W2_l[:, e, c, :], m.h_h[z][:, c, :], start=False, stop=False)
                    ins = pe.matmul(out, m.W2_h[:, e, c, :], m.h_l[z][:, c, :], start=False, stop=(c == ORDER[-1]))
                ins.then_inc(sm.down_done, 1)

            def turn_out(g):
                pe.wait_ge(sm.summed, upto(g))
                pe.wait_ge(sm.rows_in, upto(16 * g + 16))
                pe.wait_ge(sm.added, upto(7 * g + 7))
                for j in range(GROUP):
                    tok = slice(P * j, P * (j + 1))
                    pe.matmul(m.ps[0][:, tok], m.weight_t[:, tok], m.b2_sb[:, :], start=True, stop=False)
                    ins = pe.matmul(m.ps[0][:, tok], m.acc[:, tok], m.ident[:, :], start=False, stop=True)
                ins.then_inc(sm.out_done, 1)

            def body(g, first, last):
                for e in range(EXPERTS):
                    if e + 1 < EXPERTS:
                        up(g, e + 1)
                    elif not last:
                        up(g + 1, 0)
                    if e == 0 and not first:
                        turn_out(g - 1)
                    down(g, e, first)

            up(0, 0, True)
            groups(pe, body)
            turn_out(LAST)

        @block.sync
        def _(sp):
            def load_weights(g, half):
                es = slice(4 * half, 4 * half + 4)
                sp.dma_start(m.weight_wide[:, es, :], m.weight_dram[es, cols(g, 512)].partition_broadcast(P)).then_inc(sm.weight_in[half], 16)

            def load_rows(g):
                sp.dma_start(m.weight_t[:, :], m.weight_dram[:, cols(g, 512)]).then_inc(sm.rows_in, 16)

            def save(g):
                sp.wait_ge(sm.summed, upto(g + 1))
                hold(sp, m)
                sp.dma_start(m.out_tiles[:, cols(g, GROUP), :], m.x_out).then_inc(sm.saved, 16)

            def body(g, first, last):
                if not first:
                    save(g - 1)
                    load_rows(g)
                if not last:
                    for half in range(2):
                        sp.wait_ge(sm.weighed, upto(8 * g + 4 * half + 4))
                        hold(sp, m)
                        load_weights(g + 1, half)

            sp.wait_ge(m.rt.rows, GROUPS)
            sp.dma_start(m.weight_dram, m.weight_rows).then_inc(m.rt.saved, 16)
            sp.wait_ge(m.rt.saved, 16)
            load_weights(0, 0)
            load_weights(0, 1)
            load_rows(0)
            groups(sp, body)
            save(LAST)
            sp.wait_ge(sm.saved, upto(16 * GROUPS))


def build(nc, ins, out):
    m = Names(dict(ins))
    m.credited, m.reused = [], []
    with ExitStack() as ctx:
        m.scope = ctx

        def sb(name, shape, dt=F32):
            return ctx.enter_context(nc.sbuf_tensor(name, shape, dt))

        def sems(name, *names, **lists):
            table = {}
            for n in names:
                table[n] = m.scope.enter_context(nc.semaphore(f"{name}_{n}"))
            for n, k in lists.items():
                table[n] = [m.scope.enter_context(nc.semaphore(f"{name}_{n}{i}")) for i in range(k)]
            for s in table.values():
                m.reused.extend(s if isinstance(s, list) else [s])
            return Names(table)

        def counted(name, *names, **lists):
            ns = sems(name, *names, **lists)
            for s in ns.table.values():
                m.credited.extend(s if isinstance(s, list) else [s])
            return ns

        m.table.update(sems("io", "x_loaded", "ctx_loaded", "gates_loaded", "scales_loaded", "tanh_ready",
                               "const_step", "stored", "ffn0_loaded", "clips_loaded",
                               "proj_loaded", "proj_bias_loaded", "pos_loaded", "moe_loaded", "moe_small_loaded",
                               "b1_turned", "held").table)
        m.stat_sems = [sems(f"stats{k}", "dve", "variance", "root") for k in range(4)]
        m.wide = [ctx.enter_context(nc.psum_tensor(f"banks{k}", [P, 1024], F32)) for k in range(3)]
        m.ps6, m.ps7 = (ctx.enter_context(nc.psum_tensor(f"bank{k}", [P, 512], F32)) for k in (6, 7))
        m.ps = [m.wide[k // 2][:, 512 * (k % 2):512 * (k % 2 + 1)] for k in range(6)] + [m.ps6[:, :], m.ps7[:, :]]

        m.X = sb("X", [P, TILES, E])
        m.CT = sb("CT", [P, TILES * P])
        m.ident = sb("ident", [P, P])
        m.ident_bf = sb("ident_bf", [P, P], BF16)
        m.ones = sb("ones", [P, P])
        m.tanh_g = sb("tanh_g", [P, 4])
        m.row_stats = sb("row_stats", [P, TILES, 6])
        m.row_mean = sb("row_mean", [P, TILES])
        m.row_rstd = sb("row_rstd", [P, TILES])
        m.row_tmp, m.row_tmp2 = sb("row_tmp", [P, TILES]), sb("row_tmp2", [P, TILES])
        m.head_mask = sb("head_mask", [P, NH0])
        m.cumsum_mat = sb("cumsum_mat", [P, P])

        m.causal_add = sb("causal_add", [P, S])

        m.magic = sb("magic", [P, 1])
        m.clips = sb("clips", [1, 2])
        m.gu_raw_t = sb("gu_raw", [P, 6, E])
        m.proj_raw = sb("proj_raw", [P, 4, E])
        m.proj_bias = sb("proj_bias", [P, 2])
        m.bv_rows, m.bo_rows = sb("bv_rows", [P, E]), sb("bo_rows", [P, E])
        m.pos_k_raw = sb("pos_k_raw", [S, S, DH1])
        m.pos_v = sb("pos_v", [P, S, 2 * DH1])
        m.v_block = sb("v_block", [P, NH1 // 2, 2, 2, DH1 + 1])
        m.strip_mask, m.inner_mask = sb("strip_mask", [P, 4]), sb("inner_mask", [P, 4])
        m.Wr_sb, m.br_rows = sb("Wr_sb", [P, EXPERTS]), sb("br_rows", [P, EXPERTS])
        m.b2_sb, m.b1_cols = sb("b2_sb", [EXPERTS, E]), sb("b1_cols", [P, 4 * EXPERTS])
        m.b1_raw = sb("b1_raw", [4 * EXPERTS, P])
        m.ctx_tiles = m.ctx.rearrange("(i c) s f -> (c s) i f", c=2)
        m.out_tiles = out.rearrange("(i c) s f -> (c s) i f", c=2)
        m.dn_raw_t = sb("dn_raw", [P, 1, 352])
        m.gu_raw, m.dn_raw = m.gu_raw_t[:, :, :], m.dn_raw_t[:, :, :]

        with ExitStack() as early:
            m.C = early.enter_context(nc.sbuf_tensor("C", [P, TILES, E], F32))
            m.XT = early.enter_context(nc.sbuf_tensor("XT", [P, TILES * P], F32))

            with ExitStack() as l0:
                m.scope = l0
                m.gs = counted("gates", "ctx_turned", "xt_out", "ct_out", "x_turned", "normed", "gates_done", "biased", "gates_turned", "gates_out",
                               ctx_in=2, stored=2)
                m.gw = sems("gates_w", "turned", "ready")
                m.gm = sems("gmath", "act", "dve", "dve2", "log1p", "neg", "logf", "summed", "g", "g_turned", "gmax",
                            "gmax_turned", "saved")
                m.rows = sems("att0_g", rows=4).rows
                m.at = counted("att0", "diff", "qk", "spread", "av", "v", "causal", "c", "exp", "k", "out")
                m.af = sems("fin0", "dve", "centered", "squared", "var", "root")
                def sl(name, shape, dt=F32):
                    return l0.enter_context(nc.sbuf_tensor(name, shape, dt))
                m.gate_rows = sl("gate_rows", [16, 3 * E])
                m.gate_bias = sl("gate_bias", [2 * NH0, 1])
                m.gates_t = [sl(f"gates_t{j}", [2 * NH0, 512]) for j in range(2)]
                m.gate_w = sl("gate_w", [P, 2, 16])
                m.out_w_rows = sl("out_w_rows", [P, E])
                m.stage_x = [sl(f"stage_x_slot{j}", [P, GROUP, E]) for j in range(2)]
                m.stage_c = [sl(f"stage_c_slot{j}", [P, GROUP, E]) for j in range(2)]
                m.stage_xt = [sl(f"stage_xt_slot{j}", [P, 512]) for j in range(2)]
                m.stage_ct = [sl(f"stage_ct_slot{j}", [P, 512]) for j in range(2)]
                m.gates = sl("gates", [P, TILES, 16])
                m.softp = sl("softp", [P, TILES, NH0])
                m.logf = sl("logf", [P, TILES, NH0])
                m.exp_neg_max = sl("exp_neg_max", [P, TILES, NH0])
                m.g_nat = sl("g_nat", [P, TILES, NH0])
                m.cumsum = sl("cumsum", [P, TILES * NH0])
                m.g_t = sl("g_t", [P, 2, P])
                m.gmax_t = sl("gmax_t", [P, 2, P])
                m.g_rows = [sl(f"g_rows{j}", [P, NH0 * S]) for j in range(2)]
                m.decay = [sl(f"decay{j}", [P, NH0, S]) for j in range(GROUP)]
                m.c_t = [sl(f"c_t{j}", [P, NH0, S]) for j in range(2)]
                m.q_spread = [sl(f"q_spread{j}", [P, NH0, P]) for j in range(2)]
                m.k_stage = [sl(f"k_stage{j}", [P, P]) for j in range(2)]
                m.v_ones = [sl(f"v_ones{j}", [P, NH0, 2, DH0 + 1]) for j in range(2)]
                m.num = sl("num", [P, TILES, NH0 * (DH0 + 1)])
                m.den = sl("den", [P, TILES * NH0])
                m.hmean = sl("hmean", [P, TILES * NH0])
                m.hvar = sl("hvar", [P, TILES * NH0])
                m.hid = sl("hid", [P, TILES * NH0, DH0])
                m.hsq = sl("hsq", [P, TILES * NH0, DH0])
                m.gmax_dram = nc.dram_tensor("gmax_dram", (2, TILES, NH0, S), F32, kind="Internal").ap()
                with nc.Block() as block:
                    start_counts(block, m)
                load_and_constants(nc, m)
                l0_gates(nc, m)
                l0_gate_math(nc, m)
                l0_attention(nc, m)
                l0_attention_finish(nc, m)

            with ExitStack() as f0:
                m.scope = f0
                m.fw = sems("ffn0_w", "dve", "quantized", "turned")
                m.fn = counted("ffn0_norm", "normed")
                scale_sems = [sems(f"scale{k}", "exp", "dve", "col", "row", "pair", "spread") for k in range(2)]
                m.fu = counted("ffn0_up", "scaled", "shifted", "clipped", "turned", "quantized", "upped", "stood", "silu", "hidden")
                m.fd = counted("ffn0_down", "shifted", "clipped", "downed", "quantized", "out", "added")
                m.fd.dve = sems("ffn0_down", "dve").dve
                def sl(name, shape, dt=F32):
                    return f0.enter_context(nc.sbuf_tensor(name, shape, dt))
                m.XN = m.XT[:, :].rearrange("p (i f) -> p i f", f=E)
                gu_q, dn_q = sl("gu_q", [P, 6, E], BF16), sl("dn_q", [P, 1, 352], BF16)
                m.gu_q, m.dn_q = gu_q[:, :, :], dn_q[:, :, :]
                m.gu_top, m.gu_scale = sl("gu_top", [P, 6]), sl("gu_scale", [P, 6])
                m.dn_top, m.dn_scale = sl("dn_top", [P, 1]), sl("dn_scale", [P, 1])
                m.dn_diag = sl("dn_diag", [P, P])
                m.dn_row = sl("dn_row", [P, E])
                m.gu_t = sl("gu_t", [P, 6, P], BF16)
                m.dn_t = sl("dn_t", [P, 3, E], BF16)
                m.x_top = sl("x_top", [P, GROUPS])
                m.h_top = sl("h_top", [P, 3, GROUPS])
                m.clip_exp = sl("clip_exp", [1, 1])
                m.top_col = sl("top_col", [P, 1])
                m.top_one = sl("top_one", [1, 2])
                m.top_pair = sl("top_pair", [1, 2])
                m.x_scale, m.h_scale = sl("x_scale", [P, 2]), sl("h_scale", [P, 2])
                m.round_x, m.xq, m.xq_t = sl("round_x", [P, 512]), sl("xq", [P, 512], BF16), sl("xq_t", [P, 512], BF16)
                m.silu = [sl(f"silu{k}", [P, 512]) for k in range(3)]
                m.HT = sl("HT", [P, 3, TILES * P])
                m.round_h, m.hq = sl("round_h", [P, 3, 512]), sl("hq", [P, 3, 512], BF16)
                m.down = sl("down", [P, GROUP, E])
                finish_stats(nc, m, m.stat_sems[1])
                l0_ffn_weights(nc, m)
                l0_ffn_norm(nc, m)
                activation_scale(nc, m, scale_sems[0], m.x_top[:, :], m.clips[0:1, 0:1], m.x_scale)
                l0_ffn_up(nc, m)
                activation_scale(nc, m, scale_sems[1], m.h_top[:, :, :].rearrange("p k g -> p (k g)"), m.clips[0:1, 1:2], m.h_scale)
                l0_ffn_down(nc, m)

            with ExitStack() as l1:
                m.scope = l1
                m.lw = sems("l1_w", "dve", "turned", "moved")
                m.pj = counted("l1_proj", "turned", "normed", "xt_out", "q_done", "k_done", "q_out", "k_out", "rest", "middle", "low",
                               "parts_saved")
                m.rl = counted("l1_rel", "done", loaded=2, saved=2, out=4)
                m.a1 = counted("l1_att", "added", "masked", "pv_out", "pv_saved", "pv_back", "summed", "v_done", "ct_staged",
                               "scored", "q_spread", "k_spread", "av_done", "v_out", "exped", "maxed", "shifted", "av_out", "small",
                               "att_turned", "att_done", "wo_done", "p_turned", "pv_done", "pt_out", "att_out")
                m.rel_sem = sems("l1_rel_in", slot=4).slot
                m.mask_in_sem = sems("l1_mask", "loaded").loaded
                def sl(name, shape, dt=F32):
                    return l1.enter_context(nc.sbuf_tensor(name, shape, dt))
                m.proj_t = sl("proj_t", [P, 4, E])
                m.mask_in, m.mask_add = sl("mask_in", [P, TILES, S], I32), sl("mask_add", [P, TILES, S])
                m.stage_x, m.stage_xt = sl("stage_x1", [P, GROUP, E]), sl("stage_xt1", [P, 512])
                m.KT, m.QT = sl("KT", [P, TILES * P]), m.XT
                m.q_dram = nc.dram_tensor("q_dram", (GROUPS, NH1, 3, DH1, 512), BF16, kind="Internal").ap()
                m.pos_dram = nc.dram_tensor("pos_dram", (P, 3, 4 * S), BF16, kind="Internal").ap()
                m.rel_dram = nc.dram_tensor("rel_dram", (GROUPS, NH1, 8, S, S), F32, kind="Internal").ap()
                m.pv_dram = nc.dram_tensor("pv_dram", (GROUPS, S, S, 2 * DH1), F32, kind="Internal").ap()
                finish_stats(nc, m, m.stat_sems[2])
                with ExitStack() as part:
                    def sl(name, shape, dt=F32):
                        return part.enter_context(nc.sbuf_tensor(name, shape, dt))
                    m.pos_parts, m.pos_exact = sl("pos_parts", [P, 3, 4 * S], BF16), sl("pos_exact", [P, 4 * S])
                    m.pos_right = sl("pos_right", [STACK, 16, 4 * S], BF16)
                    m.q_rest, m.q_parts = sl("q_rest", [P, 512]), sl("q_parts", [P, 3, 512], BF16)
                    m.q_left = [sl(f"q_left{k}", [STACK, NH1, 512], BF16) for k in range(2)]
                    m.rel = [sl(f"rel{k}", [P, 2048]) for k in range(2)]
                    l1_weights(nc, m)
                    l1_project(nc, m)
                with ExitStack() as part:
                    def sl(name, shape, dt=F32):
                        return part.enter_context(nc.sbuf_tensor(name, shape, dt))
                    m.rel_in = [sl(f"rel_in{k}", [P, NH1, S]) for k in range(4)]
                    m.ct_twice = sl("ct_twice", [P, 2, 2, S])
                    m.q_strip = [sl(f"q_strip{k}", [P, 4, P]) for k in range(2)]
                    m.k_inner = [sl(f"k_inner{k}", [P, 4, P]) for k in range(2)]
                    m.soft = [sl(f"soft{k}", [P, NH1, S]) for k in range(2)]
                    m.expd = [sl(f"expd{k}", [P, NH1, S]) for k in range(2)]
                    m.row_max = sl("row_max", [P, NH1])
                    m.p_t = [m.C[:, :, :].rearrange("p i f -> p (i f)").rearrange("p (i k) -> p i k", k=1024),
                             sl("p_t1", [P, GROUP, 1024])[:, :, :]]
                    m.av = sl("av", [P, TILES, NH1 * (DH1 + 1)])
                    m.pv, m.pv_in = sl("pv", [P, 512]), sl("pv_in", [P, 32, 2 * DH1])
                    m.row_sum = sl("row_sum", [P, GROUP * NH1])
                    m.att, m.att_t, m.res = sl("att", [P, GROUP, E]), sl("att_t", [P, 512]), sl("res", [P, GROUP, E])
                    l1_attention(nc, m)

        with ExitStack() as f1:
            m.scope = f1
            m.ro = counted("route", "w1_high", "w2_high", turned=2, normed=2, xt_out=2, logits=2, taken=2, high=2, low=2)
            m.rt = sems("route1", "dve", "shifted", "exp", "weights", "turned", "rows", "saved")
            m.mo = counted("moe", "up_done", "gelu", "h_high", "h_high2", "h_split", "down_done", "weighed", "added",
                           "out_done", "summed", "rows_in", "saved", weight_in=2)
            def sl(name, shape, dt=F32):
                return f1.enter_context(nc.sbuf_tensor(name, shape, dt))
            m.W1_sb = m.CT[:, :].rearrange("p (e h) -> p e h", e=EXPERTS)
            m.W1_h, m.W1_l = (sl(f"W1_{k}", [P, EXPERTS, HID], F32R)[:, :, :] for k in "hl")
            m.W2_h, m.W2_l = (sl(f"W2_{k}", [P, EXPERTS, 4, E], F32R)[:, :, :, :] for k in "hl")
            m.xt_h, m.xt_l = sl("xt_h", [P, TILES * P], F32R), sl("xt_l", [P, TILES * P], F32R)
            m.stage_x = [sl(f"stage_x2{k}", [P, GROUP, E]) for k in range(2)]
            m.stage_xt = [sl(f"stage_xt2{k}", [P, 512]) for k in range(2)]
            m.weight_rows, m.weight_wide = m.CT[0:EXPERTS, :], m.CT[:, :].rearrange("p (e t) -> p e t", e=EXPERTS)
            m.weight_dram = nc.dram_tensor("weight_dram", (EXPERTS, TILES * P), F32, kind="Internal").ap()
            m.weighted, m.x_out = m.stage_xt, m.stage_x[0][:, :, :]
            m.logit, m.best, m.chosen, m.weight = (sl(k, [P, TILES, EXPERTS]) for k in ("logit", "best", "chosen", "weight"))
            m.wsum, m.weight_t = sl("wsum", [P, TILES]), sl("weight_t", [EXPERTS, 512])
            m.acc = sl("acc", [P, 512])
            with ExitStack() as part:
                m.W2_sb = part.enter_context(nc.sbuf_tensor("W2_raw", [P, EXPERTS, 4, E], F32))[:, :, :, :]
                load_expert_weights(nc, m)
                finish_stats(nc, m, m.stat_sems[3])
                router(nc, m)
            m.h = [sl(f"h{k}", [P, 512]) for k in range(4)]
            m.h_h = [sl(f"h_h{k}", [P, 4, 512], F32R) for k in range(2)]
            m.h_l = [sl(f"h_l{k}", [P, 4, 512], F32R) for k in range(2)]
            router_weights(nc, m)
            experts(nc, m)


_INS = {'x': 'x', 'ctx_1024': 'ctx', 'mask_BxSxS2_ik0': 'mask', 'g_xattn': 'g_xattn', 'g_ffn': 'g_ffn',
        'L0_xattn_igate_w': 'igate_w', 'L0_xattn_igate_b': 'igate_b', 'L0_xattn_fgate_w': 'fgate_w',
        'L0_xattn_fgate_b': 'fgate_b', 'L0_xattn_out_w': 'out_w', 'L0_ffn_clip_x': 'clip_x',
        'L0_ffn_clip_down': 'clip_down', 'L0_ffn_w_gate': 'w_gate', 'L0_ffn_w_up': 'w_up', 'L0_ffn_w_down': 'w_down',
        'L1_xattn_pos_k': 'pos_k', 'L1_xattn_pos_v': 'pos_v_in', 'L1_xattn_Wq': 'Wq', 'L1_xattn_bq': 'bq',
        'L1_xattn_Wk': 'Wk', 'L1_xattn_bk': 'bk', 'L1_xattn_Wv': 'Wv', 'L1_xattn_bv': 'bv', 'L1_xattn_Wo': 'Wo',
        'L1_xattn_bo': 'bo', 'L1_ffn_W1': 'W1', 'L1_ffn_b1': 'b1', 'L1_ffn_W2': 'W2', 'L1_ffn_b2': 'b2',
        'L1_ffn_Wr': 'Wr', 'L1_ffn_br': 'br'}


def kernel(**inputs):
    import numpy as _np
    import concourse.bacc as _bacc
    from concourse import mybir as _mybir
    from concourse.bass_utils import run_bass_kernel_spmd as _run

    nc = _bacc.Bacc("TRN2", target_bir_lowering=False, num_devices=1)
    arrays, args = {}, {}
    for name, short in _INS.items():
        a = _np.ascontiguousarray(inputs[name])
        arrays[f"in_{name}_dram"] = a
        args[short] = nc.dram_tensor(f"in_{name}_dram", a.shape, _mybir.dt.from_np(a.dtype), kind="ExternalInput").ap()
    out = nc.dram_tensor("out_0_dram", (B, S, E), _mybir.dt.float32, kind="ExternalOutput").ap()
    build(nc, args, out)
    r = _run(nc, [arrays], core_ids=[0])
    return r.results[0]["out_0_dram"]
```
